# Optimizing a Trainium2 kernel written in Bass

```python
import numpy as np
import jax
import jax.numpy as jnp

def _softmax(x, axis=-1):
    return jax.nn.softmax(x, axis=axis)

def _gelu(x):
    return jax.nn.gelu(x, approximate=True)

def _silu(x):
    return jax.nn.silu(x)

def _sigmoid(x):
    return jax.nn.sigmoid(x)

def _layernorm(x, axis=-1, eps=1e-05):
    m = jnp.mean(x, axis=axis, keepdims=True)
    v = jnp.var(x, axis=axis, keepdims=True)
    return (x - m) / jnp.sqrt(v + eps)

def _scatter_add(tgt, idx, src, axis=0):
    return tgt.at[idx].add(src)

def _segment_sum(src, seg, n):
    return jax.ops.segment_sum(src, seg, n)
kernel_name = 'mk_decoder_preln_d2_seqx_r8_3e877e'

def setup_inputs(seed: int=0):
    np.random.seed(seed)
    _w = jnp.asarray

    def _rec_inputs():
        import jax
        import jax.numpy as jnp
        _rk = jax.random.key(seed)
        x = -0.001547 + 1.001 * jax.random.normal(jax.random.fold_in(_rk, 1), (4, 512, 128), jnp.float32)
        _lenS = 512 - jax.random.randint(jax.random.fold_in(_rk, 7), (4,), 0, max(1, 512 // 4) + 1, jnp.int32)
        _lenS2 = 77 - jax.random.randint(jax.random.fold_in(_rk, 8), (4,), 0, max(1, 77 // 4) + 1, jnp.int32)
        _ctx_1024P = jax.random.normal(jax.random.fold_in(_rk, 11), (4, 16, 128), jnp.float32)
        _ctx_1024c = jax.random.dirichlet(jax.random.fold_in(_rk, 511), 0.3 * jnp.ones((16,), jnp.float32), (4, 77))
        _ctx_1024t = jnp.einsum('bsk,bkd->bsd', _ctx_1024c, _ctx_1024P)
        _ctx_1024t = _ctx_1024t * jax.lax.rsqrt(jnp.mean(jnp.square(_ctx_1024t)) + 1e-12) * 0.953939
        ctx_1024 = -0.00010331 + 0.999899 * (_ctx_1024t + 0.3 * jax.random.normal(jax.random.fold_in(_rk, 611), (4, 77, 128), jnp.float32))
        _validS = jnp.arange(512)[None, :] < _lenS[:, None]
        _validS2 = jnp.arange(77)[None, :] < _lenS2[:, None]
        _causal = jnp.tril(jnp.ones((512, 512), dtype=bool))
        mask_BxS2_bk1 = jnp.broadcast_to(_validS2[:, :], (4, 77))
        return (x, ctx_1024, _lenS2, mask_BxS2_bk1)
    x, ctx_1024, _lenS2, mask_BxS2_bk1 = _rec_inputs()

    def _L0_attn_setup():
        import jax, jax.numpy as jnp
        import numpy as np
        import math
        B, T, D, H = (2, 256, 128, 16)
        DH = D // H

        def rotate_half(x):
            x1 = x[..., ::2]
            x2 = x[..., 1::2]
            return jnp.stack((-x2, x1), axis=-1).reshape(x.shape)
        key = jax.random.key(seed)
        k1, k2, k3 = jax.random.split(key, 3)
        x = jax.random.normal(k1, (B, T, D), dtype=jnp.float32)
        Wqkv = jax.random.normal(k2, (3 * D, D), dtype=jnp.float32) * (1.0 / math.sqrt(D))
        Wo = jax.random.normal(k3, (D, D), dtype=jnp.float32) * (1.0 / math.sqrt(D))
        return {'x': x, 'Wqkv': Wqkv, 'Wo': Wo}
    _L0_attn_all = _L0_attn_setup()
    _L0_attn_in = {k: v for k, v in _L0_attn_all.items() if k in ('Wqkv', 'Wo')}
    del _L0_attn_all

    def _L0_xattn_setup():
        import jax, jax.numpy as jnp
        import numpy as np
        N_HEADS = 16
        key = jax.random.key(seed)
        ks = jax.random.split(key, 9)
        B, T, C, S = (32, 8, 128, 512)
        w_scale = 1.0 / np.sqrt(C).astype(np.float32)
        return {'x': jax.random.normal(ks[0], (B, T, C), jnp.float32), 'cache_k': jax.random.normal(ks[1], (B, S, C), jnp.float32), 'cache_v': jax.random.normal(ks[2], (B, S, C), jnp.float32), 'cache_len': jax.random.randint(ks[3], (B,), 0, S - T, jnp.int32), 'wq': jax.random.normal(ks[4], (C, C), jnp.float32) * w_scale, 'wk': jax.random.normal(ks[5], (C, C), jnp.float32) * w_scale, 'wv': jax.random.normal(ks[6], (C, C), jnp.float32) * w_scale, 'wo': jax.random.normal(ks[7], (C, C), jnp.float32) * w_scale, 'bo': jnp.zeros((C,), jnp.float32)}
    _L0_xattn_all = _L0_xattn_setup()
    _L0_xattn_in = {k: v for k, v in _L0_xattn_all.items() if k in ('wq', 'wk', 'wv', 'wo', 'bo')}
    del _L0_xattn_all

    def _L0_ffn_setup():
        import jax, jax.numpy as jnp
        import numpy as np
        TOP_K = 2
        key = jax.random.key(seed)
        ks = jax.random.split(key, 5)
        B, T, D, F, E = (2, 256, 128, 512, 8)
        x = jax.random.normal(ks[0], (B, T, D), dtype=jnp.float32)
        router_w = jax.random.normal(ks[1], (D, E + 1), dtype=jnp.float32) * 0.02
        router_b = jax.random.normal(ks[2], (E + 1,), dtype=jnp.float32) * 0.02
        w1 = jax.random.normal(ks[3], (E, D, F), dtype=jnp.float32) * 0.02
        w2 = jax.random.normal(ks[4], (E, F, D), dtype=jnp.float32) * 0.02
        return {'x': x, 'router_w': router_w, 'router_b': router_b, 'w1': w1, 'w2': w2}
    _L0_ffn_all = _L0_ffn_setup()
    _L0_ffn_in = {k: v for k, v in _L0_ffn_all.items() if k in ('router_w', 'router_b', 'w1', 'w2')}
    del _L0_ffn_all

    def _L1_attn_setup():
        import jax, jax.numpy as jnp
        import numpy as np
        D_MODEL = 128
        NHEAD = 16
        HEAD_DIM = D_MODEL // NHEAD
        GN_EPS = 0.00064
        NORM_EPS = 1e-06
        B, T = (4, 128)

        def _xavier(key, shape):
            lim = float(np.sqrt(6.0 / (shape[0] + shape[1])))
            return jax.random.uniform(key, shape, jnp.float32, -lim, lim)

        def _l2norm(t):
            n = jnp.linalg.norm(t, axis=-1, keepdims=True)
            return t / jnp.maximum(n, NORM_EPS)
        key = jax.random.key(seed)
        ks = jax.random.split(key, 10)
        D = D_MODEL
        ddd = jnp.linspace(0.0, 1.0, D, dtype=jnp.float32)
        inp = {'x': jax.random.normal(ks[0], (B, T, D), jnp.float32), 'x_r': 1.0 - ddd ** 0.2, 'x_w': 1.0 - ddd ** 0.9, 'x_k': 1.0 - ddd ** 0.7, 'x_v': 1.0 - ddd ** 0.7, 'x_a': 1.0 - ddd ** 0.9, 'x_b': 1.0 - ddd ** 0.9, 'x_g': 1.0 - ddd ** 0.2, 'W_r': _xavier(ks[1], (D, D)), 'W_w': _xavier(ks[2], (D, D)), 'W_k': _xavier(ks[3], (D, D)), 'W_v': _xavier(ks[4], (D, D)), 'W_a': _xavier(ks[5], (D, D)), 'W_b': _xavier(ks[6], (D, D)), 'W_g': _xavier(ks[7], (D, D)), 'W_o': _xavier(ks[8], (D, D)) * 0.1, 'b_o': jnp.zeros((D,), jnp.float32), 'gn_w': jnp.ones((D,), jnp.float32), 'gn_b': jnp.zeros((D,), jnp.float32)}
        return inp
    _L1_attn_all = _L1_attn_setup()
    _L1_attn_in = {k: v for k, v in _L1_attn_all.items() if k in ('x_r', 'x_w', 'x_k', 'x_v', 'x_a', 'x_b', 'x_g', 'W_r', 'W_w', 'W_k', 'W_v', 'W_a', 'W_b', 'W_g', 'W_o', 'b_o', 'gn_w', 'gn_b')}
    del _L1_attn_all

    def _L1_xattn_setup():
        import jax, jax.numpy as jnp
        import numpy as np
        B, L, E, H = (4, 256, 128, 16)
        D = E // H
        NEG_INF = -1000000000.0

        def _rope(x):
            seq = x.shape[1]
            inv_freq = 1.0 / 10000.0 ** (jnp.arange(0, D, 2, dtype=jnp.float32) / D)
            ang = jnp.arange(seq, dtype=jnp.float32)[:, None] * inv_freq
            cos = jnp.concatenate([jnp.cos(ang), jnp.cos(ang)], axis=-1)[None, :, None, :]
            sin = jnp.concatenate([jnp.sin(ang), jnp.sin(ang)], axis=-1)[None, :, None, :]
            x1, x2 = jnp.split(x, 2, axis=-1)
            rot = jnp.concatenate([-x2, x1], axis=-1)
            return x * cos + rot * sin
        key = jax.random.key(seed)
        ks = jax.random.split(key, 12)
        xavier = lambda k: jax.random.uniform(k, (E, E), jnp.float32, -np.sqrt(6.0 / (E + E)), np.sqrt(6.0 / (E + E)))
        return {'query': jax.random.normal(ks[0], (B, L, E), jnp.float32), 'key': jax.random.normal(ks[1], (B, L, E), jnp.float32), 'value': jax.random.normal(ks[2], (B, L, E), jnp.float32), 'wq': xavier(ks[3]), 'bq': jnp.zeros((E,), jnp.float32), 'wk': xavier(ks[4]), 'bk': jnp.zeros((E,), jnp.float32), 'wv': xavier(ks[5]), 'bv': jnp.zeros((E,), jnp.float32), 'wo': xavier(ks[6]), 'bo': jnp.zeros((E,), jnp.float32), 'key_padding_mask': jax.random.randint(ks[7], (B, L), 0, 2).astype(bool)}
    _L1_xattn_all = _L1_xattn_setup()
    _L1_xattn_in = {k: v for k, v in _L1_xattn_all.items() if k in ('wq', 'bq', 'wk', 'bk', 'wv', 'bv', 'wo', 'bo')}
    del _L1_xattn_all

    def _L1_ffn_setup():
        import jax, jax.numpy as jnp
        import numpy as np
        BS, SLEN, DIM = (1, 256, 128)
        NUM_EXPERTS, TOP_K = (8, 2)
        HID = 176

        def _masked_grouped_mm(x, w, onehot):
            g = jnp.einsum('tk,gnk->tgn', x, w, preferred_element_type=jnp.float32)
            return jnp.einsum('tgn,tg->tn', g, onehot)

        def moe_forward(x, gate_w, expert_bias, w_up, w_down, shared_w_up, shared_w_down):
            bs, slen, dim = x.shape
            xf = x.reshape(-1, dim)
            scores = jax.nn.sigmoid((xf @ gate_w.T).astype(jnp.float32))
            biased = scores + expert_bias
            _, sel = jax.lax.top_k(biased, TOP_K)
            top_scores = jnp.take_along_axis(scores, sel, axis=-1)
            flat_sel = sel.reshape(-1)
            counts = jnp.bincount(flat_sel, length=NUM_EXPERTS)
            order = jnp.argsort(flat_sel, stable=True)
            scores_sorted = top_scores.reshape(-1)[order]
            token_ids = order // TOP_K
            routed_in = (xf[token_ids] * scores_sorted[:, None]).astype(x.dtype)
            seg = jnp.repeat(jnp.arange(NUM_EXPERTS), counts, total_repeat_length=flat_sel.shape[0])
            onehot = jax.nn.one_hot(seg, NUM_EXPERTS, dtype=jnp.float32)
            h = _masked_grouped_mm(routed_in.astype(jnp.bfloat16), w_up.astype(jnp.bfloat16), onehot)
            h = jnp.square(jax.nn.relu(h.astype(jnp.bfloat16)))
            routed_out = _masked_grouped_mm(h.astype(jnp.bfloat16), w_down.astype(jnp.bfloat16), onehot)
            routed_out = routed_out.astype(jnp.bfloat16).astype(x.dtype)
            hs = jnp.square(jax.nn.relu(xf @ shared_w_up.T))
            shared_out = hs @ shared_w_down.T
            combined = jnp.zeros((flat_sel.shape[0], dim), routed_out.dtype).at[order].set(routed_out)
            out = combined.reshape(-1, TOP_K, dim).sum(axis=1) + shared_out
            return out.reshape(bs, slen, dim)
        key = jax.random.key(seed)
        k = jax.random.split(key, 6)
        s = 0.02
        return {'x': jax.random.normal(k[0], (BS, SLEN, DIM), jnp.float32), 'gate_w': jax.random.normal(k[1], (NUM_EXPERTS, DIM), jnp.float32) * s, 'expert_bias': jnp.zeros((NUM_EXPERTS,), jnp.float32), 'w_up': jax.random.normal(k[2], (NUM_EXPERTS, HID, DIM), jnp.float32) * s, 'w_down': jax.random.normal(k[3], (NUM_EXPERTS, DIM, HID), jnp.float32) * s, 'shared_w_up': jax.random.normal(k[4], (HID, DIM), jnp.float32) * s, 'shared_w_down': jax.random.normal(k[5], (DIM, HID), jnp.float32) * s}
    _L1_ffn_all = _L1_ffn_setup()
    _L1_ffn_in = {k: v for k, v in _L1_ffn_all.items() if k in ('gate_w', 'expert_bias', 'w_up', 'w_down', 'shared_w_up', 'shared_w_down')}
    del _L1_ffn_all
    return {'x': x, 'ctx_1024': ctx_1024, '_lenS2': _lenS2, 'mask_BxS2_bk1': mask_BxS2_bk1, 'L0_attn_Wqkv': _L0_attn_in['Wqkv'], 'L0_attn_Wo': _L0_attn_in['Wo'], 'L0_xattn_wq': _L0_xattn_in['wq'], 'L0_xattn_wk': _L0_xattn_in['wk'], 'L0_xattn_wv': _L0_xattn_in['wv'], 'L0_xattn_wo': _L0_xattn_in['wo'], 'L0_xattn_bo': _L0_xattn_in['bo'], 'L0_ffn_router_w': _L0_ffn_in['router_w'], 'L0_ffn_router_b': _L0_ffn_in['router_b'], 'L0_ffn_w1': _L0_ffn_in['w1'], 'L0_ffn_w2': _L0_ffn_in['w2'], 'L1_attn_x_r': _L1_attn_in['x_r'], 'L1_attn_x_w': _L1_attn_in['x_w'], 'L1_attn_x_k': _L1_attn_in['x_k'], 'L1_attn_x_v': _L1_attn_in['x_v'], 'L1_attn_x_a': _L1_attn_in['x_a'], 'L1_attn_x_b': _L1_attn_in['x_b'], 'L1_attn_x_g': _L1_attn_in['x_g'], 'L1_attn_W_r': _L1_attn_in['W_r'], 'L1_attn_W_w': _L1_attn_in['W_w'], 'L1_attn_W_k': _L1_attn_in['W_k'], 'L1_attn_W_v': _L1_attn_in['W_v'], 'L1_attn_W_a': _L1_attn_in['W_a'], 'L1_attn_W_b': _L1_attn_in['W_b'], 'L1_attn_W_g': _L1_attn_in['W_g'], 'L1_attn_W_o': _L1_attn_in['W_o'], 'L1_attn_b_o': _L1_attn_in['b_o'], 'L1_attn_gn_w': _L1_attn_in['gn_w'], 'L1_attn_gn_b': _L1_attn_in['gn_b'], 'L1_xattn_wq': _L1_xattn_in['wq'], 'L1_xattn_bq': _L1_xattn_in['bq'], 'L1_xattn_wk': _L1_xattn_in['wk'], 'L1_xattn_bk': _L1_xattn_in['bk'], 'L1_xattn_wv': _L1_xattn_in['wv'], 'L1_xattn_bv': _L1_xattn_in['bv'], 'L1_xattn_wo': _L1_xattn_in['wo'], 'L1_xattn_bo': _L1_xattn_in['bo'], 'L1_ffn_gate_w': _L1_ffn_in['gate_w'], 'L1_ffn_expert_bias': _L1_ffn_in['expert_bias'], 'L1_ffn_w_up': _L1_ffn_in['w_up'], 'L1_ffn_w_down': _L1_ffn_in['w_down'], 'L1_ffn_shared_w_up': _L1_ffn_in['shared_w_up'], 'L1_ffn_shared_w_down': _L1_ffn_in['shared_w_down']}

def reference(x, ctx_1024, _lenS2, mask_BxS2_bk1, L0_attn_Wqkv, L0_attn_Wo, L0_xattn_wq, L0_xattn_wk, L0_xattn_wv, L0_xattn_wo, L0_xattn_bo, L0_ffn_router_w, L0_ffn_router_b, L0_ffn_w1, L0_ffn_w2, L1_attn_x_r, L1_attn_x_w, L1_attn_x_k, L1_attn_x_v, L1_attn_x_a, L1_attn_x_b, L1_attn_x_g, L1_attn_W_r, L1_attn_W_w, L1_attn_W_k, L1_attn_W_v, L1_attn_W_a, L1_attn_W_b, L1_attn_W_g, L1_attn_W_o, L1_attn_b_o, L1_attn_gn_w, L1_attn_gn_b, L1_xattn_wq, L1_xattn_bq, L1_xattn_wk, L1_xattn_bk, L1_xattn_wv, L1_xattn_bv, L1_xattn_wo, L1_xattn_bo, L1_ffn_gate_w, L1_ffn_expert_bias, L1_ffn_w_up, L1_ffn_w_down, L1_ffn_shared_w_up, L1_ffn_shared_w_down):
    import jax
    import jax.numpy as jnp

    def _L0_attn_ref(x, Wqkv, Wo):
        import jax, jax.numpy as jnp
        import numpy as np
        import math
        B, T, D, H = (2, 256, 128, 16)
        DH = D // H

        def rotate_half(x):
            x1 = x[..., ::2]
            x2 = x[..., 1::2]
            return jnp.stack((-x2, x1), axis=-1).reshape(x.shape)
        b, t, d = x.shape
        pos = jnp.arange(t, dtype=jnp.float32)
        freqs = jnp.exp(-math.log(10000.0) * jnp.arange(0, DH, 2, dtype=jnp.float32) / DH)
        angles = pos[:, None] * freqs[None, :]
        angles = jnp.repeat(angles, 2, axis=-1)
        sin = jnp.sin(angles)[None, None, :, :]
        cos = jnp.cos(angles)[None, None, :, :]
        qkv = x @ Wqkv.T
        q, k, v = jnp.split(qkv, 3, axis=-1)
        q = q.reshape(b, t, H, DH).transpose(0, 2, 1, 3)
        k = k.reshape(b, t, H, DH).transpose(0, 2, 1, 3)
        v = v.reshape(b, t, H, DH).transpose(0, 2, 1, 3)
        q = cos * q + rotate_half(q) * sin
        k = cos * k + rotate_half(k) * sin
        scores = jnp.einsum('bhqd,bhkd->bhqk', q, k) / math.sqrt(DH)
        causal = jnp.tril(jnp.ones((t, t), dtype=bool))
        scores = jnp.where(causal, scores, -jnp.inf)
        attn = jax.nn.softmax(scores, axis=-1)
        out = jnp.einsum('bhqk,bhkd->bhqd', attn, v)
        out = out.transpose(0, 2, 1, 3).reshape(b, t, d)
        return out @ Wo.T

    def _L0_xattn_ref(x, cache_k, cache_v, cache_len, wq, wk, wv, wo, bo):
        import jax, jax.numpy as jnp
        import numpy as np
        N_HEADS = 16
        B, T, C = x.shape
        S = cache_k.shape[1]
        H = N_HEADS
        hd = C // H
        q = x @ wq.T
        k_new = x @ wk.T
        v_new = x @ wv.T
        pos = jnp.arange(S)
        past_mask = (pos[None, :] < cache_len[:, None])[..., None]
        past_k = jnp.where(past_mask, cache_k, 0.0)
        past_v = jnp.where(past_mask, cache_v, 0.0)
        k = jnp.concatenate([past_k, k_new], axis=1)
        v = jnp.concatenate([past_v, v_new], axis=1)

        def to_heads(t):
            return t.reshape(B, t.shape[1], H, hd).transpose(0, 2, 1, 3)
        qh, kh, vh = (to_heads(q), to_heads(k), to_heads(v))
        scores = jnp.einsum('bhqd,bhkd->bhqk', qh, kh) / np.sqrt(hd).astype(np.float32)
        max_cl = jnp.max(cache_len)
        key_valid = jnp.concatenate([pos < max_cl, jnp.ones((T,), bool)])
        NEG = jnp.float32(-1e+30)
        scores = jnp.where(key_valid[None, None, None, :], scores, NEG)
        attn = jax.nn.softmax(scores, axis=-1)
        out = jnp.einsum('bhqk,bhkd->bhqd', attn, vh)
        out = out.transpose(0, 2, 1, 3).reshape(B, T, C)
        return out @ wo.T + bo

    def _L0_ffn_ref(x, router_w, router_b, w1, w2):
        import jax, jax.numpy as jnp
        import numpy as np
        TOP_K = 2
        E = w1.shape[0]
        logits = x @ router_w + router_b
        probs = jax.nn.softmax(logits, axis=-1)
        top_v, top_i = jax.lax.top_k(probs, TOP_K)
        gates = jnp.sum(jax.nn.one_hot(top_i, E + 1, dtype=x.dtype) * top_v[..., None], axis=-2)
        h = jax.nn.gelu(jnp.einsum('btd,edf->ebtf', x, w1), approximate=False)
        y = jnp.einsum('ebtf,efd->ebtd', h, w2)
        out = jnp.einsum('bte,ebtd->btd', gates[..., :E], y) + gates[..., E:] * x
        return out

    def _L1_attn_ref(x, x_r, x_w, x_k, x_v, x_a, x_b, x_g, W_r, W_w, W_k, W_v, W_a, W_b, W_g, W_o, b_o, gn_w, gn_b):
        import jax, jax.numpy as jnp
        import numpy as np
        D_MODEL = 128
        NHEAD = 16
        HEAD_DIM = D_MODEL // NHEAD
        GN_EPS = 0.00064
        NORM_EPS = 1e-06
        B, T = (4, 128)

        def _xavier(key, shape):
            lim = float(np.sqrt(6.0 / (shape[0] + shape[1])))
            return jax.random.uniform(key, shape, jnp.float32, -lim, lim)

        def _l2norm(t):
            n = jnp.linalg.norm(t, axis=-1, keepdims=True)
            return t / jnp.maximum(n, NORM_EPS)
        Bs, Ts, D = x.shape
        H, K = (NHEAD, HEAD_DIM)
        prev = jnp.concatenate([jnp.zeros_like(x[:, :1]), x[:, :-1]], axis=1)
        xx = prev - x

        def proj(mix, W):
            return jnp.einsum('btd,ed->bte', x + xx * mix, W)
        heads = lambda t: t.reshape(Bs, Ts, H, K)
        r = heads(proj(x_r, W_r))
        w = -jax.nn.softplus(heads(proj(x_w, W_w)))
        k = jnp.tanh(heads(proj(x_k, W_k)))
        v = heads(proj(x_v, W_v))
        a = _l2norm(heads(proj(x_a, W_a)))
        b = _l2norm(heads(proj(x_b, W_b)))
        g = jax.nn.sigmoid(proj(x_g, W_g))

        def step(S, ins):
            r_t, w_t, k_t, v_t, a_t, b_t = ins
            Sa = jnp.einsum('bhvk,bhk->bhv', S, a_t)
            S = S * jnp.exp(w_t)[:, :, None, :] + Sa[..., None] * b_t[:, :, None, :] + v_t[..., None] * k_t[:, :, None, :]
            o = jnp.einsum('bhvk,bhk->bhv', S, r_t)
            return (S, o)
        tm = lambda t: jnp.moveaxis(t, 1, 0)
        S0 = jnp.zeros((Bs, H, K, K), jnp.float32)
        _, o = jax.lax.scan(step, S0, (tm(r), tm(w), tm(k), tm(v), tm(a), tm(b)))
        mixed = jnp.moveaxis(o, 0, 1).reshape(Bs, Ts, D)
        gm = mixed.reshape(Bs * Ts, H, K)
        mu = gm.mean(-1, keepdims=True)
        var = gm.var(-1, keepdims=True)
        normed = ((gm - mu) * jax.lax.rsqrt(var + GN_EPS)).reshape(Bs * Ts, D)
        normed = (normed * gn_w + gn_b).reshape(Bs, Ts, D)
        return jnp.einsum('btd,ed->bte', normed * g, W_o) + b_o

    def _L1_xattn_ref(query, key, value, wq, bq, wk, bk, wv, bv, wo, bo, key_padding_mask):
        import jax, jax.numpy as jnp
        import numpy as np
        B, L, E, H = (4, 256, 128, 16)
        D = E // H
        NEG_INF = -1000000000.0

        def _rope(x):
            seq = x.shape[1]
            inv_freq = 1.0 / 10000.0 ** (jnp.arange(0, D, 2, dtype=jnp.float32) / D)
            ang = jnp.arange(seq, dtype=jnp.float32)[:, None] * inv_freq
            cos = jnp.concatenate([jnp.cos(ang), jnp.cos(ang)], axis=-1)[None, :, None, :]
            sin = jnp.concatenate([jnp.sin(ang), jnp.sin(ang)], axis=-1)[None, :, None, :]
            x1, x2 = jnp.split(x, 2, axis=-1)
            rot = jnp.concatenate([-x2, x1], axis=-1)
            return x * cos + rot * sin
        b, ql = (query.shape[0], query.shape[1])
        sl = key.shape[1]
        q = (query @ wq.T + bq).reshape(b, ql, H, D)
        k = (key @ wk.T + bk).reshape(b, sl, H, D)
        v = (value @ wv.T + bv).reshape(b, sl, H, D)
        q = _rope(q)
        k = _rope(k)
        causal = jnp.where(jnp.triu(jnp.ones((ql, sl), bool), k=1), NEG_INF, 0.0)
        kpm = jnp.where(key_padding_mask[:, None, None, :], NEG_INF, 0.0)
        mask = causal[None, None, :, :] + kpm
        scores = jnp.einsum('bqhd,bkhd->bhqk', q, k) / np.sqrt(D) + mask
        attn = jax.nn.softmax(scores, axis=-1)
        out = jnp.einsum('bhqk,bkhd->bqhd', attn, v).reshape(b, ql, E)
        return out @ wo.T + bo

    def _L1_ffn_ref(x, gate_w, expert_bias, w_up, w_down, shared_w_up, shared_w_down):
        import jax, jax.numpy as jnp
        import numpy as np
        BS, SLEN, DIM = (1, 256, 128)
        NUM_EXPERTS, TOP_K = (8, 2)
        HID = 176

        def _masked_grouped_mm(x, w, onehot):
            g = jnp.einsum('tk,gnk->tgn', x, w, preferred_element_type=jnp.float32)
            return jnp.einsum('tgn,tg->tn', g, onehot)

        def moe_forward(x, gate_w, expert_bias, w_up, w_down, shared_w_up, shared_w_down):
            bs, slen, dim = x.shape
            xf = x.reshape(-1, dim)
            scores = jax.nn.sigmoid((xf @ gate_w.T).astype(jnp.float32))
            biased = scores + expert_bias
            _, sel = jax.lax.top_k(biased, TOP_K)
            top_scores = jnp.take_along_axis(scores, sel, axis=-1)
            flat_sel = sel.reshape(-1)
            counts = jnp.bincount(flat_sel, length=NUM_EXPERTS)
            order = jnp.argsort(flat_sel, stable=True)
            scores_sorted = top_scores.reshape(-1)[order]
            token_ids = order // TOP_K
            routed_in = (xf[token_ids] * scores_sorted[:, None]).astype(x.dtype)
            seg = jnp.repeat(jnp.arange(NUM_EXPERTS), counts, total_repeat_length=flat_sel.shape[0])
            onehot = jax.nn.one_hot(seg, NUM_EXPERTS, dtype=jnp.float32)
            h = _masked_grouped_mm(routed_in.astype(jnp.bfloat16), w_up.astype(jnp.bfloat16), onehot)
            h = jnp.square(jax.nn.relu(h.astype(jnp.bfloat16)))
            routed_out = _masked_grouped_mm(h.astype(jnp.bfloat16), w_down.astype(jnp.bfloat16), onehot)
            routed_out = routed_out.astype(jnp.bfloat16).astype(x.dtype)
            hs = jnp.square(jax.nn.relu(xf @ shared_w_up.T))
            shared_out = hs @ shared_w_down.T
            combined = jnp.zeros((flat_sel.shape[0], dim), routed_out.dtype).at[order].set(routed_out)
            out = combined.reshape(-1, TOP_K, dim).sum(axis=1) + shared_out
            return out.reshape(bs, slen, dim)
        return moe_forward(x, gate_w, expert_bias, w_up, w_down, shared_w_up, shared_w_down)
    x = x + _L0_attn_ref(_layernorm(x, axis=-1), L0_attn_Wqkv, L0_attn_Wo)
    x = x + _L0_xattn_ref(_layernorm(x, axis=-1), ctx_1024, ctx_1024, _lenS2, L0_xattn_wq, L0_xattn_wk, L0_xattn_wv, L0_xattn_wo, L0_xattn_bo)
    x = x + _L0_ffn_ref(_layernorm(x, axis=-1), L0_ffn_router_w, L0_ffn_router_b, L0_ffn_w1, L0_ffn_w2)
    x = x + _L1_attn_ref(_layernorm(x, axis=-1), L1_attn_x_r, L1_attn_x_w, L1_attn_x_k, L1_attn_x_v, L1_attn_x_a, L1_attn_x_b, L1_attn_x_g, L1_attn_W_r, L1_attn_W_w, L1_attn_W_k, L1_attn_W_v, L1_attn_W_a, L1_attn_W_b, L1_attn_W_g, L1_attn_W_o, L1_attn_b_o, L1_attn_gn_w, L1_attn_gn_b)
    x = x + _L1_xattn_ref(_layernorm(x, axis=-1), ctx_1024, ctx_1024, L1_xattn_wq, L1_xattn_bq, L1_xattn_wk, L1_xattn_bk, L1_xattn_wv, L1_xattn_bv, L1_xattn_wo, L1_xattn_bo, mask_BxS2_bk1)
    x = x + _L1_ffn_ref(_layernorm(x, axis=-1), L1_ffn_gate_w, L1_ffn_expert_bias, L1_ffn_w_up, L1_ffn_w_down, L1_ffn_shared_w_up, L1_ffn_shared_w_down)
    return x

_drawn_inputs = setup_inputs


def setup_inputs(seed=0):
    import zlib

    import numpy as np

    out = dict(_drawn_inputs(seed))
    spreads = {'L0_xattn_bo': (0.0, 0.1),
     'L1_attn_b_o': (0.0, 0.1),
     'L1_attn_gn_w': (1.0, 0.6),
     'L1_attn_gn_b': (0.0, 0.8),
     'L1_xattn_bq': (0.0, 0.314),
     'L1_xattn_bk': (0.0, 0.758),
     'L1_xattn_bv': (0.0, 0.1),
     'L1_xattn_bo': (0.0, 0.1),
     'L1_ffn_expert_bias': (0.0, 0.8)}
    factors = {'L0_ffn_router_b': 5.771,
     'L0_ffn_w1': 6.66,
     'L0_ffn_w2': 6.55,
     'L1_attn_x_r': 3.465,
     'L1_attn_x_w': 8.0,
     'L1_attn_x_a': 4.054,
     'L1_attn_x_b': 3.913,
     'L1_attn_x_g': 8.0,
     'L1_attn_W_w': 3.911,
     'L1_attn_W_g': 3.54,
     'L1_ffn_gate_w': 8.0,
     'L1_ffn_w_up': 8.0,
     'L1_ffn_w_down': 8.0,
     'L1_ffn_shared_w_up': 4.773,
     'L1_ffn_shared_w_down': 4.453}
    for name, (base, spread) in spreads.items():
        noise = np.random.default_rng([zlib.crc32(name.encode()), seed]).standard_normal(out[name].shape)
        drawn = base * np.exp(spread * noise) if base else spread * noise
        out[name] = jnp.asarray(drawn.astype(out[name].dtype))
    for name, factor in factors.items():
        out[name] = (out[name] * factor).astype(out[name].dtype)
    return out
```

```python
from collections import namedtuple
from contextlib import ExitStack

import numpy as np

import concourse.bass as bass
from concourse import mybir

F32 = mybir.dt.float32
BF16 = mybir.dt.bfloat16
I32 = mybir.dt.int32
U32 = mybir.dt.uint32
U8 = mybir.dt.uint8
ALU = mybir.AluOpType
ACT = mybir.ActivationFunctionType
AX = mybir.AxisListType

P = 128
B, T, D = 4, 512, 128
H, DH = 16, 8
NT = T // P
SC = 77
KW = 592
LN_EPS = 1e-5
NEG = -1e30
NORM_EPS, GN_EPS = 1e-6, 0.00064
E0, F0 = 8, 512
E1, HID = 8, 176
ROW_MASK, ROW_HI, ROW_MAX, ROWS = 0, 1, 49, 52
HB, PB = 32, 16
NB = P // HB


def per(i, count, n):
    return i * count + n


def decoder(nc, io, out):
    with ExitStack() as ctx:
        def sb(name, shape, dt=F32):
            return ctx.enter_context(nc.sbuf_tensor(name, shape, dt))

        def group(stack):
            return lambda name, shape, dt=F32: stack.enter_context(nc.sbuf_tensor(name, shape, dt))

        cleared = []

        def signals(name, names, **facts):
            made = [cleared.pop() if cleared else sem(f"{name}_{n}") for n in names.split()]
            return namedtuple(name, names.split() + list(facts))(*made, **facts)

        def bank(name, shape, dt=F32):
            return ctx.enter_context(nc.psum_tensor(name, shape, dt))

        def sem(name):
            return ctx.enter_context(nc.semaphore(name))

        smax_bank = [bank(f"smax_bank{n}", [P, 512]) for n in range(2)]
        st_bank = [bank(f"st_bank{n}", [P, 2, 512]) for n in range(2)]
        pv_bank = bank("pv_bank", [P, 512])
        mix_bank = bank("mix_bank", [P, 512])
        mix_bf = mix_bank[:, :].bitcast(BF16)

        x_sb = sb("x_sb", [P, B, NT, D])
        ident = sb("ident", [P, P])
        ident_bf = sb("ident_bf", [P, P], BF16)
        mask_qk = sb("mask_qk", [P, P], BF16)
        mask_kq = sb("mask_kq", [P, P], BF16)
        neg_half = sb("neg_half", [P, NT])
        one_row = sb("one_row", [1, P])
        gn_eps = sb("gn_eps", [P, 1])

        stats = sb("stats", [P, NT, 6])
        meanvar = sb("meanvar", [P, NT, 2])
        sdev = sb("sdev", [P, NT])
        rstd = sb("rstd", [P, NT])
        xn = sb("xn", [P, NT, D])
        xT = sb("xT", [P, T])
        q_stack = sb("q_stack", [ROWS, H, T], BF16)
        blk_ones = sb("blk_ones", [P, P])
        blk_mean = sb("blk_mean", [P, P])

        layer0 = ExitStack()
        sa = group(layer0)
        bo0x = sa("bo0x", [1, D])
        w0x = sa("w0x", [P, 4, D])
        w0 = sa("w0", [P, 6, D])
        rope0 = sa("rope0", [P, 4, T])
        turn_a = sa("turn_a", [P, 2, T])
        turn_b = sa("turn_b", [P, 2, T])
        qk_f = sa("qk_f", [P, 2, T])
        qk_r = sa("qk_r", [P, 2, T])
        parts = sa("parts", [P, 2, 3, T], BF16)
        k_stack = sa("k_stack", [ROWS, H, KW], BF16)
        v_aug = sa("v_aug", [P, NT + 1, H, 32])
        mx = sa("mx", [P, 2, NT, 4])
        mxc = sa("mxc", [P, 2, NT, 4])
        mx_f = sa("mx_f", [P, 2, 2, NT, 4])
        mx_parts = sa("mx_parts", [P, 2, NT, 3, 4], BF16)
        mx_rows = sa("mx_rows", [12, 2, T], BF16)
        NPR = 4
        probs = sa("probs", [P, NPR, 2, 512])
        heads_T = sa("heads_T", [P, 2, T])
        rden = sa("rden", [P, 2, NT, 4])
        heads = sa("heads", [P, NT, D])
        hT = sa("hT", [P, T])

        ctx_hd = sa("ctx_hd", [SC, B, D])
        ctx_dh = sa("ctx_dh", [SC, B, D])
        len_i = sa("len_i", [P, B], I32)
        len_f = sa("len_f", [P, B])
        len_max = sa("len_max", [P, 1])
        pos_col = sa("pos_col", [P, 1])
        keep = sa("keep", [P, B])
        pos_row = sa("pos_row", [1, H * SC])
        mask_row = sa("mask_row", [1, H * SC], BF16)
        cparts = sa("cparts", [P, 3, SC], BF16)
        cres = sa("cres", [P, SC])
        ctxT = sa("ctxT", [P, SC])

        ctx_now = sa("ctx_now", [SC, 2, D])
        layer0.close()

        ffn0 = ExitStack()
        sf = group(ffn0)
        up0 = sf("up0", [P, E0, F0])
        down0 = sf("down0", [P, E0, F0 // P, D])
        router_w = sf("router_w", [P, E0 + 1])
        router_b = sf("router_b", [1, E0 + 1])
        places = sf("places", [P, E0 + 1])
        lmax = sf("lmax", [P, NT])
        shifted = sf("shifted", [P, NT, E0 + 1])
        expd = sf("expd", [P, NT, E0 + 1])
        esum = sf("esum", [P, NT])
        erec = sf("erec", [P, NT])
        gprobs = sf("gprobs", [P, NT, E0 + 1])
        top_v = sf("top_v", [P, NT, 8])
        top_i = sf("top_i", [P, NT, 8], U32)
        top_f = sf("top_f", [P, NT, 8])
        gate_a = sf("gate_a", [P, NT, E0 + 1])
        gate_b = sf("gate_b", [P, NT, E0 + 1])
        gates = sf("gates", [P, NT, E0 + 1])
        hidden = sf("hidden", [P, 2, F0 // P, T])
        ffn0.close()

        rec = ExitStack()
        sr = group(rec)
        w1a = sr("w1a", [P, 8, D])
        mix1 = sr("mix1", [P, 7])
        bo1a = sr("bo1a", [1, D])
        gn_w = sr("gn_w", [P, 1])
        gn_b = sr("gn_b", [P, 1])
        xs = sr("xs", [P, 2, B, P + 1])
        xx = sr("xx", [P, B, P])
        xi = sr("xi", [P, 3, T])
        dense = sr("dense", [P, 6, T])
        gate_T = sr("gate_T", [P, NT, T])
        sq = sr("sq", [P, 2, T])
        nrm = sr("nrm", [P, 2, T])
        inv = sr("inv", [P, 2, T])
        seqs = sr("seqs", [P, 2, 5, DH, P])
        seq_v = sr("seq_v", [P, 2, DH // 2, P])
        by_state = sr("by_state", [P, 2, 3, DH, PB])
        dot_prod = sr("dot_prod", [P, 2, 4, DH, PB])
        dots = sr("dots", [P, 2, 4, PB])
        kb_w = sr("kb_w", [P, 2, 2, DH, PB])
        kb_dot = sr("kb_dot", [P, 2, 2, DH, PB])
        rows_kb = sr("rows_kb", [P, 2, 3, DH, PB])
        vk = sr("vk", [P, 2, PB, DH // 2, DH])
        state0 = sr("state0", [P, DH // 2, DH])
        hist = sr("hist", [P, 2, PB, DH // 2, DH])
        terms = sr("terms", [P, 2, PB, 6, DH // 2, DH])
        sums = sr("sums", [P, 2, PB, 2, DH // 2])
        first_r = sr("first_r", [P, 2, DH, PB])
        o_prod = sr("o_prod", [P, 2, PB, 2, DH // 2, DH])
        o_more = sr("o_more", [P, 2, 3, DH // 2, PB])
        o_seq = sr("o_seq", [P, 2, DH // 2, P])
        o_T = sr("o_T", [P, B, P])
        o_cen = sr("o_cen", [P, T])
        o_sq = sr("o_sq", [P, T])
        o_sd = sr("o_sd", [P, T])
        o_inv = sr("o_inv", [P, T])
        o_n = sr("o_n", [P, T])
        rec.close()

        cross1 = ExitStack()
        sx = group(cross1)
        w1x = sx("w1x", [P, 6, D])
        b1x = sx("b1x", [P, 4])
        bv1x = sx("bv1x", [1, D])
        bo1x = sx("bo1x", [1, D])
        rope1 = sx("rope1", [P, 4, T])
        ctx1 = sx("ctx1", [SC, B, D])
        ctx1_T = sx("ctx1_T", [P, B, SC])
        pad_i = sx("pad_i", [P, B, SC], I32)
        pad_f = sx("pad_f", [P, B, SC])
        causal1 = sx("causal1", [P, SC])
        mask1 = sx("mask1", [P, B, SC])
        mask1c = sx("mask1c", [P, B, SC])
        turn1_a = sx("turn1_a", [P, T])
        turn1_b = sx("turn1_b", [P, T])
        full1 = sx("full1", [P, T])
        res1 = sx("res1", [P, T])
        parts1 = sx("parts1", [P, 3, T], BF16)
        k1_stack = sx("k1_stack", [ROW_MAX, B, H, SC], BF16)
        v1_aug = sx("v1_aug", [SC, B, H, 32])
        t1 = sx("t1", [P, 2, H, SC])
        mx1 = sx("mx1", [P, 2, H])
        t2 = sx("t2", [P, 2, H, SC])
        p1 = sx("p1", [P, 2, H, SC])
        p1_T = sx("p1_T", [SC, 2, H, P])
        o1_T = sx("o1_T", [P, 2, 4, P])
        rden1 = sx("rden1", [P, 2, 4, 4])
        heads1 = sx("heads1", [P, B, D])
        h1_T = sx("h1_T", [P, B, P])
        cross1.close()

        ffn1 = ExitStack()
        sm = group(ffn1)
        gate1_w = sm("gate1_w", [P, E1])
        bias1 = sm("bias1", [P, NT, E1])
        up1_f = sm("up1_f", [P, E1, HID])
        down1_f = sm("down1_f", [P, 2, E1, D])
        up1 = sm("up1", [P, E1, HID], BF16)
        down1 = sm("down1", [P, 2, E1, D], BF16)
        sup = sm("sup", [P, HID])
        sdown = sm("sdown", [P, 2, D])
        pick1 = sm("pick1", [64, E1, P], BF16)
        places1 = sm("places1", [P, E1])
        scores1 = sm("scores1", [P, NT, E1])
        biased1 = sm("biased1", [P, NT, E1])
        top1_v = sm("top1_v", [P, NT, 8])
        top1_i = sm("top1_i", [P, NT, 8], U32)
        top1_f = sm("top1_f", [P, NT, 8])
        sel_a = sm("sel_a", [P, NT, E1])
        sel_b = sm("sel_b", [P, NT, E1])
        sel_s = sm("sel_s", [P, NT, E1])
        wgt1 = sm("wgt1", [P, NT, E1])
        wgt_r = sm("wgt_r", [P, NT, E1])
        wgt_parts = sm("wgt_parts", [P, NT, 3, E1], BF16)
        wgt_T = sm("wgt_T", [64, 2, T], BF16)
        x1_T = sm("x1_T", [P, 2, T])
        rin = sm("rin", [P, 2, T], BF16)
        hr_bf = sm("hr_bf", [P, 2, 2, T], BF16)
        h2_bf = sm("h2_bf", [P, 2, 2, T], BF16)
        hs_r = sm("hs_r", [P, 2, T])
        hs_2 = sm("hs_2", [P, 2, T])
        y1 = sm("y1", [P, 2, B, D], BF16)
        ffn1.close()

        scr_qk = nc.dram_tensor("scr_qk", [2, 3, P, T], BF16, kind="Internal").ap()
        scr_mx = nc.dram_tensor("scr_mx", [2, 12, T], BF16, kind="Internal").ap()
        scr_c = nc.dram_tensor("scr_c", [3, P, SC], BF16, kind="Internal").ap()

        s_load = sem("s_load")
        s_init = sem("s_init")
        s_out = sem("s_out")
        ln = signals("ln", "stats mv sd rs xn tr xT")

        loads = [
            (x_sb[:, 0, :, :], io["x"][0].rearrange("(c p) d -> p c d", p=P)),
            (x_sb[:, 1, :, :], io["x"][1].rearrange("(c p) d -> p c d", p=P)),
            (x_sb[:, 2, :, :], io["x"][2].rearrange("(c p) d -> p c d", p=P)),
            (x_sb[:, 3, :, :], io["x"][3].rearrange("(c p) d -> p c d", p=P)),
            (ident[:, :], io["ident"]), (ident_bf[:, :], io["ident_bf"]),
            (mask_qk[:, :], io["mask_qk"]), (mask_kq[:, :], io["mask_kq"]),
            (rope0[:, :, :], io["rope0"]),
            (w0[:, :, :], io["w0"]), (w0x[:, :, :], io["w0x"]), (bo0x[:, :], io["bo0x"]),
            (q_stack[0:1, :, :].rearrange("p h t -> p (h t)"), io["ones_row"][:, 0:H * T]),
            (k_stack[0:1, :, :].rearrange("p h t -> p (h t)"), io["zero_row"]),
            (k_stack[ROW_MAX:ROWS, :, :].rearrange("p h t -> p (h t)"), io["ones_rows"]),
            (ctx_hd[:, :, :], io["ctx"].rearrange("b s d -> s b d")),
            (ctx_dh[:, :, :], io["ctx_dh"].rearrange("b s d -> s b d")),
            (len_i[:, :], io["lens"].partition_broadcast(P)),
            (blk_ones[:, :], io["blk_ones"]), (blk_mean[:, :], io["blk_mean"]),
            (pos_col[:, :], io["pos_col"]), (pos_row[:, :], io["pos_row"]),
        ]
        LOADED = 16 * len(loads)
        INIT = 5

        ATTENTION = ("proj turned qk_sum v_in scr_in stack smax mx_done mx_comb mx_split mx_tr mx_row mx_scr mx_in st ex pv heads_T "
                     "heads_Tt rden heads heads_tr hT wo res q_parts k_parts mx_chain")

        def uses_of_mix():
            order = [("ln", 0), ("mx", 0)]
            for g in range(4):
                if g < 3:
                    order.append(("mx", g + 1))
                order.append(("heads", g))
            return order + [("hT", 0), ("wo", 0)]

        def attention(name, causal, weights, k0, more=""):
            names = ATTENTION + more
            tiles = [(kt * P, P, kt * P if causal else 0) for kt in range(NT)]
            if not causal:
                tiles.append((T, SC, 0))
            a = signals(name, names, causal=causal, w=weights, k0=k0, tiles=tiles,
                        units=[(qt, j) for qt in range(NT) for j in range(4 if causal else 5)],
                        steps=[(kt, pair) for kt in range(len(tiles)) for pair in range(2)],
                        turned_n=4 if causal else 2, stack_n=16 * (9 if causal else 12), v_n=1 if causal else 2, chain_n=4,
                        mix_order=uses_of_mix())
            in_block_1.extend(a[:len(names.split())])
            return a

        def mix_waits(a, eng, i, use):
            order = a.mix_order
            k = order.index(use)
            if k:
                kind, g = order[k - 1]
                if kind == "ln":
                    eng.wait_ge(ln.xT, per(a.k0 + i, 1, 1))
                elif kind == "mx":
                    eng.wait_ge(a.mx_row, per(i, 4, g + 1))
                elif kind == "heads":
                    eng.wait_ge(a.heads, per(i, 4, g + 1))
                elif kind == "hT":
                    eng.wait_ge(a.hT, per(i, 1, 1))

        def pe_attention(pe, i, a):
            NU, NS = len(a.units), len(a.steps)
            n_proj = 5 if a.causal else 3
            for c in range(NT):
                pe.wait_ge(ln.xn, per(a.k0 + i, NT, c + 1))
                pe.transpose(mix_bank[:, c * P:(c + 1) * P], xn[:, c, :], ident[:, :]).then_inc(ln.tr, 1)
            pe.wait_ge(ln.xT, per(a.k0 + i, 1, 1))
            dst = [smax_bank[0][:, :], smax_bank[1][:, :], st_bank[0][:, 0, :], st_bank[0][:, 1, :]]
            for n in range(n_proj - 1):
                pe.matmul(dst[n] if a.causal else dst[2 * n], a.w[:, n, :], xT[:, :], start=True, stop=True).then_inc(a.proj, 1)
            for c in range(NT):
                m = pe.matmul(st_bank[1][:, 0, c * P:(c + 1) * P], xT[:, c * P:(c + 1) * P], a.w[:, n_proj - 1, :],
                              start=True, stop=True)
            m.then_inc(a.proj, 1)
            if not a.causal:
                pe.wait_ge(a.ctx_copy, per(i, 2, 2))
                pe.transpose(st_bank[1][:, 1, 0:SC], ctx_now[:, 1, :], ident[0:SC, 0:SC]).then_inc(a.ctx_tr, 1)

            def scores_for_max(g, u):
                n = g * NU + u
                qt, j = a.units[u]
                if n == 0:
                    pe.wait_ge(a.stack, per(i, a.stack_n, a.stack_n))
                if n >= 2:
                    pe.wait_ge(a.mx_done, per(i, 4 * NU, n - 1))
                else:
                    pe.wait_ge(a.turned, per(i, a.turned_n, a.turned_n))
                dst = smax_bank[n % 2]
                if j < 4:
                    h = 4 * g + j
                    w = (qt + 1) * P if a.causal else T
                    m = pe.matmul(dst[:, 0:w], q_stack[0:ROW_MAX, h, qt * P:(qt + 1) * P], k_stack[0:ROW_MAX, h, 0:w],
                                  start=True, stop=not a.causal)
                    if a.causal:
                        m = pe.matmul(dst[:, qt * P:w], ident_bf[:, :], mask_qk[:, :], start=False, stop=True)
                else:
                    for jj in range(4):
                        h = 4 * g + jj
                        m = pe.matmul(dst[:, jj * SC:(jj + 1) * SC], q_stack[0:ROW_MAX, h, qt * P:(qt + 1) * P],
                                      k_stack[0:ROW_MAX, h, T:T + SC], start=True, stop=True)
                m.then_inc(a.smax, 1)

            def turn_max(g):
                pe.wait_ge(a.mx_split, per(i, 4, g + 1))
                mix_waits(a, pe, i, ("mx", g))
                for qt in range(NT):
                    m = pe.transpose(mix_bf[0:12, qt * P:(qt + 1) * P],
                                     mx_parts[:, g % 2, qt, :, :].rearrange("p c j -> p (c j)"), ident_bf[:, :])
                m.then_inc(a.mx_tr, 1)

            def scores(g, s):
                n = g * NS + s
                kt, pair = a.steps[s]
                k0, kn, q0 = a.tiles[kt]
                if s == 0:
                    pe.wait_ge(a.mx_in, per(i, 64, 16 * (g + 1)))
                if n >= 2:
                    pe.wait_ge(a.ex, per(i, 4 * NS, n - 1))
                elif n == 0:
                    pe.wait_ge(a.v_in, per(i, a.v_n, a.v_n))
                for jj in range(2):
                    h = 4 * g + 2 * pair + jj
                    m = pe.matmul(st_bank[n % 2][0:kn, jj, 0:T - q0], k_stack[:, h, k0:k0 + kn], q_stack[:, h, q0:T],
                                  start=True, stop=not a.causal)
                    if a.causal:
                        m = pe.matmul(st_bank[n % 2][:, jj, 0:P], ident_bf[:, :], mask_kq[:, :], start=False, stop=True)
                m.then_inc(a.st, 1)

            def weigh(g, s):
                n = g * NS + s
                kt, pair = a.steps[s]
                k0, kn, q0 = a.tiles[kt]
                pe.wait_ge(a.ex, per(i, 4 * NS, n + 1))
                if s == 0 and g:
                    pe.wait_ge(a.heads_T, per(i, 4, g))
                for jj in range(2):
                    j = 2 * pair + jj
                    m = pe.matmul(pv_bank[32 * j:32 * j + 32, q0:T], v_aug[0:kn, kt, 4 * g + j, :],
                                  probs[0:kn, n % NPR, jj, 0:T - q0], start=(kt == 0), stop=(kt == len(a.tiles) - 1))
                m.then_inc(a.pv, 1)

            def turn_heads(g):
                pe.wait_ge(a.heads_T, per(i, 4, g + 1))
                mix_waits(a, pe, i, ("heads", g))
                for qt in range(NT):
                    m = pe.transpose(mix_bank[:, qt * P:(qt + 1) * P], heads_T[:, g % 2, qt * P:(qt + 1) * P], ident[:, :])
                m.then_inc(a.heads_Tt, 1)

            for u in range(NU):
                scores_for_max(0, u)
            turn_max(0)
            for g in range(4):
                u = 0
                for s in range(NS):
                    scores(g, s)
                    if s >= 2:
                        weigh(g, s - 2)
                    if s == 4 and g:
                        turn_heads(g - 1)
                    while g < 3 and u < min(NU, 3 * (s + 1)):
                        scores_for_max(g + 1, u)
                        u += 1
                while g < 3 and u < NU:
                    scores_for_max(g + 1, u)
                    u += 1
                weigh(g, NS - 2)
                weigh(g, NS - 1)
                if g < 3:
                    turn_max(g + 1)
            turn_heads(3)
            pe.wait_ge(a.heads, per(i, 4, 4))
            for qt in range(NT):
                m = pe.transpose(mix_bank[:, qt * P:(qt + 1) * P], heads[:, qt, :], ident[:, :])
            m.then_inc(a.heads_tr, 1)
            pe.wait_ge(a.hT, per(i, 1, 1))
            for qt in range(NT):
                out_q = mix_bank[:, qt * P:(qt + 1) * P]
                if not a.causal:
                    pe.matmul(out_q, one_row[:, :], bo0x[:, :], start=True, stop=False)
                m = pe.matmul(out_q, hT[:, qt * P:(qt + 1) * P], a.w[:, n_proj, :], start=a.causal, stop=True)
            m.then_inc(a.wo, 1)

        def dve_norm_stats(dve, i, a, x_tiles):
            for c in range(NT):
                dve.bn_stats(stats[:, c, :], x_tiles(c)).then_inc(ln.stats, 1)
            for c in range(NT):
                dve.wait_ge(ln.stats, per(a.k0 + i, NT, c + 1))
                dve.bn_aggr(meanvar[:, c, :], stats[:, c, :]).then_inc(ln.mv, 1)

        def dve_norm_apply(dve, i, a, x_tiles):
            dve.wait_ge(ln.rs, per(a.k0 + i, 1, 1))
            for c in range(NT):
                dve.tensor_scalar(xn[:, c, :], x_tiles(c), meanvar[:, c, 0:1], rstd[:, c:c + 1],
                                  ALU.subtract, ALU.mult).then_inc(ln.xn, 1)

        def dve_norm(dve, i, a, x_tiles):
            dve_norm_stats(dve, i, a, x_tiles)
            dve_norm_apply(dve, i, a, x_tiles)

        def dve_attention(dve, i, a):
            NU = len(a.units)

            def x_tile(c):
                return x_sb[:, i, c, :]

            dve_norm(dve, i, a, x_tile)
            if a.causal:
                src = [smax_bank[0][:, :], smax_bank[1][:, :], st_bank[0][:, 0, :], st_bank[0][:, 1, :]]
                for n in range(2):
                    dve.wait_ge(a.proj, per(i, 5, 2 * n + 1))
                    dve.tensor_tensor(turn_a[:, n, :], src[2 * n], rope0[:, 2 * n, :], ALU.mult).then_inc(a.turned, 1)
                    dve.wait_ge(a.proj, per(i, 5, 2 * n + 2))
                    dve.tensor_tensor(turn_b[:, n, :], src[2 * n + 1], rope0[:, 2 * n + 1, :], ALU.mult).then_inc(a.turned, 1)
                    dve.wait_ge(a.turned, per(i, 4, 2 * n + 2))
                    dve.tensor_tensor(qk_f[:, n, :], turn_a[:, n, :], turn_b[:, n, :], ALU.add).then_inc(a.qk_sum, 1)
            else:
                dve.wait_ge(a.proj, per(i, 3, 1))
                dve.tensor_scalar(qk_f[:, 0, :], smax_bank[0][:, :], DH ** -0.5, None, ALU.mult).then_inc(a.turned, 1)
                dve.wait_ge(a.proj, per(i, 3, 2))
                dve.tensor_copy(qk_f[:, 1, :], st_bank[0][:, 0, :]).then_inc(a.turned, 1)
                dve.wait_ge(a.ctx_tr, per(i, 1, 1))
                dve.tensor_copy(ctxT[:, :], st_bank[1][:, 1, 0:SC]).then_inc(a.ctx_f, 1)

            def split(dst, res, full, done, before, count, base):
                dve.tensor_copy(dst(0), full).then_inc(done, 1)
                dve.wait_ge(done, per(i, count, base + 1))
                dve.tensor_tensor(res, full, dst(0), ALU.subtract).then_inc(done, 1)
                dve.wait_ge(done, per(i, count, base + 2))
                dve.tensor_copy(dst(1), res).then_inc(done, 1)
                dve.wait_ge(done, per(i, count, base + 3))
                dve.tensor_tensor(dst(2), res, dst(1), ALU.subtract).then_inc(done, 1)

            if a.causal:
                dve.wait_ge(a.qk_sum, per(i, 2, 1))
            else:
                dve.wait_ge(a.turned, per(i, 2, 1))
            split(lambda c: parts[:, 0, c, :], qk_r[:, 0, :], qk_f[:, 0, :], a.q_parts, None, 4, 0)
            if not a.causal:
                dve.wait_ge(a.ctx_f, per(i, 1, 1))
                split(lambda c: cparts[:, c, :], cres[:, :], ctxT[:, :], a.c_parts, None, 4, 0)

            def maxima(g):
                for u, (qt, j) in enumerate(a.units):
                    n = g * NU + u
                    dve.wait_ge(a.smax, per(i, 4 * NU, n + 1))
                    if u == 0 and g >= 2:
                        dve.wait_ge(a.mx_split, per(i, 4, g - 1))
                    if j < 4:
                        w = (qt + 1) * P if a.causal else T
                        dve.tensor_reduce(mx[:, g % 2, qt, j:j + 1], smax_bank[n % 2][:, 0:w], AX.X, ALU.max).then_inc(a.mx_done, 1)
                    else:
                        dve.tensor_reduce(mxc[:, g % 2, qt, :], smax_bank[n % 2][:, 0:4 * SC].rearrange("p (j s) -> p j s", s=SC),
                                          AX.X, ALU.max).then_inc(a.mx_done, 1)
                if not a.causal:
                    dve.wait_ge(a.mx_done, per(i, 4 * NU, (g + 1) * NU))
                    dve.tensor_tensor(mx[:, g % 2, :, :], mx[:, g % 2, :, :], mxc[:, g % 2, :, :], ALU.max).then_inc(a.mx_comb, 1)

            def normalize(g):
                dve.wait_ge(a.heads_Tt, per(i, 4, g + 1))
                src = mix_bank[:, :].rearrange("p (q j d) -> p q j d", q=NT, j=4)
                dve.reciprocal(rden[:, g % 2, :, :], src[:, :, :, DH]).then_inc(a.rden, 1)
                dve.wait_ge(a.rden, per(i, 4, g + 1))
                for qt in range(NT):
                    m = dve.tensor_tensor(heads[:, qt, 32 * g:32 * g + 32].rearrange("p (j d) -> p j d", d=DH), src[:, qt, :, 0:DH],
                                          rden[:, g % 2, qt, :].unsqueeze(2).to_broadcast([P, 4, DH]), ALU.mult)
                m.then_inc(a.heads, 1)

            maxima(0)
            for g in range(4):
                if g < 3:
                    maxima(g + 1)
                if g:
                    normalize(g - 1)
            normalize(3)
            dve.wait_ge(a.wo, per(i, 1, 1))
            xi = x_sb[:, i, :, :].rearrange("p c d -> p (c d)")
            dve.tensor_tensor(xi, xi, mix_bank[:, :], ALU.add).then_inc(a.res, 1)
            dve.wait_ge(a.res, per(i, 1, 1))

        def act_attention(act, i, a):
            NS = len(a.steps)
            act.wait_ge(ln.tr, per(a.k0 + i, NT, NT))
            act.activation(xT[:, :], mix_bank[:, :], ACT.Copy).then_inc(ln.xT, 1)
            act.wait_ge(a.proj, per(i, 5 if a.causal else 3, 5 if a.causal else 3))
            act.activation(v_aug[:, 0:NT, :, 0:DH], st_bank[1][:, 0, :].rearrange("p (c h d) -> p c h d", c=NT, h=H),
                           ACT.Copy).then_inc(a.v_in, 1)

            def max_rows(g):
                act.wait_ge(a.mx_tr, per(i, 4, g + 1))
                if g >= 2:
                    act.wait_ge(a.mx_scr, per(i, 64, 16 * (g - 1)))
                act.activation(mx_rows[:, g % 2, :], mix_bf[0:12, 0:T], ACT.Copy).then_inc(a.mx_row, 1)

            def take_heads(g):
                act.wait_ge(a.pv, per(i, 4 * NS, (g + 1) * NS))
                if g >= 2:
                    act.wait_ge(a.heads_Tt, per(i, 4, g - 1))
                act.activation(heads_T[:, g % 2, :], pv_bank[:, :], ACT.Copy).then_inc(a.heads_T, 1)

            max_rows(0)
            for g in range(4):
                for s, (kt, pair) in enumerate(a.steps):
                    n = g * NS + s
                    k0, kn, q0 = a.tiles[kt]
                    act.wait_ge(a.st, per(i, 4 * NS, n + 1))
                    if n >= NPR:
                        act.wait_ge(a.pv, per(i, 4 * NS, n - NPR + 1))
                    act.activation(probs[0:kn, n % NPR, :, 0:T - q0], st_bank[n % 2][0:kn, :, 0:T - q0],
                                   ACT.Exp).then_inc(a.ex, 1)
                    if s == 1 and g:
                        take_heads(g - 1)
                if g < 3:
                    max_rows(g + 1)
            take_heads(3)
            act.wait_ge(a.heads_tr, per(i, 1, 1))
            act.activation(hT[:, :], mix_bank[:, :], ACT.Copy).then_inc(a.hT, 1)

        def pool_norm(pool, i, a):
            pool.wait_ge(ln.mv, per(a.k0 + i, NT, NT))
            pool.tensor_scalar(sdev[:, :], meanvar[:, :, 1], LN_EPS, None, ALU.add).then_inc(ln.sd, 1)
            pool.wait_ge(ln.sd, per(a.k0 + i, 1, 1))
            pool.tensor_tensor(rstd[:, :], sdev[:, :], neg_half[:, :], ALU.pow).then_inc(ln.rs, 1)

        def pool_attention(pool, i, a):
            pool_norm(pool, i, a)
            if a.causal:
                pool.wait_ge(a.qk_sum, per(i, 2, 2))
            else:
                for n, src in enumerate((ctx_hd, ctx_dh)):
                    pool.tensor_scalar(ctx_now[:, n, :], src[:, i, :],
                                       keep[0:SC, i:i + 1], None, ALU.mult).then_inc(a.ctx_copy, 1)
                pool.wait_ge(a.ctx_copy, per(i, 2, 2))
                pool.tensor_copy(v_aug[0:SC, NT, :, 0:DH], ctx_now[:, 0, :].rearrange("p (h d) -> p h d", h=H)).then_inc(a.v_in, 1)
                pool.wait_ge(a.turned, per(i, 2, 2))
            full, res = qk_f[:, 1, :], qk_r[:, 1, :]
            dst = [parts[:, 1, c, :] for c in range(3)]
            pool.tensor_copy(dst[0], full).then_inc(a.k_parts, 1)
            pool.wait_ge(a.k_parts, per(i, 4, 1))
            pool.tensor_tensor(res, full, dst[0], ALU.subtract).then_inc(a.k_parts, 1)
            pool.wait_ge(a.k_parts, per(i, 4, 2))
            pool.tensor_copy(dst[1], res).then_inc(a.k_parts, 1)
            pool.wait_ge(a.k_parts, per(i, 4, 3))
            pool.tensor_tensor(dst[2], res, dst[1], ALU.subtract).then_inc(a.k_parts, 1)
            NU = len(a.units)
            CH = a.chain_n
            for g in range(4):
                b0 = CH * g
                pool.wait_ge(a.mx_done, per(i, 4 * NU, (g + 1) * NU))
                if g >= 2:
                    pool.wait_ge(a.mx_tr, per(i, 4, g - 1))
                if not a.causal:
                    pool.wait_ge(a.mx_comb, per(i, 4, g + 1))
                neg, res = mx_f[:, g % 2, 0, :, :], mx_f[:, g % 2, 1, :, :]
                part = [mx_parts[:, g % 2, :, c, :] for c in range(3)]
                pool.tensor_scalar(neg, mx[:, g % 2, :, :], -1.0, None, ALU.mult).then_inc(a.mx_chain, 1)
                pool.wait_ge(a.mx_chain, per(i, 4 * CH, b0 + 1))
                pool.tensor_copy(part[0], neg).then_inc(a.mx_chain, 1)
                pool.wait_ge(a.mx_chain, per(i, 4 * CH, b0 + 2))
                pool.tensor_tensor(res, neg, part[0], ALU.subtract).then_inc(a.mx_chain, 1)
                pool.wait_ge(a.mx_chain, per(i, 4 * CH, b0 + 3))
                pool.tensor_copy(part[1], res).then_inc(a.mx_chain, 1)
                pool.wait_ge(a.mx_chain, per(i, 4 * CH, b0 + 4))
                pool.tensor_tensor(part[2], res, part[1], ALU.subtract).then_inc(a.mx_split, 1)

        def sp_attention(sp, i, a):
            def rows(n):
                return scr_qk[n].rearrange("c (d h) t -> (c d) h t", h=H)

            if not a.causal and i == 0:
                sp.wait_ge(s_mask, 1)
                sp.dma_start(k_stack[0:1, :, T:T + SC], mask_row[:, :].rearrange("p (h s) -> p h s", h=H)).then_inc(a.mask_in, 16)
            sp.wait_ge(a.q_parts, per(i, 4, 4))
            sp.dma_start(scr_qk[0].rearrange("c p t -> p c t"), parts[:, 0, :, :]).then_inc(a.scr_in, 16)
            sp.wait_ge(a.k_parts, per(i, 4, 4))
            sp.dma_start(scr_qk[1].rearrange("c p t -> p c t"), parts[:, 1, :, :]).then_inc(a.scr_in, 16)
            n_scr = 32 if a.causal else 48
            if not a.causal:
                sp.wait_ge(a.c_parts, per(i, 4, 4))
                sp.dma_start(scr_c.rearrange("c p t -> p c t"), cparts[:, :, :]).then_inc(a.scr_in, 16)
            sp.wait_ge(a.scr_in, per(i, n_scr, n_scr))
            flat = scr_qk[0].rearrange("c (d h) t -> c d (h t)", h=H)
            at = ROW_HI
            for c, times in ((0, 3), (1, 2), (2, 1)):
                for _ in range(times):
                    sp.dma_start(q_stack[at:at + DH, :, :].rearrange("p h t -> p (h t)"), flat[c]).then_inc(a.stack, 16)
                    at += DH
            at = ROW_HI
            for last in (3, 2, 1):
                sp.dma_start(k_stack[at:at + DH * last, :, 0:T], rows(1)[0:DH * last]).then_inc(a.stack, 16)
                at += DH * last
            if not a.causal:
                at = ROW_HI
                for last in (3, 2, 1):
                    sp.dma_start(k_stack[at:at + DH * last, :, T:T + SC],
                                 scr_c.rearrange("c (d h) t -> (c d) h t", h=H)[0:DH * last]).then_inc(a.stack, 16)
                    at += DH * last
                if i == 0:
                    sp.wait_ge(a.mask_in, 16)
            for g in range(4):
                sp.wait_ge(a.mx_row, per(i, 4, g + 1))
                sp.dma_start(scr_mx[g % 2], mx_rows[:, g % 2, :]).then_inc(a.mx_scr, 16)
                sp.wait_ge(a.mx_scr, per(i, 64, 16 * (g + 1)))
                sp.dma_start(q_stack[ROW_MAX:ROWS, 4 * g:4 * g + 4, :].rearrange("p h t -> p (h t)"),
                             scr_mx[g % 2].rearrange("(c j) t -> c (j t)", c=3)).then_inc(a.mx_in, 16)

        s_mask = sem("s_mask")
        s_len = sem("s_len")
        in_block_1 = []
        own = attention("own", True, w0, 0)
        cross = attention("cross", False, w0x, B, " ctx_copy ctx_tr ctx_f c_parts mask_in")
        cleared.extend(in_block_1)

        def chunk(c):
            return lambda b: x_sb[:, b, c, :]

        def pe_norm(pe, c, a, to=None):
            to = mix_bank[:, :] if to is None else to
            for b in range(B):
                pe.wait_ge(ln.xn, per(a.k0 + c, B, b + 1))
                pe.transpose(to[:, b * P:(b + 1) * P], xn[:, b, :], ident[:, :]).then_inc(ln.tr, 1)

        def tiles(ap):
            return ap.rearrange("p (b t) -> p b t", b=B)

        ring = [smax_bank[0][:, :], smax_bank[1][:, :], st_bank[0][:, 0, :], st_bank[0][:, 1, :]]
        y_bank = [st_bank[1][:, 0, :], st_bank[1][:, 1, :]]
        mix = mix_bank[:, :]

        f = signals("ffn0", "load logits lmax shift exp sum rec prob top idx idxf ga gb gates up gelu down skip acc", k0=2 * B)
        NF = F0 // P
        ffn0_loads = [(up0[:, :, :], "up0"), (down0[:, :, :, :], "down0"), (router_w[:, :], "router_w"),
                      (router_b[:, :], "router_b"), (places[:, :], "places")]

        def pe_ffn0(pe, c):
            pe_norm(pe, c, f)
            pe.wait_ge(ln.xT, f.k0 + c + 1)
            logits = mix[:, 0:B * 16].rearrange("p (b e) -> p b e", e=16)
            for b in range(B):
                pe.matmul(logits[:, b, 0:E0 + 1], one_row[:, :], router_b[:, :], start=True, stop=False)
                m = pe.matmul(logits[:, b, 0:E0 + 1], xT[:, b * P:(b + 1) * P], router_w[:, :], start=False, stop=True)
            m.then_inc(f.logits, 1)

            def up(e):
                for n in range(NF):
                    k = NF * e + n
                    if k >= 4:
                        pe.wait_ge(f.gelu, per(c, E0 * NF, k - 3))
                    pe.matmul(ring[k % 4], up0[:, e, n * P:(n + 1) * P], xT[:, :], start=True, stop=True).then_inc(f.up, 1)

            def down(e):
                if e >= 2:
                    pe.wait_ge(f.acc, per(c, E0 * B, (e - 1) * B))
                pe.wait_ge(f.gelu, per(c, E0 * NF, NF * (e + 1)))
                for b in range(B):
                    for n in range(NF):
                        m = pe.matmul(y_bank[e % 2][:, b * P:(b + 1) * P], hidden[:, e % 2, n, b * P:(b + 1) * P], down0[:, e, n, :],
                                      start=(n == 0), stop=(n == NF - 1))
                m.then_inc(f.down, 1)

            up(0)
            up(1)
            for e in range(E0):
                down(e)
                if e + 2 < E0:
                    up(e + 2)

        def dve_ffn0(dve, c):
            dve_norm(dve, c, f, chunk(c))
            logits = mix[:, 0:B * 16].rearrange("p (b e) -> p b e", e=16)[:, :, 0:E0 + 1]
            wide = [P, B, E0 + 1]
            dve.wait_ge(f.logits, c + 1)
            dve.tensor_reduce(lmax[:, :], logits, AX.X, ALU.max).then_inc(f.lmax, 1)
            dve.wait_ge(f.lmax, c + 1)
            dve.tensor_tensor(shifted[:, :, :], logits, lmax[:, :].unsqueeze(2).to_broadcast(wide), ALU.subtract).then_inc(f.shift, 1)
            dve.wait_ge(f.exp, c + 1)
            dve.tensor_reduce(esum[:, :], expd[:, :, :], AX.X, ALU.add).then_inc(f.sum, 1)
            dve.wait_ge(f.sum, c + 1)
            dve.reciprocal(erec[:, :], esum[:, :]).then_inc(f.rec, 1)
            dve.wait_ge(f.rec, c + 1)
            dve.tensor_tensor(gprobs[:, :, :], expd[:, :, :], erec[:, :].unsqueeze(2).to_broadcast(wide), ALU.mult).then_inc(f.prob, 1)
            dve.wait_ge(f.prob, c + 1)
            for b in range(B):
                dve.max(top_v[:, b, :], gprobs[:, b, :]).then_inc(f.top, 1)
            for b in range(B):
                dve.wait_ge(f.top, per(c, B, b + 1))
                dve.max_index(top_i[:, b, :], top_v[:, b, :], gprobs[:, b, :]).then_inc(f.idx, 1)
            dve.wait_ge(f.idx, per(c, B, B))
            dve.tensor_copy(top_f[:, :, :], top_i[:, :, :]).then_inc(f.idxf, 1)
            dve.wait_ge(f.idxf, c + 1)
            for b in range(B):
                dve.tensor_scalar(gate_a[:, b, :], places[:, :], top_f[:, b, 0:1], top_v[:, b, 0:1], ALU.is_equal, ALU.mult).then_inc(f.ga, 1)
                dve.tensor_scalar(gate_b[:, b, :], places[:, :], top_f[:, b, 1:2], top_v[:, b, 1:2], ALU.is_equal, ALU.mult).then_inc(f.gb, 1)
            dve.wait_ge(f.ga, per(c, B, B))
            dve.wait_ge(f.gb, per(c, B, B))
            dve.tensor_tensor(gates[:, :, :], gate_a[:, :, :], gate_b[:, :, :], ALU.add).then_inc(f.gates, 1)
            dve.wait_ge(f.gates, c + 1)
            for b in range(B):
                dve.scalar_tensor_tensor(out=x_sb[:, b, c, :], in0=xn[:, b, :], scalar=gates[:, b, E0:E0 + 1], in1=x_sb[:, b, c, :],
                                         op0=ALU.mult, op1=ALU.add).then_inc(f.skip, 1)
            dve.wait_ge(f.skip, per(c, B, B))
            for e in range(E0):
                if e:
                    dve.wait_ge(f.acc, per(c, E0 * B, e * B))
                dve.wait_ge(f.down, per(c, E0, e + 1))
                for b in range(B):
                    dve.scalar_tensor_tensor(out=x_sb[:, b, c, :], in0=y_bank[e % 2][:, b * P:(b + 1) * P],
                                             scalar=gates[:, b, e:e + 1], in1=x_sb[:, b, c, :],
                                             op0=ALU.mult, op1=ALU.add).then_inc(f.acc, 1)
            dve.wait_ge(f.acc, per(c + 1, E0 * B, 0))

        def act_ffn0(act, c):
            act.wait_ge(ln.tr, per(f.k0 + c, B, B))
            act.activation(xT[:, :], mix, ACT.Copy).then_inc(ln.xT, 1)
            act.wait_ge(f.shift, c + 1)
            act.activation(expd[:, :, :], shifted[:, :, :], ACT.Exp).then_inc(f.exp, 1)

            def gelu(e):
                for n in range(NF):
                    k = NF * e + n
                    act.wait_ge(f.up, per(c, E0 * NF, k + 1))
                    if e >= 2:
                        act.wait_ge(f.down, per(c, E0, e - 1))
                    act.activation(hidden[:, e % 2, n, :], ring[k % 4], ACT.Gelu).then_inc(f.gelu, 1)

            for e in range(E0):
                gelu(e)

        r = signals("rec", "init load edge xx mixed proj kept sq n2 n2f n2s inv unit scr seq "
                    "dprod dots kbd rows vkp vk prod sum outer step wr oprod osum omore oadd oscr oT mean cen osq var sd oinv on gn gated wo res", k0=2 * B + NT)
        rec_loads = [(w1a[:, :, :], "w1a"), (mix1[:, :], "mix1"), (bo1a[:, :], "bo1a"), (gn_w[:, :], "gn_w"), (gn_b[:, :], "gn_b")]
        R_, W_, K_, V_, A_, B_, G_ = range(7)
        scr_seq = nc.dram_tensor("scr_seq", [6, B, D, T], F32, kind="Internal").ap()
        scr_o = nc.dram_tensor("scr_o", [B * H, DH, T], F32, kind="Internal").ap()
        PLACE = {K_: 0, B_: 1, A_: 2, W_: 3, R_: 4}

        def pe_rec(pe, c):
            pe_norm(pe, c, r)
            for n in range(7):
                pe.wait_ge(r.mixed, per(c, 7, n + 1))
                if n >= 4:
                    pe.wait_ge(r.kept, per(c, 5, n - 3))
                pe.matmul(ring[n % 4], w1a[:, n, :], xi[:, n % 3, :], start=True, stop=True).then_inc(r.proj, 1)
                if n in (A_, B_):
                    pe.wait_ge(r.sq, per(c, 2, n - A_ + 1))
                    pe.matmul(y_bank[n - A_], blk_ones[:, :], sq[:, n - A_, :], start=True, stop=True).then_inc(r.n2, 1)

        def dve_rec_mix(dve, c, which):
            dve.wait_ge(r.xx, c + 1)
            dve.wait_ge(ln.xT, r.k0 + c + 1)
            for n in which:
                if n >= 3:
                    dve.wait_ge(r.proj, per(c, 7, n - 2))
                dve.scalar_tensor_tensor(out=tiles(xi[:, n % 3, :]), in0=xx[:, :, :], scalar=mix1[:, n:n + 1],
                                         in1=xs[:, c % 2, :, 1:P + 1], op0=ALU.mult, op1=ALU.add).then_inc(r.mixed, 1)

        def dve_rec_norms(dve, c):
            for k in range(2):
                dve.wait_ge(r.n2, per(c, 2, k + 1))
                dve.tensor_scalar(nrm[:, k, :], y_bank[k], NORM_EPS ** 2, None, ALU.max).then_inc(r.n2f, 1)

        def dve_rec_units(dve, c):
            for k in range(2):
                dve.wait_ge(r.n2s, per(c, 2, k + 1))
                dve.reciprocal(inv[:, k, :], sq[:, k, :]).then_inc(r.inv, 1)
            if c:
                dve.wait_ge(r.scr, per(c - 1, 96, 96))
            for k in range(2):
                dve.wait_ge(r.inv, per(c, 2, k + 1))
                dve.tensor_tensor(dense[:, A_ + k, :], ring[(A_ + k) % 4], inv[:, k, :], ALU.mult).then_inc(r.unit, 1)

        def act_rec(act, c):
            act.wait_ge(ln.tr, per(r.k0 + c, B, B))
            act.activation(xs[:, c % 2, :, 1:P + 1], mix.rearrange("p (b t) -> p b t", b=B), ACT.Copy).then_inc(ln.xT, 1)
            func = {R_: ACT.Copy, W_: ACT.Sigmoid, K_: ACT.Tanh, V_: ACT.Copy}
            for n in (R_, W_, K_, V_):
                act.wait_ge(r.proj, per(c, 7, n + 1))
                if c:
                    act.wait_ge(r.scr, per(c - 1, 96, 96))
                act.activation(dense[:, n, :], ring[n % 4], func[n], scale=-1.0 if n == W_ else 1.0).then_inc(r.kept, 1)
            for k in range(2):
                act.wait_ge(r.proj, per(c, 7, A_ + k + 1))
                act.activation(sq[:, k, :], ring[(A_ + k) % 4], ACT.Square).then_inc(r.sq, 1)
            act.wait_ge(r.proj, per(c, 7, 7))
            act.activation(gate_T[:, c, :], ring[G_ % 4], ACT.Sigmoid).then_inc(r.kept, 1)
            for k in range(2):
                act.wait_ge(r.n2f, per(c, 2, k + 1))
                act.activation(sq[:, k, :], nrm[:, k, :], ACT.Sqrt).then_inc(r.n2s, 1)

        def pool_rec_before(pool, c):
            pool.wait_ge(ln.xT, r.k0 + c + 1)
            if c:
                pool.tensor_copy(xs[:, c % 2, :, 0:1], xs[:, (c - 1) % 2, :, P:P + 1]).then_inc(r.edge, 1)
                pool.wait_ge(r.edge, c)
            pool.tensor_tensor(xx[:, :, :], xs[:, c % 2, :, 0:P], xs[:, c % 2, :, 1:P + 1], ALU.subtract).then_inc(r.xx, 1)

        def sp_rec(sp, c):
            span = slice(c * P, (c + 1) * P)
            for k, n in enumerate((R_, W_, K_, V_, A_, B_)):
                if n >= A_:
                    sp.wait_ge(r.unit, per(c, 2, n - A_ + 1))
                else:
                    sp.wait_ge(r.kept, per(c, 5, n + 1))
                sp.dma_start(scr_seq[n].rearrange("b r t -> r b t")[:, :, span], tiles(dense[:, n, :])).then_inc(r.scr, 16)
            sp.wait_ge(r.scr, per(c, 96, 96))
            if c >= 2:
                sp.wait_ge(r.oadd, (c - 1) * NB)
            for k, n in enumerate((R_, W_, K_, V_, A_, B_)):
                src = scr_seq[n].rearrange("b (h k) t -> (b h) k t", h=H)
                for half in range(2):
                    rows = src[:, 4 * half:4 * half + 4, span] if n == V_ else src[:, :, span]
                    to = seq_v[:, c % 2, :, :] if n == V_ else seqs[:, c % 2, PLACE[n], :, :]
                    sp.dma_start(to[64 * half:64 * half + 64], rows).then_inc(r.seq, 16)

        I = DH // 2
        KB = slice(0, 2)

        def seq_of(blk, which, first):
            t0 = (blk % NB) * HB
            return seqs[:, (blk // NB) % 2, which, :, t0 + 1 - first:t0 + HB:2]

        def v_of(blk, first):
            t0 = (blk % NB) * HB
            return seq_v[:, (blk // NB) % 2, :, t0 + 1 - first:t0 + HB:2]

        def pool_pairs_a(pool, blk):
            buf = blk % 2
            two = [P, 2, DH, PB]
            pool.wait_ge(r.seq, per(blk // NB, 192, 192))
            if blk >= 2:
                pool.wait_ge(r.step, (blk - 1) * PB)
            kb = seq_of(blk, KB, 1)
            pool.tensor_tensor(dot_prod[:, buf, 0:2, :, :], kb, seq_of(blk, PLACE[A_], 0).unsqueeze(1).to_broadcast(two), ALU.mult)
            pool.tensor_tensor(dot_prod[:, buf, 2:4, :, :], kb, seq_of(blk, PLACE[R_], 1).unsqueeze(1).to_broadcast(two),
                               ALU.mult).then_inc(r.dprod, 1)
            pool.tensor_tensor(kb_w[:, buf, :, :, :], kb, seq_of(blk, PLACE[W_], 0).unsqueeze(1).to_broadcast(two), ALU.mult)
            pool.tensor_copy(by_state[:, buf, 0, :, :], seq_of(blk, PLACE[A_], 1))
            pool.tensor_tensor(by_state[:, buf, 1:3, :, :], seq_of(blk, slice(PLACE[A_], PLACE[W_] + 1), 0),
                               seq_of(blk, PLACE[W_], 1).unsqueeze(1).to_broadcast(two), ALU.mult)
            pool.tensor_copy(rows_kb[:, buf, 2, :, :], seq_of(blk, PLACE[B_], 0)).then_inc(r.wr, 1)

        def dve_dots(dve, blk):
            dve.wait_ge(r.dprod, blk + 1)
            if blk >= 2:
                dve.wait_ge(r.omore, 3 * (blk - 1))
            dve.tensor_reduce(dots[:, blk % 2, :, :], dot_prod[:, blk % 2, :, :, :].rearrange("p x k t -> p x t k"), AX.X,
                              ALU.add).then_inc(r.dots, 1)

        def pool_pairs_b(pool, blk):
            buf = blk % 2
            two = [P, 2, DH, PB]
            pool.wait_ge(r.dots, blk + 1)
            pool.wait_ge(r.wr, blk + 1)
            pool.tensor_tensor(kb_dot[:, buf, :, :, :], dots[:, buf, 0:2, :].unsqueeze(2).to_broadcast(two),
                               rows_kb[:, buf, 2, :, :].unsqueeze(1).to_broadcast(two), ALU.mult).then_inc(r.kbd, 1)
            pool.wait_ge(r.kbd, blk + 1)
            pool.tensor_tensor(rows_kb[:, buf, 0:2, :, :], kb_dot[:, buf, :, :, :], kb_w[:, buf, :, :, :], ALU.add).then_inc(r.rows, 1)
            wide = [P, PB, I, DH]
            pool.tensor_tensor(vk[:, 1, :, :, :], v_of(blk, 0).rearrange("p i t -> p t i").unsqueeze(3).to_broadcast(wide),
                               seq_of(blk, PLACE[K_], 0).rearrange("p k t -> p t k").unsqueeze(2).to_broadcast(wide), ALU.mult)
            pool.wait_ge(r.rows, blk + 1)
            pool.tensor_tensor(vk[:, 0, :, :, :], v_of(blk, 1).rearrange("p i t -> p t i").unsqueeze(3).to_broadcast(wide),
                               rows_kb[:, buf, 0, :, :].rearrange("p k t -> p t k").unsqueeze(2).to_broadcast(wide),
                               ALU.mult).then_inc(r.vkp, 1)
            pool.wait_ge(r.vkp, blk + 1)
            pool.tensor_tensor(terms[:, buf, :, 5, :, :], vk[:, 0, :, :, :], vk[:, 1, :, :, :], ALU.add).then_inc(r.vk, 1)

        def dve_steps(dve, c, t0, t1):
            for n in range((c * P + t0) // 2, (c * P + t1) // 2):
                blk, s = n // PB, n % PB
                buf = blk % 2
                if s == 0:
                    dve.wait_ge(r.vk, blk + 1)
                    if blk >= 2:
                        dve.wait_ge(r.oadd, blk - 1)
                if n:
                    dve.wait_ge(r.step, n)
                    prev = hist[:, ((n - 1) // PB) % 2, (n - 1) % PB, :, :]
                else:
                    prev = state0[:, :, :]
                dve.tensor_tensor(terms[:, buf, s, 0:3, :, :], prev.unsqueeze(1).to_broadcast([P, 3, I, DH]),
                                  by_state[:, buf, :, :, s].unsqueeze(2).to_broadcast([P, 3, I, DH]), ALU.mult).then_inc(r.prod, 1)
                dve.wait_ge(r.prod, n + 1)
                dve.tensor_reduce(sums[:, buf, s, :, :], terms[:, buf, s, 0:2, :, :], AX.X, ALU.add).then_inc(r.sum, 1)
                dve.wait_ge(r.sum, n + 1)
                dve.tensor_tensor(terms[:, buf, s, 3:5, :, :], sums[:, buf, s, :, :].unsqueeze(3).to_broadcast([P, 2, I, DH]),
                                  rows_kb[:, buf, 1:3, :, s].unsqueeze(2).to_broadcast([P, 2, I, DH]), ALU.mult).then_inc(r.outer, 1)
                dve.wait_ge(r.outer, n + 1)
                dve.tensor_reduce(hist[:, buf, s, :, :], terms[:, buf, s, 2:6, :, :].rearrange("p x i k -> p i k x"), AX.X,
                                  ALU.add).then_inc(r.step, 1)
                if s == 5 and blk + 1 < NT * NB:
                    dve_dots(dve, blk + 1)
                if s == 10 and blk:
                    dve_outputs(dve, blk - 1)

        def pool_products(pool, blk):
            buf = blk % 2
            pool.tensor_tensor(first_r[:, buf, :, :], seq_of(blk, PLACE[W_], 1), seq_of(blk, PLACE[R_], 1), ALU.mult).then_inc(r.omore, 1)
            pool.wait_ge(r.step, (blk + 1) * PB)
            if blk >= 2:
                pool.wait_ge(r.osum, blk - 1)
            wide = [P, PB, I, DH]
            pool.tensor_tensor(o_prod[:, buf, :, 1, :, :], hist[:, buf, :, :, :],
                               seq_of(blk, PLACE[R_], 0).rearrange("p k t -> p t k").unsqueeze(2).to_broadcast(wide), ALU.mult)
            by = first_r[:, buf, :, :].rearrange("p k t -> p t k").unsqueeze(2).to_broadcast(wide)
            before = hist[:, 1 - buf, PB - 1:PB, :, :] if blk else state0[:, :, :].unsqueeze(1)
            pool.wait_ge(r.omore, 3 * blk + 1)
            pool.tensor_tensor(o_prod[:, buf, 0:1, 0, :, :], before, by[:, 0:1], ALU.mult)
            pool.tensor_tensor(o_prod[:, buf, 1:PB, 0, :, :], hist[:, buf, 0:PB - 1, :, :], by[:, 1:PB], ALU.mult).then_inc(r.oprod, 1)
            small = [P, I, PB]
            pool.tensor_tensor(o_more[:, buf, 0, :, :], sums[:, buf, :, 0, :].rearrange("p t i -> p i t"),
                               dots[:, buf, 3, :].unsqueeze(1).to_broadcast(small), ALU.mult)
            pool.tensor_tensor(o_more[:, buf, 1, :, :], v_of(blk, 1), dots[:, buf, 2, :].unsqueeze(1).to_broadcast(small),
                               ALU.mult).then_inc(r.omore, 1)
            pool.wait_ge(r.omore, 3 * blk + 2)
            pool.tensor_tensor(o_more[:, buf, 2, :, :], o_more[:, buf, 0, :, :], o_more[:, buf, 1, :, :], ALU.add).then_inc(r.omore, 1)

        def dve_outputs(dve, blk):
            c, t0 = blk // NB, (blk % NB) * HB
            dve.wait_ge(r.oprod, blk + 1)
            if c >= 2 and t0 == 0:
                dve.wait_ge(r.oscr, per(c - 2, 32, 32))
            dve.tensor_reduce(o_seq[:, c % 2, :, t0:t0 + HB].rearrange("p i (s x) -> p s x i", x=2), o_prod[:, blk % 2, :, :, :, :],
                              AX.X, ALU.add).then_inc(r.osum, 1)

        def pool_outputs(pool, blk):
            c, t0 = blk // NB, (blk % NB) * HB
            o1 = o_seq[:, c % 2, :, t0:t0 + HB:2]
            pool.wait_ge(r.osum, blk + 1)
            pool.wait_ge(r.omore, 3 * blk + 3)
            pool.tensor_tensor(o1, o1, o_more[:, blk % 2, 2, :, :], ALU.add).then_inc(r.oadd, 1)

        def sp_out1(sp, c):
            span = slice(c * P, (c + 1) * P)
            sp.wait_ge(r.oadd, per(c, NB, NB))
            for half in range(2):
                sp.dma_start(scr_o[:, 4 * half:4 * half + 4, span], o_seq[64 * half:64 * half + 64, c % 2, :, :]).then_inc(r.oscr, 16)
            sp.wait_ge(r.oscr, per(c, 32, 32))
            if c:
                sp.wait_ge(r.cen, c)
            sp.dma_start(o_T[:, :, :],
                         scr_o.rearrange("(b h) v t -> b (h v) t", b=B).rearrange("b r t -> r b t")[:, :, span]).then_inc(r.oT, 16)

        def pe_out1(pe, c):
            pe.wait_ge(r.unit, per(min(c + 2, NT - 1), 2, 2))
            pe.wait_ge(r.oT, per(c, 16, 16))
            pe.matmul(ring[0], blk_mean[:, :], o_T[:, :, :], start=True, stop=True).then_inc(r.mean, 1)
            pe.wait_ge(r.osq, c + 1)
            pe.matmul(ring[1], blk_mean[:, :], o_sq[:, :], start=True, stop=True).then_inc(r.var, 1)
            pe.wait_ge(r.gated, c + 1)
            for b in range(B):
                pe.matmul(mix[:, b * P:(b + 1) * P], one_row[:, :], bo1a[:, :], start=True, stop=False)
                m = pe.matmul(mix[:, b * P:(b + 1) * P], o_n[:, b * P:(b + 1) * P], w1a[:, 7, :], start=False, stop=True)
            m.then_inc(r.wo, 1)

        def dve_out1_center(dve, c):
            dve.wait_ge(r.mean, c + 1)
            dve.tensor_tensor(tiles(o_cen[:, :]), o_T[:, :, :], tiles(ring[0]), ALU.subtract).then_inc(r.cen, 1)

        def dve_out1_norm(dve, c):
            dve.wait_ge(r.sd, c + 1)
            dve.reciprocal(o_inv[:, :], o_sd[:, :]).then_inc(r.oinv, 1)
            dve.wait_ge(r.oinv, c + 1)
            dve.tensor_tensor(o_n[:, :], o_cen[:, :], o_inv[:, :], ALU.mult).then_inc(r.on, 1)
            dve.wait_ge(r.on, c + 1)
            dve.tensor_scalar(o_cen[:, :], o_n[:, :], gn_w[:, 0:1], gn_b[:, 0:1], ALU.mult, ALU.add).then_inc(r.gn, 1)
            dve.wait_ge(r.gn, c + 1)
            dve.tensor_tensor(o_n[:, :], o_cen[:, :], gate_T[:, c, :], ALU.mult).then_inc(r.gated, 1)

        def dve_out1_residual(dve, c):
            dve.wait_ge(r.wo, c + 1)
            dve.tensor_tensor(x_sb[:, :, c, :], x_sb[:, :, c, :], mix.rearrange("p (b d) -> p b d", b=B), ALU.add).then_inc(r.res, 1)
            dve.wait_ge(r.res, c + 1)

        def act_out1(act, c):
            act.wait_ge(r.cen, c + 1)
            act.activation(o_sq[:, :], o_cen[:, :], ACT.Square).then_inc(r.osq, 1)
            act.wait_ge(r.var, c + 1)
            act.activation(o_sd[:, :], ring[1], ACT.Sqrt, bias=gn_eps[:, :]).then_inc(r.sd, 1)

        z = signals("cross1", "init load ctxT ctxTs ck ckt kf kparts cscr cstk cv cvs pad padf pm proj turned full split scr "
                    "stack sc masked mx sub ex ptr pT pv o1 o1t rd hd hdt hT wo res", k0=2 * B + 2 * NT)
        cross1_loads = [(w1x[:, :, :], "w1x"), (b1x[:, :], "b1x"), (bv1x[:, :], "bv1x"), (bo1x[:, :], "bo1x"),
                        (rope1[:, :, :], "rope1"), (causal1[:, :], "causal1")]
        scr_k1 = nc.dram_tensor("scr_k1", [3, P, B, SC], BF16, kind="Internal").ap()
        scr_q1 = nc.dram_tensor("scr_q1", [3, P, T], BF16, kind="Internal").ap()
        NSC = B * SC
        HEADS_OF = [(0, 6), (6, 6), (12, 4)]

        def pe_ctx1(pe):
            for b in range(B):
                m = pe.transpose(mix[:, b * SC:(b + 1) * SC], ctx1[:, b, :], ident[0:SC, 0:SC])
            m.then_inc(z.ctxT, 1)
            pe.wait_ge(z.ctxTs, 1)
            for n in range(2):
                pe.matmul(ring[n][:, 0:NSC], w1x[:, 2 + n, :], ctx1_T[:, :, :].rearrange("p b s -> p (b s)"),
                          start=True, stop=True).then_inc(z.ck, 1)
            for b in range(B):
                pe.matmul(ring[2][0:SC, b * P:(b + 1) * P], one_row[:, 0:SC], bv1x[:, :], start=True, stop=False)
                m = pe.matmul(ring[2][0:SC, b * P:(b + 1) * P], ctx1_T[:, b, :], w1x[:, 4, :], start=False, stop=True)
            m.then_inc(z.cv, 1)

        def dve_ctx1(dve):
            flat = [turn1_a[:, 0:NSC], turn1_b[:, 0:NSC]]
            for n in range(2):
                dve.wait_ge(z.ck, n + 1)
                table = rope1[:, 2 + n, 0:SC].unsqueeze(1).to_broadcast([P, B, SC])
                dve.scalar_tensor_tensor(out=flat[n].rearrange("p (b s) -> p b s", b=B),
                                         in0=ring[n][:, 0:NSC].rearrange("p (b s) -> p b s", b=B),
                                         scalar=b1x[:, 2 + n:3 + n], in1=table, op0=ALU.add, op1=ALU.mult).then_inc(z.ckt, 1)
            dve.wait_ge(z.ckt, 2)
            dve.tensor_tensor(full1[:, 0:NSC], flat[0], flat[1], ALU.add).then_inc(z.kf, 1)
            dve.wait_ge(z.kf, 1)
            split(dve, [parts1[:, k, 0:NSC] for k in range(3)], res1[:, 0:NSC], full1[:, 0:NSC], z.kparts, 0)
            dve.tensor_copy(pad_f[:, :, :], pad_i[:, :, :]).then_inc(z.pad, 1)
            dve.wait_ge(z.pad, 1)
            dve.tensor_scalar(mask1[:, :, :], pad_f[:, :, :], -1e9, None, ALU.mult).then_inc(z.padf, 1)
            dve.wait_ge(z.padf, 1)
            dve.tensor_tensor(mask1c[:, :, :], mask1[:, :, :], causal1[:, :].unsqueeze(1).to_broadcast([P, B, SC]),
                              ALU.add).then_inc(z.pm, 1)
            dve.wait_ge(z.pm, 1)

        def act_ctx1(act):
            act.wait_ge(z.ctxT, 1)
            act.activation(ctx1_T[:, :, :], mix[:, 0:NSC].rearrange("p (b s) -> p b s", b=B), ACT.Copy).then_inc(z.ctxTs, 1)
            act.wait_ge(z.cv, 1)
            act.wait_ge(z.init, 3)
            for b in range(B):
                act.activation(v1_aug[:, b, :, 0:DH], ring[2][0:SC, b * P:(b + 1) * P].rearrange("p (h d) -> p h d", h=H),
                               ACT.Copy).then_inc(z.cvs, 1)

        def sp_ctx1(sp):
            sp.wait_ge(z.kparts, 4)
            sp.dma_start(scr_k1.rearrange("k p b s -> p k (b s)"), parts1[:, :, 0:NSC]).then_inc(z.cscr, 16)
            sp.wait_ge(z.cscr, 16)
            sp.wait_ge(z.init, 3)
            for b in range(B):
                rows = scr_k1.rearrange("k (d h) b s -> (k d) b h s", h=H)
                at = ROW_HI
                for last in (3, 2, 1):
                    sp.dma_start(k1_stack[at:at + DH * last, b, :, :], rows[0:DH * last, b]).then_inc(z.cstk, 16)
                    at += DH * last

        q_bank = ring[3]

        def pe_query1(pe, c, n):
            if n == 0:
                pe.wait_ge(ln.xT, z.k0 + c + 1)
            else:
                pe.wait_ge(z.turned, per(c, 2, 1))
            pe.matmul(q_bank, w1x[:, n, :], xT[:, :], start=True, stop=True).then_inc(z.proj, 1)

        def dve_query1(dve, c, n):
            dve.wait_ge(z.proj, per(c, 2, n + 1))
            table = rope1[:, n, c * P:(c + 1) * P].unsqueeze(1).to_broadcast([P, B, P])
            dve.scalar_tensor_tensor(out=tiles((turn1_a if n == 0 else turn1_b)[:, :]), in0=tiles(q_bank),
                                     scalar=b1x[:, n:n + 1], in1=table, op0=ALU.add, op1=ALU.mult).then_inc(z.turned, 1)

        def dve_query1_parts(dve, c):
            dve.wait_ge(z.turned, per(c, 2, 2))
            dve.tensor_tensor(full1[:, :], turn1_a[:, :], turn1_b[:, :], ALU.add).then_inc(z.full, 1)
            dve.wait_ge(z.full, c + 1)
            if c == 0:
                dve.wait_ge(z.cscr, 16)
            else:
                dve.wait_ge(z.scr, per(c - 1, 16, 16))
            split(dve, [parts1[:, k, :] for k in range(3)], res1[:, :], full1[:, :], z.split, c)

        def act_query1(act, c):
            act.wait_ge(ln.tr, per(z.k0 + c, B, B))
            act.activation(xT[:, :], q_bank, ACT.Copy).then_inc(ln.xT, 1)

        def pe_cross1(pe, c):
            pe.wait_ge(z.stack, per(c, 96, 96))
            if c == 0:
                pe.wait_ge(z.cstk, 16 * 12)
                pe.wait_ge(z.cvs, B)

            def scores(b):
                k0 = 3 * (B * c + b)
                for k, (h0, nh) in enumerate(HEADS_OF):
                    if b:
                        pe.wait_ge(z.masked, k0 + k - 2)
                    for h in range(h0, h0 + nh):
                        m = pe.matmul(ring[k][:, (h - h0) * SC:(h - h0 + 1) * SC], q_stack[0:ROW_MAX, h, b * P:(b + 1) * P],
                                      k1_stack[:, b, h, :], start=True, stop=True)
                    m.then_inc(z.sc, 1)

            def turn_probs(b):
                n0 = 4 * (B * c + b)
                pe.wait_ge(z.ex, B * c + b + 1)
                for g in range(4):
                    n = n0 + g
                    if n >= 2:
                        pe.wait_ge(z.pT, n - 1)
                    for j in range(4):
                        m = pe.transpose(y_bank[n % 2][0:SC, j * P:(j + 1) * P], p1[:, b % 2, 4 * g + j, :], ident[:, :])
                    m.then_inc(z.ptr, 1)

            def weigh(b):
                n0 = 4 * (B * c + b)
                if B * c + b:
                    pe.wait_ge(z.o1, B * c + b)
                for g in range(4):
                    pe.wait_ge(z.pT, n0 + g + 1)
                    for j in range(4):
                        m = pe.matmul(pv_bank[32 * j:32 * j + 32, g * P:(g + 1) * P], v1_aug[:, b, 4 * g + j, :],
                                      p1_T[:, b % 2, 4 * g + j, :], start=True, stop=True)
                m.then_inc(z.pv, 1)

            def back(b):
                n = B * c + b
                pe.wait_ge(z.o1, n + 1)
                if b:
                    pe.wait_ge(z.hd, n)
                for g in range(4):
                    m = pe.transpose(mix[:, g * P:(g + 1) * P], o1_T[:, b % 2, g, :], ident[:, :])
                m.then_inc(z.o1t, 1)

            scores(0)
            for b in range(B):
                if b + 1 < B:
                    scores(b + 1)
                turn_probs(b)
                if b == 3 and c + 1 < NT:
                    pe_query1(pe, c + 1, 1)
                if b:
                    back(b - 1)
                weigh(b)
                if b == 1 and c + 1 < NT:
                    pe_norm(pe, c + 1, z, q_bank)
                if b == 2 and c + 1 < NT:
                    pe_query1(pe, c + 1, 0)
            back(B - 1)
            pe.wait_ge(z.hd, per(c, B, B))
            for b in range(B):
                m = pe.transpose(mix[:, b * P:(b + 1) * P], heads1[:, b, :], ident[:, :])
            m.then_inc(z.hdt, 1)
            pe.wait_ge(z.hT, c + 1)
            for b in range(B):
                pe.matmul(mix[:, b * P:(b + 1) * P], one_row[:, :], bo1x[:, :], start=True, stop=False)
                m = pe.matmul(mix[:, b * P:(b + 1) * P], h1_T[:, b, :], w1x[:, 5, :], start=False, stop=True)
            m.then_inc(z.wo, 1)

        def dve_cross1(dve, c):
            mask = (mask1 if c else mask1c)

            def masked(b):
                n = B * c + b
                if n >= 2:
                    dve.wait_ge(z.sub, n - 1)
                for k, (h0, nh) in enumerate(HEADS_OF):
                    dve.wait_ge(z.sc, 3 * n + k + 1)
                    dve.tensor_tensor(t1[:, b % 2, h0:h0 + nh, :], ring[k][:, 0:nh * SC].rearrange("p (h s) -> p h s", s=SC),
                                      mask[:, b, :].unsqueeze(1).to_broadcast([P, nh, SC]), ALU.add).then_inc(z.masked, 1)
                dve.wait_ge(z.masked, 3 * n + 3)
                dve.tensor_reduce(mx1[:, b % 2, :], t1[:, b % 2, :, :], AX.X, ALU.max).then_inc(z.mx, 1)

            def finish(b):
                n = B * c + b
                dve.wait_ge(z.o1t, n + 1)
                src = mix.rearrange("p (g j d) -> p g j d", g=4, j=4)
                dve.reciprocal(rden1[:, b % 2, :, :], src[:, :, :, DH]).then_inc(z.rd, 1)
                dve.wait_ge(z.rd, n + 1)
                for g in range(4):
                    m = dve.tensor_tensor(heads1[:, b, 32 * g:32 * g + 32].rearrange("p (j d) -> p j d", d=DH), src[:, g, :, 0:DH],
                                          rden1[:, b % 2, g, :].unsqueeze(2).to_broadcast([P, 4, DH]), ALU.mult)
                m.then_inc(z.hd, 1)

            masked(0)
            for b in range(B):
                if b + 1 < B:
                    masked(b + 1)
                if b == 3 and c + 1 < NT:
                    dve_query1(dve, c + 1, 1)
                    dve_query1_parts(dve, c + 1)
                if b:
                    finish(b - 1)
                if b == 0 and c + 1 < NT:
                    dve_norm_stats(dve, c + 1, z, chunk(c + 1))
                if b == 1 and c + 1 < NT:
                    dve_norm_apply(dve, c + 1, z, chunk(c + 1))
                if b == 2 and c + 1 < NT:
                    dve_query1(dve, c + 1, 0)
            finish(B - 1)
            dve.wait_ge(z.wo, c + 1)
            dve.tensor_tensor(x_sb[:, :, c, :], x_sb[:, :, c, :], mix.rearrange("p (b d) -> p b d", b=B), ALU.add).then_inc(z.res, 1)
            dve.wait_ge(z.res, c + 1)

        def act_cross1(act, c):
            def expo(b):
                n = B * c + b
                act.wait_ge(z.sub, n + 1)
                if n >= 2:
                    act.wait_ge(z.ptr, 4 * (n - 1))
                act.activation(p1[:, b % 2, :, :], t2[:, b % 2, :, :], ACT.Exp).then_inc(z.ex, 1)

            expo(0)
            for b in range(B):
                n = B * c + b
                for g in range(4):
                    act.wait_ge(z.ptr, 4 * n + g + 1)
                    if n >= 2:
                        act.wait_ge(z.pv, n - 1)
                    act.activation(p1_T[:, b % 2, 4 * g:4 * g + 4, :], y_bank[(4 * n + g) % 2][0:SC, :].rearrange("p (j q) -> p j q", j=4),
                                   ACT.Copy).then_inc(z.pT, 1)
                if b + 1 < B:
                    expo(b + 1)
                act.wait_ge(z.pv, n + 1)
                if n >= 2:
                    act.wait_ge(z.o1t, n - 1)
                act.activation(o1_T[:, b % 2, :, :], pv_bank[:, :].rearrange("p (g q) -> p g q", g=4), ACT.Copy).then_inc(z.o1, 1)
                if b == 1 and c + 1 < NT:
                    act_query1(act, c + 1)
            act.wait_ge(z.hdt, c + 1)
            act.activation(h1_T[:, :, :], tiles(mix), ACT.Copy).then_inc(z.hT, 1)

        def pool_cross1(pool, c):
            for b in range(B):
                n = B * c + b
                pool.wait_ge(z.mx, n + 1)
                if n >= 2:
                    pool.wait_ge(z.ex, n - 1)
                pool.tensor_tensor(t2[:, b % 2, :, :], t1[:, b % 2, :, :], mx1[:, b % 2, :].unsqueeze(2).to_broadcast([P, H, SC]),
                                   ALU.subtract).then_inc(z.sub, 1)
                if b == 1 and c + 1 < NT:
                    pool_norm(pool, c + 1, z)

        def sp_cross1(sp, c):
            sp.wait_ge(z.split, per(c, 4, 4))
            sp.dma_start(scr_q1.rearrange("k p t -> p k t"), parts1[:, :, :]).then_inc(z.scr, 16)
            sp.wait_ge(z.scr, per(c, 16, 16))
            if c:
                sp.wait_ge(z.sc, per(c, 3 * B, 0))
            flat = scr_q1.rearrange("k (d h) t -> k d (h t)", h=H)
            at = ROW_HI
            for k, times in ((0, 3), (1, 2), (2, 1)):
                for _ in range(times):
                    sp.dma_start(q_stack[at:at + DH, :, :].rearrange("p h t -> p (h t)"), flat[k]).then_inc(z.stack, 16)
                    at += DH

        m1 = signals("ffn1", "init load cast logits sig bias top idx idxf sa sb sel wgt wsplit wtr wT pick rin up relu sq "
                     "sup srelu ssq sdown y y_sb res", k0=2 * B + 3 * NT)
        ffn1_loads = [(gate1_w[:, :], "gate1_w"), (bias1[:, :, :], "bias1"), (up1_f[:, :, :], "up1"), (down1_f[:, 0, :, :], "down1_a"),
                      (down1_f[0:HID - P, 1, :, :], "down1_b"), (sup[:, :], "sup"), (sdown[:, 0, :], "sdown_a"),
                      (sdown[0:HID - P, 1, :], "sdown_b"), (pick1[:, :, :], "pick1"), (places1[:, :], "places1")]
        HR = HID - P
        HP = [P, HR]

        def pe_route1(pe, c, part):
            if part == 0:
                pe_norm(pe, c, m1)
            elif part == 1:
                pe.wait_ge(ln.xT, m1.k0 + c + 1)
                logits = mix[:, 0:B * 16].rearrange("p (b e) -> p b e", e=16)
                for b in range(B):
                    m = pe.matmul(logits[:, b, 0:E1], x1_T[:, c % 2, b * P:(b + 1) * P], gate1_w[:, :], start=True, stop=True)
                m.then_inc(m1.logits, 1)
            else:
                pe.wait_ge(m1.wsplit, per(c, 4, 4))
                for b in range(B):
                    m = pe.transpose(mix_bf[0:3 * E1, b * P:(b + 1) * P], wgt_parts[:, b, :, :].rearrange("p k e -> p (k e)"), ident_bf[:, :])
                m.then_inc(m1.wtr, 1)

        def pe_ffn1(pe, c):
            for k in range(2):
                if c:
                    pe.wait_ge(m1.relu, 2 * E1 * c)
                pe.matmul(ring[k][0:HP[k], :], sup[:, k * P:k * P + HP[k]], x1_T[:, c % 2, :], start=True, stop=True).then_inc(m1.sup, 1)
            if c:
                pe.wait_ge(m1.y_sb, (E1 + 1) * c)
            for k in range(2):
                pe.wait_ge(m1.ssq, per(c, 2, k + 1))
            for b in range(B):
                for k in range(2):
                    m = pe.matmul(y_bank[0][:, b * P:(b + 1) * P], hs_2[0:HP[k], k, b * P:(b + 1) * P], sdown[0:HP[k], k, :],
                                  start=(k == 0), stop=(k == 1))
            m.then_inc(m1.sdown, 1)
            pe.wait_ge(m1.wT, c + 1)

            def pick(e):
                n = E1 * c + e
                if e >= 1:
                    pe.wait_ge(m1.rin, n)
                pe.matmul(pv_bank[:, :], pick1[:, e, :], wgt_T[:, c % 2, :], start=True, stop=True).then_inc(m1.pick, 1)

            def up(e):
                n = E1 * c + e
                pe.wait_ge(m1.rin, n + 1)
                for k in range(2):
                    if e >= 2:
                        pe.wait_ge(m1.relu, 2 * (n - 2) + k + 1)
                    pe.matmul(ring[2 * (e % 2) + k][0:HP[k], :], up1[:, e, k * P:k * P + HP[k]], rin[:, e % 2, :],
                              start=True, stop=True).then_inc(m1.up, 1)

            def down(e):
                n = E1 * c + e
                use = (E1 + 1) * c + e + 1
                for k in range(2):
                    pe.wait_ge(m1.sq, 2 * n + k + 1)
                if use >= 2:
                    pe.wait_ge(m1.y_sb, use - 1)
                for b in range(B):
                    for k in range(2):
                        m = pe.matmul(y_bank[(e + 1) % 2][:, b * P:(b + 1) * P], h2_bf[0:HP[k], e % 2, k, b * P:(b + 1) * P],
                                      down1[0:HP[k], k, e, :], start=(k == 0), stop=(k == 1))
                m.then_inc(m1.y, 1)

            pick(0)
            for e in range(E1):
                up(e)
                if e + 1 < E1:
                    pick(e + 1)
                if e >= 1:
                    down(e - 1)
                if e in (2, 3, 6) and c + 1 < NT:
                    pe_route1(pe, c + 1, (2, 3, 6).index(e))
            down(E1 - 1)

        def dve_route1(dve, c):
            dve.wait_ge(m1.sig, c + 1)
            dve.tensor_tensor(biased1[:, :, :], scores1[:, :, :], bias1[:, :, :], ALU.add).then_inc(m1.bias, 1)
            dve.wait_ge(m1.bias, c + 1)
            for b in range(B):
                dve.max(top1_v[:, b, :], biased1[:, b, :]).then_inc(m1.top, 1)
            for b in range(B):
                dve.wait_ge(m1.top, per(c, B, b + 1))
                dve.max_index(top1_i[:, b, :], top1_v[:, b, :], biased1[:, b, :]).then_inc(m1.idx, 1)
            dve.wait_ge(m1.idx, per(c, B, B))
            dve.tensor_copy(top1_f[:, :, :], top1_i[:, :, :]).then_inc(m1.idxf, 1)
            dve.wait_ge(m1.idxf, c + 1)
            for b in range(B):
                dve.tensor_scalar(sel_a[:, b, :], places1[:, :], top1_f[:, b, 0:1], None, ALU.is_equal).then_inc(m1.sa, 1)
                dve.tensor_scalar(sel_b[:, b, :], places1[:, :], top1_f[:, b, 1:2], None, ALU.is_equal).then_inc(m1.sb, 1)
            dve.wait_ge(m1.sa, per(c, B, B))
            dve.wait_ge(m1.sb, per(c, B, B))
            dve.tensor_tensor(sel_s[:, :, :], sel_a[:, :, :], sel_b[:, :, :], ALU.add).then_inc(m1.sel, 1)
            dve.wait_ge(m1.sel, c + 1)
            dve.tensor_tensor(wgt1[:, :, :], sel_s[:, :, :], scores1[:, :, :], ALU.mult).then_inc(m1.wgt, 1)
            dve.wait_ge(m1.wgt, c + 1)
            split(dve, [wgt_parts[:, :, k, :] for k in range(3)], wgt_r[:, :, :], wgt1[:, :, :], m1.wsplit, c)

        def dve_ffn1(dve, c):
            dve.wait_ge(m1.sdown, c + 1)
            dve.tensor_tensor(x_sb[:, :, c, :], x_sb[:, :, c, :], y_bank[0].rearrange("p (b d) -> p b d", b=B), ALU.add).then_inc(m1.y_sb, 1)
            for e in range(E1):
                n = E1 * c + e
                dve.wait_ge(m1.pick, n + 1)
                if n >= 2:
                    dve.wait_ge(m1.up, 2 * (n - 1))
                dve.tensor_tensor(rin[:, e % 2, :], x1_T[:, c % 2, :], pv_bank[:, :], ALU.mult).then_inc(m1.rin, 1)
                if e:
                    square(dve, n - 1)
                if e >= 2:
                    round_y(dve, c, e - 2)
                if e == 0 and c + 1 < NT:
                    dve_norm_stats(dve, c + 1, m1, chunk(c + 1))
                if e == 1 and c + 1 < NT:
                    dve_norm_apply(dve, c + 1, m1, chunk(c + 1))
                if e == 5 and c + 1 < NT:
                    dve_route1(dve, c + 1)
            square(dve, E1 * c + E1 - 1)
            for e in range(E1 - 2, E1):
                round_y(dve, c, e)

        def round_y(dve, c, e):
            n = E1 * c + e
            dve.wait_ge(m1.y, n + 1)
            if n >= 2:
                dve.wait_ge(m1.res, n - 1)
            dve.tensor_copy(y1[:, n % 2, :, :], y_bank[(e + 1) % 2].rearrange("p (b d) -> p b d", b=B)).then_inc(m1.y_sb, 1)

        def pool_ffn1(pool, c):
            for e in range(E1):
                n = E1 * c + e
                if e == 0 and c + 1 < NT:
                    pool_norm(pool, c + 1, m1)
                pool.wait_ge(m1.y_sb, (E1 + 1) * c + e + 2)
                if n:
                    pool.wait_ge(m1.res, n)
                pool.tensor_tensor(x_sb[:, :, c, :], x_sb[:, :, c, :], y1[:, n % 2, :, :], ALU.add).then_inc(m1.res, 1)

        def square(dve, n):
            for k in range(2):
                dve.wait_ge(m1.relu, 2 * n + k + 1)
                dve.tensor_tensor(h2_bf[0:HP[k], n % 2, k, :], hr_bf[0:HP[k], n % 2, k, :], hr_bf[0:HP[k], n % 2, k, :],
                                  ALU.mult).then_inc(m1.sq, 1)

        def act_route1(act, c, part):
            if part == 0:
                act.wait_ge(ln.tr, per(m1.k0 + c, B, B))
                act.activation(x1_T[:, c % 2, :], mix, ACT.Copy).then_inc(ln.xT, 1)
            elif part == 1:
                logits = mix[:, 0:B * 16].rearrange("p (b e) -> p b e", e=16)
                act.wait_ge(m1.logits, c + 1)
                act.activation(scores1[:, :, :], logits[:, :, 0:E1], ACT.Sigmoid).then_inc(m1.sig, 1)
            else:
                act.wait_ge(m1.wtr, c + 1)
                act.activation(wgt_T[0:3 * E1, c % 2, :], mix_bf[0:3 * E1, 0:T], ACT.Copy).then_inc(m1.wT, 1)

        def act_ffn1(act, c):
            for k in range(2):
                act.wait_ge(m1.sup, per(c, 2, k + 1))
                act.activation(hs_r[0:HP[k], k, :], ring[k][0:HP[k], :], ACT.Relu).then_inc(m1.srelu, 1)
            for k in range(2):
                act.wait_ge(m1.srelu, per(c, 2, k + 1))
                act.activation(hs_2[0:HP[k], k, :], hs_r[0:HP[k], k, :], ACT.Square).then_inc(m1.ssq, 1)
            for e in range(E1):
                n = E1 * c + e
                for k in range(2):
                    act.wait_ge(m1.up, 2 * n + k + 1)
                    if n >= 2:
                        act.wait_ge(m1.sq, 2 * (n - 2) + k + 1)
                    act.activation(hr_bf[0:HP[k], e % 2, k, :], ring[2 * (e % 2) + k][0:HP[k], :], ACT.Relu).then_inc(m1.relu, 1)
                if e in (2, 3, 6) and c + 1 < NT:
                    act_route1(act, c + 1, (2, 3, 6).index(e))

        def split(eng, dst, res, full, done, i):
            eng.tensor_copy(dst[0], full).then_inc(done, 1)
            eng.wait_ge(done, per(i, 4, 1))
            eng.tensor_tensor(res, full, dst[0], ALU.subtract).then_inc(done, 1)
            eng.wait_ge(done, per(i, 4, 2))
            eng.tensor_copy(dst[1], res).then_inc(done, 1)
            eng.wait_ge(done, per(i, 4, 3))
            eng.tensor_tensor(dst[2], res, dst[1], ALU.subtract).then_inc(done, 1)

        def load_stage(eng, sem_, what):
            for dst, name in what:
                eng.dma_start(dst, io[name]).then_inc(sem_, 16)

        attend = ctx.enter_context(ExitStack())
        block = attend.enter_context(nc.Block())

        @block.sync
        def _(sp):
            for dst, src in loads:
                sp.dma_start(dst, src).then_inc(s_load, 16)
            sp.wait_ge(s_load, LOADED)
            for a in (own, cross):
                for i in range(B):
                    sp_attention(sp, i, a)

        @block.tensor
        def _(pe):
            pe.wait_ge(s_load, LOADED)
            pe.wait_ge(s_init, INIT)
            for a in (own, cross):
                for i in range(B):
                    pe_attention(pe, i, a)

        @block.vector
        def _(dve):
            dve.memset(neg_half[:, :], -0.5).then_inc(s_init, 1)
            dve.memset(one_row[:, :], 1.0).then_inc(s_init, 1)
            dve.memset(gn_eps[:, :], GN_EPS).then_inc(s_init, 1)
            dve.wait_ge(s_load, LOADED)
            for a in (own, cross):
                if a is cross:
                    dve.tensor_copy(len_f[:, :], len_i[:, :]).then_inc(s_len, 1)
                    dve.wait_ge(s_len, 1)
                    dve.tensor_scalar(keep[:, :], len_f[:, :], pos_col[:, 0:1], None, ALU.is_gt).then_inc(s_len, 1)
                    dve.tensor_reduce(len_max[:, :], len_f[:, :], AX.X, ALU.max).then_inc(s_len, 1)
                    dve.wait_ge(s_len, 3)
                    dve.tensor_scalar(mask_row[:, :], pos_row[:, :], len_max[0:1, 0:1], NEG, ALU.is_ge, ALU.mult).then_inc(s_mask, 1)
                for i in range(B):
                    dve_attention(dve, i, a)

        @block.scalar
        def _(act):
            act.wait_ge(s_load, LOADED)
            act.wait_ge(s_init, INIT)
            for a in (own, cross):
                for i in range(B):
                    act_attention(act, i, a)

        @block.gpsimd
        def _(pool):
            pool.memset(v_aug[:, :, :, :], 0.0).then_inc(s_init, 1)
            pool.wait_ge(s_init, 4)
            pool.memset(v_aug[:, :, :, DH:DH + 1], 1.0).then_inc(s_init, 1)
            pool.wait_ge(s_load, LOADED)
            pool.wait_ge(s_init, INIT)
            for a in (own, cross):
                if a is cross:
                    pool.wait_ge(s_len, 3)
                for i in range(B):
                    pool_attention(pool, i, a)

        attend.close()
        with nc.Block() as reset:
            @reset.gpsimd
            def _(pool):
                for s in in_block_1:
                    pool.sem_clear(s)

        block = ctx.enter_context(nc.Block())

        @block.sync
        def _(sp):
            load_stage(sp, f.load, ffn0_loads)
            sp.wait_ge(f.acc, NT * E0 * B)
            load_stage(sp, r.load, rec_loads)
            sp_rec(sp, 0)
            for c in range(NT):
                if c:
                    sp_out1(sp, c - 1)
                if c + 1 < NT:
                    sp_rec(sp, c + 1)
            sp_out1(sp, NT - 1)
            sp.wait_ge(r.res, NT)
            load_stage(sp, z.load, cross1_loads)
            sp.dma_start(ctx1[:, :, :], io["ctx"].rearrange("b s d -> s b d")).then_inc(z.load, 16)
            sp.dma_start(pad_i[:, :, :].rearrange("p b s -> p (b s)"), io["pad"].partition_broadcast(P)).then_inc(z.load, 16)
            sp_ctx1(sp)
            for c in range(NT):
                sp_cross1(sp, c)
            sp.wait_ge(z.res, NT)
            load_stage(sp, m1.load, ffn1_loads)
            sp.wait_ge(m1.res, NT * E1)
            for b in range(B):
                sp.dma_start(out[b].rearrange("(c p) d -> p c d", p=P), x_sb[:, b, :, :]).then_inc(s_out, 16)
            sp.wait_ge(s_out, 16 * B)

        @block.tensor
        def _(pe):
            pe.wait_ge(f.load, 16 * len(ffn0_loads))
            for c in range(NT):
                pe_ffn0(pe, c)
            pe.wait_ge(r.load, 16 * len(rec_loads))
            pe_rec(pe, 0)
            for c in range(NT):
                if c + 1 < NT:
                    pe_rec(pe, c + 1)
                if c:
                    pe_out1(pe, c - 1)
            pe_out1(pe, NT - 1)
            pe.wait_ge(z.load, 16 * (len(cross1_loads) + 2))
            pe_ctx1(pe)
            pe_norm(pe, 0, z, q_bank)
            pe_query1(pe, 0, 0)
            pe_query1(pe, 0, 1)
            for c in range(NT):
                pe_cross1(pe, c)
            pe.wait_ge(m1.load, 16 * len(ffn1_loads))
            pe.wait_ge(m1.init, 1)
            pe.wait_ge(m1.cast, 3)
            for part in range(3):
                pe_route1(pe, 0, part)
            for c in range(NT):
                pe_ffn1(pe, c)

        @block.vector
        def _(dve):
            dve.wait_ge(f.load, 16 * len(ffn0_loads))
            for c in range(NT):
                dve_ffn0(dve, c)
            dve.memset(xs[:, 0, :, 0:1], 0.0).then_inc(r.init, 1)
            dve.memset(state0[:, :, :], 0.0).then_inc(r.init, 1)
            dve.wait_ge(r.load, 16 * len(rec_loads))
            dve.wait_ge(r.init, 2)
            dve_norm(dve, 0, r, chunk(0))
            dve_rec_mix(dve, 0, range(7))
            dve_rec_norms(dve, 0)
            dve_rec_units(dve, 0)
            dve_dots(dve, 0)
            for c in range(NT):
                before, after = c > 0, c + 1 < NT
                dve_steps(dve, c, 0, 6)
                if after:
                    dve_norm_stats(dve, c + 1, r, chunk(c + 1))
                dve_steps(dve, c, 6, 16)
                if after:
                    dve_norm_apply(dve, c + 1, r, chunk(c + 1))
                dve_steps(dve, c, 16, 28)
                if after:
                    dve_rec_mix(dve, c + 1, range(4))
                dve_steps(dve, c, 28, 34)
                if after:
                    dve_rec_mix(dve, c + 1, range(4, 7))
                dve_steps(dve, c, 34, 42)
                if after:
                    dve_rec_norms(dve, c + 1)
                dve_steps(dve, c, 42, 50)
                if after:
                    dve_rec_units(dve, c + 1)
                dve_steps(dve, c, 50, 60)
                if before:
                    dve_out1_center(dve, c - 1)
                dve_steps(dve, c, 60, 76)
                if before:
                    dve_out1_norm(dve, c - 1)
                dve_steps(dve, c, 76, 92)
                if before:
                    dve_out1_residual(dve, c - 1)
                dve_steps(dve, c, 92, P)
            dve_outputs(dve, NT * NB - 1)
            dve_out1_center(dve, NT - 1)
            dve_out1_norm(dve, NT - 1)
            dve_out1_residual(dve, NT - 1)
            dve.memset(k1_stack[0:1, :, :, :], 0.0).then_inc(z.init, 1)
            dve.memset(v1_aug[:, :, :, :], 0.0).then_inc(z.init, 1)
            dve.wait_ge(z.init, 2)
            dve.memset(v1_aug[:, :, :, DH:DH + 1], 1.0).then_inc(z.init, 1)
            dve.wait_ge(z.load, 16 * (len(cross1_loads) + 2))
            dve_ctx1(dve)
            dve_norm(dve, 0, z, chunk(0))
            dve_query1(dve, 0, 0)
            dve_query1(dve, 0, 1)
            dve_query1_parts(dve, 0)
            for c in range(NT):
                dve_cross1(dve, c)
            dve.memset(wgt_T[:, :, :], 0.0).then_inc(m1.init, 1)
            dve.wait_ge(m1.load, 16 * len(ffn1_loads))
            dve.tensor_copy(up1[:, :, :], up1_f[:, :, :]).then_inc(m1.cast, 1)
            dve.tensor_copy(down1[:, 0, :, :], down1_f[:, 0, :, :]).then_inc(m1.cast, 1)
            dve.tensor_copy(down1[0:HR, 1, :, :], down1_f[0:HR, 1, :, :]).then_inc(m1.cast, 1)
            dve_norm(dve, 0, m1, chunk(0))
            dve_route1(dve, 0)
            for c in range(NT):
                dve_ffn1(dve, c)

        @block.scalar
        def _(act):
            for c in range(NT):
                act_ffn0(act, c)
            act_rec(act, 0)
            for c in range(NT):
                if c + 1 < NT:
                    act_rec(act, c + 1)
                if c:
                    act_out1(act, c - 1)
            act_out1(act, NT - 1)
            act_ctx1(act)
            act_query1(act, 0)
            for c in range(NT):
                act_cross1(act, c)
            act.wait_ge(m1.init, 1)
            for part in range(3):
                act_route1(act, 0, part)
            for c in range(NT):
                act_ffn1(act, c)

        @block.gpsimd
        def _(pool):
            for c in range(NT):
                pool_norm(pool, c, f)
            pool.wait_ge(r.init, 2)
            pool_norm(pool, 0, r)
            pool_rec_before(pool, 0)
            pool_pairs_a(pool, 0)
            pool_pairs_b(pool, 0)
            for blk in range(NT * NB):
                c, k = blk // NB, blk % NB
                ahead = blk + 1 < NT * NB
                if ahead:
                    pool_pairs_a(pool, blk + 1)
                if k == 0 and c + 1 < NT:
                    pool_norm(pool, c + 1, r)
                if blk:
                    pool_products(pool, blk - 1)
                if ahead:
                    pool_pairs_b(pool, blk + 1)
                if blk:
                    pool_outputs(pool, blk - 1)
                if k == 0 and c + 1 < NT:
                    pool_rec_before(pool, c + 1)
            pool_products(pool, NT * NB - 1)
            pool_outputs(pool, NT * NB - 1)
            pool_norm(pool, 0, z)
            for c in range(NT):
                pool_cross1(pool, c)
            pool_norm(pool, 0, m1)
            for c in range(NT):
                pool_ffn1(pool, c)


HD = np.arange(H * DH).reshape(H, DH)
DH_ORDER = HD.T.reshape(-1)


def _rope_tables(positions, turned_sign, freqs, scale):
    ang = positions[None, :].astype(np.float32) * freqs[:, None].astype(np.float32)
    cos = np.cos(ang) * np.float32(scale)
    sin = np.sin(ang) * turned_sign[:, None] * np.float32(scale)
    return (np.repeat(cos, H, axis=0).astype(np.float32), np.repeat(sin, H, axis=0).astype(np.float32))


def _columns(w, order):
    return np.ascontiguousarray(np.asarray(w).T[:, order])


def _layout(inp):
    bf = mybir.dt.np(BF16)
    a = {k: np.asarray(v) for k, v in inp.items()}
    pair = np.arange(DH) ^ 1
    turn0 = HD[:, pair].T.reshape(-1)
    io = {}
    io["x"] = a["x"]
    io["ident"] = np.eye(P, dtype=np.float32)
    io["ident_bf"] = np.eye(P, dtype=bf)
    later = np.triu(np.ones((P, P), np.float32), 1) * np.float32(NEG)
    io["mask_qk"] = later.astype(bf)
    io["mask_kq"] = np.ascontiguousarray(later.T).astype(bf)
    f0 = np.exp(-np.log(np.float32(10000.0)) * np.arange(0, DH, 2, dtype=np.float32) / np.float32(DH)).astype(np.float32)
    sign0 = np.where(np.arange(DH) % 2 == 0, -1.0, 1.0).astype(np.float32)
    pos = np.arange(T, dtype=np.float32)
    cq, sq = _rope_tables(pos, sign0, np.repeat(f0, 2), DH ** -0.5)
    ck, sk = _rope_tables(pos, sign0, np.repeat(f0, 2), 1.0)
    io["rope0"] = np.ascontiguousarray(np.stack([cq, sq, ck, sk], axis=1))
    wq, wk, wv = np.split(a["L0_attn_Wqkv"], 3, axis=0)
    plain = np.arange(D)
    io["w0"] = np.ascontiguousarray(np.stack([_columns(wq, DH_ORDER), _columns(wq, turn0), _columns(wk, DH_ORDER),
                                              _columns(wk, turn0), _columns(wv, plain), _columns(a["L0_attn_Wo"], plain)], axis=1))
    io["w0x"] = np.ascontiguousarray(np.stack([_columns(a["L0_xattn_wq"], DH_ORDER), _columns(a["L0_xattn_wk"], DH_ORDER),
                                               _columns(a["L0_xattn_wv"], plain), _columns(a["L0_xattn_wo"], plain)], axis=1))
    io["bo0x"] = a["L0_xattn_bo"][None]
    io["ones_row"] = np.ones((1, H * KW), bf)
    io["zero_row"] = np.zeros((1, H * KW), bf)
    io["ones_rows"] = np.ones((3, H * KW), bf)
    io["ctx"] = a["ctx_1024"]
    io["ctx_dh"] = np.ascontiguousarray(a["ctx_1024"][:, :, DH_ORDER])
    io["lens"] = a["_lenS2"].astype(np.int32)
    io["pos_col"] = np.arange(P, dtype=np.float32)[:, None]
    io["pos_row"] = np.tile(np.arange(SC, dtype=np.float32), H)[None]
    io["up0"] = np.ascontiguousarray(a["L0_ffn_w1"].transpose(1, 0, 2))
    io["down0"] = np.ascontiguousarray(a["L0_ffn_w2"].reshape(E0, F0 // P, P, D).transpose(2, 0, 1, 3))
    io["router_w"], io["router_b"] = a["L0_ffn_router_w"], a["L0_ffn_router_b"][None]

    def picks(rows, experts):
        out = np.zeros((64, experts, P), bf)
        for e in range(experts):
            out[[e, rows + e, 2 * rows + e], e, :] = 1
        return out

    io["pick1"] = picks(E1, E1)
    io["places"] = np.tile(np.arange(E0 + 1, dtype=np.float32), (P, 1))
    io["places1"] = np.tile(np.arange(E1, dtype=np.float32), (P, 1))
    names = ["r", "w", "k", "v", "a", "b", "g"]
    io["w1a"] = np.ascontiguousarray(np.stack([a[f"L1_attn_W_{n}"].T for n in names + ["o"]], axis=1))
    io["mix1"] = np.ascontiguousarray(np.stack([a[f"L1_attn_x_{n}"] for n in names], axis=1))
    io["bo1a"] = a["L1_attn_b_o"][None]
    io["gn_w"], io["gn_b"] = a["L1_attn_gn_w"][:, None], a["L1_attn_gn_b"][:, None]
    same = np.kron(np.eye(H), np.ones((DH, DH))).astype(np.float32)
    io["blk_ones"], io["blk_mean"] = same, (same / DH).astype(np.float32)
    turn1 = HD[:, (np.arange(DH) + DH // 2) % DH].T.reshape(-1)
    sign1 = np.where(np.arange(DH) < DH // 2, -1.0, 1.0).astype(np.float32)
    f1 = (1.0 / 10000.0 ** (np.arange(0, DH, 2, dtype=np.float32) / np.float32(DH))).astype(np.float32)
    cq, sq = _rope_tables(pos, sign1, np.tile(f1, 2), DH ** -0.5)
    ck, sk = _rope_tables(pos, sign1, np.tile(f1, 2), 1.0)
    io["rope1"] = np.ascontiguousarray(np.stack([cq, sq, ck, sk], axis=1))
    wq, wk = a["L1_xattn_wq"], a["L1_xattn_wk"]
    io["w1x"] = np.ascontiguousarray(np.stack([_columns(wq, DH_ORDER), _columns(wq, turn1), _columns(wk, DH_ORDER),
                                               _columns(wk, turn1), a["L1_xattn_wv"].T, a["L1_xattn_wo"].T], axis=1))
    bq, bk = a["L1_xattn_bq"], a["L1_xattn_bk"]
    io["b1x"] = np.ascontiguousarray(np.stack([bq[DH_ORDER], bq[turn1], bk[DH_ORDER], bk[turn1]], axis=1))
    io["bv1x"], io["bo1x"] = a["L1_xattn_bv"][None], a["L1_xattn_bo"][None]
    io["causal1"] = np.where(np.arange(SC)[None, :] > np.arange(P)[:, None], -1e9, 0.0).astype(np.float32)
    io["pad"] = a["mask_BxS2_bk1"].astype(np.int32).reshape(-1)
    io["gate1_w"] = np.ascontiguousarray(a["L1_ffn_gate_w"].T)
    io["bias1"] = np.ascontiguousarray(np.broadcast_to(a["L1_ffn_expert_bias"], (P, NT, E1)))
    io["up1"] = np.ascontiguousarray(a["L1_ffn_w_up"].transpose(2, 0, 1))
    down = a["L1_ffn_w_down"].transpose(2, 0, 1)
    io["down1_a"], io["down1_b"] = np.ascontiguousarray(down[0:P]), np.ascontiguousarray(down[P:])
    io["sup"] = np.ascontiguousarray(a["L1_ffn_shared_w_up"].T)
    sd = a["L1_ffn_shared_w_down"].T
    io["sdown_a"], io["sdown_b"] = np.ascontiguousarray(sd[0:P]), np.ascontiguousarray(sd[P:])
    return io


def kernel(**inputs):
    import concourse.bacc as _bacc
    from concourse.bass_utils import run_bass_kernel_spmd as _run

    io = _layout(inputs)
    nc = _bacc.Bacc("TRN2", target_bir_lowering=False, num_devices=1)
    arrays, aps = {}, {}
    for name, arr in io.items():
        arrays[f"in_{name}"] = arr
        aps[name] = nc.dram_tensor(f"in_{name}", arr.shape, mybir.dt.from_np(arr.dtype), kind="ExternalInput").ap()
    out = nc.dram_tensor("out_x", [B, T, D], F32, kind="ExternalOutput").ap()
    decoder(nc, aps, out)
    r = _run(nc, [arrays], core_ids=[0])
    return r.results[0]["out_x"]
```

```python
from collections import namedtuple
from contextlib import ExitStack

import numpy as np

import concourse.bass as bass
from concourse import mybir

F32 = mybir.dt.float32
BF16 = mybir.dt.bfloat16
I32 = mybir.dt.int32
U32 = mybir.dt.uint32
U8 = mybir.dt.uint8
ALU = mybir.AluOpType
ACT = mybir.ActivationFunctionType
AX = mybir.AxisListType

P = 128
B, T, D = 4, 512, 128
H, DH = 16, 8
NT = T // P
SC = 77
KW = 592
LN_EPS = 1e-5
NEG = -1e30
NORM_EPS, GN_EPS = 1e-6, 0.00064
E0, F0 = 8, 512
E1, HID = 8, 176
ROW_MASK, ROW_HI, ROW_MAX, ROWS = 0, 1, 49, 52
HB, PB = 32, 16
NB = P // HB


def per(i, count, n):
    return i * count + n


def decoder(nc, io, out):
    with ExitStack() as ctx:
        def sb(name, shape, dt=F32):
            return ctx.enter_context(nc.sbuf_tensor(name, shape, dt))

        def group(stack):
            return lambda name, shape, dt=F32: stack.enter_context(nc.sbuf_tensor(name, shape, dt))

        cleared = []

        def signals(name, names, **facts):
            made = [cleared.pop() if cleared else sem(f"{name}_{n}") for n in names.split()]
            return namedtuple(name, names.split() + list(facts))(*made, **facts)

        def bank(name, shape, dt=F32):
            return ctx.enter_context(nc.psum_tensor(name, shape, dt))

        def sem(name):
            return ctx.enter_context(nc.semaphore(name))

        smax_bank = [bank(f"smax_bank{n}", [P, 512]) for n in range(2)]
        st_bank = [bank(f"st_bank{n}", [P, 2, 512]) for n in range(2)]
        pv_bank = bank("pv_bank", [P, 512])
        mix_bank = bank("mix_bank", [P, 512])
        mix_bf = mix_bank[:, :].bitcast(BF16)

        x_sb = sb("x_sb", [P, B, NT, D])
        ident = sb("ident", [P, P])
        ident_bf = sb("ident_bf", [P, P], BF16)
        mask_qk = sb("mask_qk", [P, P], BF16)
        mask_kq = sb("mask_kq", [P, P], BF16)
        neg_half = sb("neg_half", [P, NT])
        one_row = sb("one_row", [1, P])
        gn_eps = sb("gn_eps", [P, 1])

        stats = sb("stats", [P, NT, 6])
        meanvar = sb("meanvar", [P, NT, 2])
        sdev = sb("sdev", [P, NT])
        rstd = sb("rstd", [P, NT])
        xn = sb("xn", [P, NT, D])
        xT = sb("xT", [P, T])
        q_stack = sb("q_stack", [ROWS, H, T], BF16)
        blk_ones = sb("blk_ones", [P, P])
        blk_mean = sb("blk_mean", [P, P])

        layer0 = ExitStack()
        sa = group(layer0)
        bo0x = sa("bo0x", [1, D])
        w0x = sa("w0x", [P, 4, D])
        w0 = sa("w0", [P, 6, D])
        rope0 = sa("rope0", [P, 4, T])
        turn_a = sa("turn_a", [P, 2, T])
        turn_b = sa("turn_b", [P, 2, T])
        qk_f = sa("qk_f", [P, 2, T])
        qk_r = sa("qk_r", [P, 2, T])
        parts = sa("parts", [P, 2, 3, T], BF16)
        q_stacks = [q_stack, sa("q_stack_b", [ROWS, H, T], BF16)]
        k_stacks = [sa(f"k_stack_{n}", [ROWS, H, KW], BF16) for n in range(2)]
        v_augs = [sa(f"v_aug_{n}", [P, NT + 1, H, 32]) for n in range(2)]
        mx = sa("mx", [P, 2, NT, 4])
        mxc = sa("mxc", [P, 2, NT, 4])
        mx_f = sa("mx_f", [P, 2, 2, NT, 4])
        mx_parts = sa("mx_parts", [P, 2, NT, 3, 4], BF16)
        mx_rows = sa("mx_rows", [12, 2, T], BF16)
        NPR = 4
        probs = sa("probs", [P, NPR, 2, 512])
        heads_T = sa("heads_T", [P, 2, T])
        rden = sa("rden", [P, 2, NT, 4])
        heads = sa("heads", [P, NT, D])
        hT = sa("hT", [P, T])

        ctx_hd = sa("ctx_hd", [SC, B, D])
        ctx_dh = sa("ctx_dh", [SC, B, D])
        len_i = sa("len_i", [P, B], I32)
        len_f = sa("len_f", [P, B])
        len_max = sa("len_max", [P, 1])
        pos_col = sa("pos_col", [P, 1])
        keep = sa("keep", [P, B])
        pos_row = sa("pos_row", [1, H * SC])
        mask_row = sa("mask_row", [1, H * SC], BF16)
        cparts = sa("cparts", [P, 3, SC], BF16)
        cres = sa("cres", [P, SC])
        ctxT = sa("ctxT", [P, SC])

        ctx_now = sa("ctx_now", [SC, 2, D])
        layer0.close()

        ffn0 = ExitStack()
        sf = group(ffn0)
        up0 = sf("up0", [P, E0, F0])
        down0 = sf("down0", [P, E0, F0 // P, D])
        router_w = sf("router_w", [P, E0 + 1])
        router_b = sf("router_b", [1, E0 + 1])
        places = sf("places", [P, E0 + 1])
        lmax = sf("lmax", [P, NT])
        shifted = sf("shifted", [P, NT, E0 + 1])
        expd = sf("expd", [P, NT, E0 + 1])
        esum = sf("esum", [P, NT])
        erec = sf("erec", [P, NT])
        gprobs = sf("gprobs", [P, NT, E0 + 1])
        top_v = sf("top_v", [P, NT, 8])
        top_i = sf("top_i", [P, NT, 8], U32)
        top_f = sf("top_f", [P, NT, 8])
        gate_a = sf("gate_a", [P, NT, E0 + 1])
        gate_b = sf("gate_b", [P, NT, E0 + 1])
        gates = sf("gates", [P, 2, NT, E0 + 1])
        x0_T = sf("x0_T", [P, 2, T])
        xn0 = sf("xn0", [P, 2, NT, D])
        hidden = sf("hidden", [P, 2, F0 // P, T])
        ffn0.close()

        rec = ExitStack()
        sr = group(rec)
        xs = sr("xs", [P, 2, B, P + 1])
        xx = sr("xx", [P, B, P])
        xi = sr("xi", [P, 3, T])
        dense = sr("dense", [P, 6, T])
        sq = sr("sq", [P, 2, T])
        nrm = sr("nrm", [P, 2, T])
        inv = sr("inv", [P, 2, T])
        seqs = sr("seqs", [P, 2, 5, DH, P])
        seq_v = sr("seq_v", [P, 2, DH // 2, P])
        by_state = sr("by_state", [P, 2, 3, DH, PB])
        dot_prod = sr("dot_prod", [P, 2, 4, DH, PB])
        dots = sr("dots", [P, 2, 4, PB])
        kb_w = sr("kb_w", [P, 2, 2, DH, PB])
        kb_dot = sr("kb_dot", [P, 2, 2, DH, PB])
        rows_kb = sr("rows_kb", [P, 2, 3, DH, PB])
        vk = sr("vk", [P, 2, PB, DH // 2, DH])
        state0 = sr("state0", [P, DH // 2, DH])
        hist = sr("hist", [P, 2, PB, DH // 2, DH])
        terms = sr("terms", [P, 2, PB, 6, DH // 2, DH])
        sums = sr("sums", [P, 2, PB, 2, DH // 2])
        first_r = sr("first_r", [P, 2, DH, PB])
        o_prod = sr("o_prod", [P, 2, PB, 2, DH // 2, DH])
        o_more = sr("o_more", [P, 2, 3, DH // 2, PB])
        o_seq = sr("o_seq", [P, 2, DH // 2, P])
        o_T = sr("o_T", [P, B, P])
        o_cen = sr("o_cen", [P, T])
        o_sq = sr("o_sq", [P, T])
        o_sd = sr("o_sd", [P, T])
        o_inv = sr("o_inv", [P, T])
        o_n = sr("o_n", [P, T])
        gate_T = sr("gate_T", [P, NT, T])
        w1a = sr("w1a", [P, 8, D])
        mix1 = sr("mix1", [P, 7])
        bo1a = sr("bo1a", [1, D])
        gn_w = sr("gn_w", [P, 1])
        gn_b = sr("gn_b", [P, 1])
        rec.close()

        cross1 = ExitStack()
        sx = group(cross1)
        w1x = sx("w1x", [P, 6, D])
        b1x = sx("b1x", [P, 4])
        bv1x = sx("bv1x", [1, D])
        bo1x = sx("bo1x", [1, D])
        rope1 = sx("rope1", [P, 4, T])
        ctx1 = sx("ctx1", [SC, B, D])
        ctx1_T = sx("ctx1_T", [P, B, SC])
        pad_i = sx("pad_i", [P, B, SC], I32)
        pad_f = sx("pad_f", [P, B, SC])
        causal1 = sx("causal1", [P, SC])
        mask1 = sx("mask1", [P, B, SC])
        mask1c = sx("mask1c", [P, B, SC])
        turn1_a = sx("turn1_a", [P, T])
        turn1_b = sx("turn1_b", [P, T])
        full1 = sx("full1", [P, T])
        res1 = sx("res1", [P, T])
        parts1 = sx("parts1", [P, 3, T], BF16)
        k1_stack = sx("k1_stack", [ROW_MAX, B, H, SC], BF16)
        v1_aug = sx("v1_aug", [SC, B, H, 32])
        t1 = sx("t1", [P, 2, H, SC])
        mx1 = sx("mx1", [P, 2, H])
        t2 = sx("t2", [P, 2, H, SC])
        p1 = sx("p1", [P, 2, H, SC])
        p1_T = sx("p1_T", [SC, 2, H, P])
        o1_T = sx("o1_T", [P, 2, 4, P])
        rden1 = sx("rden1", [P, 2, 4, 4])
        heads1 = sx("heads1", [P, B, D])
        h1_T = sx("h1_T", [P, B, P])

        ffn1 = ExitStack()
        sm = group(ffn1)
        gate1_w = sm("gate1_w", [P, E1])
        bias1 = sm("bias1", [P, NT, E1])
        up1_f = sm("up1_f", [P, E1, HID])
        down1_f = sm("down1_f", [P, 2, E1, D])
        up1 = sm("up1", [P, E1, HID], BF16)
        down1 = sm("down1", [P, 2, E1, D], BF16)
        sup = sm("sup", [P, HID])
        sdown = sm("sdown", [P, 2, D])
        pick1 = sm("pick1", [64, E1, P], BF16)
        places1 = sm("places1", [P, E1])
        scores1 = sm("scores1", [P, NT, E1])
        biased1 = sm("biased1", [P, NT, E1])
        top1_v = sm("top1_v", [P, NT, 8])
        top1_i = sm("top1_i", [P, NT, 8], U32)
        top1_f = sm("top1_f", [P, NT, 8])
        sel_a = sm("sel_a", [P, NT, E1])
        sel_b = sm("sel_b", [P, NT, E1])
        sel_s = sm("sel_s", [P, NT, E1])
        wgt1 = sm("wgt1", [P, NT, E1])
        wgt_r = sm("wgt_r", [P, NT, E1])
        wgt_parts = sm("wgt_parts", [P, NT, 3, E1], BF16)
        wgt_T = sm("wgt_T", [64, 2, T], BF16)
        x1_T = sm("x1_T", [P, 2, T])
        rin = sm("rin", [P, 2, T], BF16)
        hr_bf = sm("hr_bf", [P, 2, 2, T], BF16)
        h2_bf = sm("h2_bf", [P, 2, 2, T], BF16)
        hs_r = sm("hs_r", [P, 2, T])
        hs_2 = sm("hs_2", [P, 2, T])
        y1 = sm("y1", [P, 2, B, D], BF16)
        ffn1.close()
        cross1.close()

        scr_qk = nc.dram_tensor("scr_qk", [2, 3, P, T], BF16, kind="Internal").ap()
        scr_mx = nc.dram_tensor("scr_mx", [2, 12, T], BF16, kind="Internal").ap()
        scr_c = nc.dram_tensor("scr_c", [3, P, SC], BF16, kind="Internal").ap()

        s_load = sem("s_load")
        s_first = sem("s_first")
        s_init = sem("s_init")
        s_out = sem("s_out")
        ln = signals("ln", "stats mv sd rs xn tr xT")

        first_loads = [
            (x_sb[:, 0, :, :], io["x"][0].rearrange("(c p) d -> p c d", p=P)), (ident[:, :], io["ident"]),
            (w0[:, :, :], io["w0"]), (rope0[:, :, :], io["rope0"]),
        ]
        loads = [
            (x_sb[:, 1, :, :], io["x"][1].rearrange("(c p) d -> p c d", p=P)),
            (x_sb[:, 2, :, :], io["x"][2].rearrange("(c p) d -> p c d", p=P)),
            (x_sb[:, 3, :, :], io["x"][3].rearrange("(c p) d -> p c d", p=P)),
            (ident_bf[:, :], io["ident_bf"]),
            (mask_qk[:, :], io["mask_qk"]), (mask_kq[:, :], io["mask_kq"]),
            (w0x[:, :, :], io["w0x"]), (bo0x[:, :], io["bo0x"]),
            (ctx_hd[:, :, :], io["ctx"].rearrange("b s d -> s b d")),
            (ctx_dh[:, :, :], io["ctx_dh"].rearrange("b s d -> s b d")),
            (len_i[:, :], io["lens"].partition_broadcast(P)),
            (blk_ones[:, :], io["blk_ones"]), (blk_mean[:, :], io["blk_mean"]),
            (pos_col[:, :], io["pos_col"]), (pos_row[:, :], io["pos_row"]),
        ]
        for n in range(2):
            loads += [
                (q_stacks[n][0:1, :, :].rearrange("p h t -> p (h t)"), io["ones_row"][:, 0:H * T]),
                (k_stacks[n][0:1, :, :].rearrange("p h t -> p (h t)"), io["zero_row"]),
                (k_stacks[n][ROW_MAX:ROWS, :, :].rearrange("p h t -> p (h t)"), io["ones_rows"]),
            ]
        FIRST_LOADED, LOADED = 16 * len(first_loads), 16 * len(loads)
        INIT = 7

        ATTENTION = ("proj turned qk_sum v_in scr_q scr_k stack smax mx_done mx_comb mx_split mx_tr mx_row mx_scr mx_in st ex pv heads_T "
                     "heads_Tt rden heads heads_tr hT wo res q_parts k_parts mx_chain")

        def uses_of_mix():
            order = [("mx", 0)]
            for g in range(4):
                if g < 3:
                    order.append(("mx", g + 1))
                order.append(("heads", g))
            return order + [("hT", 0), ("wo", 0)]

        NS_TURN = {True: 5, False: 6}

        def attention(name, causal, weights, k0, more=""):
            names = ATTENTION + more
            tiles = [(kt * P, P, kt * P if causal else 0) for kt in range(NT)]
            if not causal:
                tiles.append((T, SC, 0))
            a = signals(name, names, causal=causal, w=weights, k0=k0, tiles=tiles,
                        units=[(qt, j) for qt in range(NT) for j in range(4 if causal else 5)],
                        steps=[(kt, pair) for kt in range(len(tiles)) for pair in range(2)],
                        turned_n=4 if causal else 2, stack_n=16 * (6 if causal else 9), v_n=1 if causal else 2, chain_n=4, turn_at=NS_TURN[causal],
                        mix_order=uses_of_mix())
            in_block_1.extend(a[:len(names.split())])
            return a

        def mix_waits(a, eng, i, use):
            order = a.mix_order
            k = order.index(use)
            if k == 0:
                if i:
                    eng.wait_ge(a.res, i)
                elif a is cross:
                    eng.wait_ge(own.res, B)
            else:
                kind, g = order[k - 1]
                if kind == "mx":
                    eng.wait_ge(a.mx_row, per(i, 4, g + 1))
                elif kind == "heads":
                    eng.wait_ge(a.heads, per(i, 4, g + 1))
                elif kind == "hT":
                    eng.wait_ge(a.hT, per(i, 1, 1))

        def pe_prepare(pe, i, a, part):
            n_proj = 5 if a.causal else 3
            if part == 0:
                for c in range(NT):
                    pe.wait_ge(ln.xn, per(a.k0 + i, NT, c + 1))
                    pe.transpose(smax_bank[0][:, c * P:(c + 1) * P], xn[:, c, :], ident[:, :]).then_inc(ln.tr, 1)
            elif part == 1:
                pe.wait_ge(ln.xT, per(a.k0 + i, 1, 1))
                for n in range(2):
                    pe.matmul(smax_bank[n][:, :], a.w[:, n, :], xT[:, :], start=True, stop=True).then_inc(a.proj, 1)
            elif part == 2:
                if a.causal:
                    for n in range(2):
                        pe.wait_ge(a.turned, per(i, a.turned_n, n + 1))
                        pe.matmul(smax_bank[n][:, :], a.w[:, 2 + n, :], xT[:, :], start=True, stop=True).then_inc(a.proj, 1)
                else:
                    pe.wait_ge(a.turned, per(i, a.turned_n, 2))
                    pe.wait_ge(a.ctx_copy, per(i, 2, 2))
                    pe.transpose(smax_bank[1][:, 0:SC], ctx_now[:, 1, :], ident[0:SC, 0:SC]).then_inc(a.ctx_tr, 1)
            else:
                pe.wait_ge(a.turned, per(i, a.turned_n, 3 if a.causal else 1))
                for c in range(NT):
                    m = pe.matmul(smax_bank[0][:, c * P:(c + 1) * P], xT[:, c * P:(c + 1) * P], a.w[:, n_proj - 1, :],
                                  start=True, stop=True)
                m.then_inc(a.proj, 1)

        def pe_attention(pe, i, a):
            NU, NS = len(a.units), len(a.steps)
            n_proj = 5 if a.causal else 3
            q_stack, k_stack, v_aug = q_stacks[i % 2], k_stacks[i % 2], v_augs[i % 2]

            def scores_for_max(g, u):
                n = g * NU + u
                qt, j = a.units[u]
                if n == 0:
                    pe.wait_ge(a.stack, per(i, a.stack_n, a.stack_n))
                    pe.wait_ge(a.v_in, per(i, a.v_n, a.v_n))
                if n >= 2:
                    pe.wait_ge(a.mx_done, per(i, 4 * NU, n - 1))
                elif a.causal:
                    pe.wait_ge(a.turned, per(i, a.turned_n, a.turned_n))
                else:
                    pe.wait_ge(a.ctx_f, i + 1)
                dst = smax_bank[n % 2]
                if j < 4:
                    h = 4 * g + j
                    w = (qt + 1) * P if a.causal else T
                    m = pe.matmul(dst[:, 0:w], q_stack[0:ROW_MAX, h, qt * P:(qt + 1) * P], k_stack[0:ROW_MAX, h, 0:w],
                                  start=True, stop=not a.causal)
                    if a.causal:
                        m = pe.matmul(dst[:, qt * P:w], ident_bf[:, :], mask_qk[:, :], start=False, stop=True)
                else:
                    for jj in range(4):
                        h = 4 * g + jj
                        m = pe.matmul(dst[:, jj * SC:(jj + 1) * SC], q_stack[0:ROW_MAX, h, qt * P:(qt + 1) * P],
                                      k_stack[0:ROW_MAX, h, T:T + SC], start=True, stop=True)
                m.then_inc(a.smax, 1)

            def turn_max(g):
                pe.wait_ge(a.mx_split, per(i, 4, g + 1))
                mix_waits(a, pe, i, ("mx", g))
                for qt in range(NT):
                    m = pe.transpose(mix_bf[0:12, qt * P:(qt + 1) * P],
                                     mx_parts[:, g % 2, qt, :, :].rearrange("p c j -> p (c j)"), ident_bf[:, :])
                m.then_inc(a.mx_tr, 1)

            def scores(g, s):
                n = g * NS + s
                kt, pair = a.steps[s]
                k0, kn, q0 = a.tiles[kt]
                if s == 0:
                    pe.wait_ge(a.mx_in, per(i, 64, 16 * (g + 1)))
                if n >= 2:
                    pe.wait_ge(a.ex, per(i, 4 * NS, n - 1))
                for jj in range(2):
                    h = 4 * g + 2 * pair + jj
                    m = pe.matmul(st_bank[n % 2][0:kn, jj, 0:T - q0], k_stack[:, h, k0:k0 + kn], q_stack[:, h, q0:T],
                                  start=True, stop=not a.causal)
                    if a.causal:
                        m = pe.matmul(st_bank[n % 2][:, jj, 0:P], ident_bf[:, :], mask_kq[:, :], start=False, stop=True)
                m.then_inc(a.st, 1)

            def weigh(g, kt):
                n = g * NS + 2 * kt
                k0, kn, q0 = a.tiles[kt]
                pe.wait_ge(a.ex, per(i, 4 * NS, n + 2))
                if kt == 0 and g:
                    pe.wait_ge(a.heads_T, per(i, 4, g))
                for j in range(4):
                    m = pe.matmul(pv_bank[32 * j:32 * j + 32, q0:T], v_aug[0:kn, kt, 4 * g + j, :],
                                  probs[0:kn, (n + j // 2) % NPR, j % 2, 0:T - q0], start=(kt == 0), stop=(kt == len(a.tiles) - 1))
                m.then_inc(a.pv, 1)

            def turn_heads(g):
                pe.wait_ge(a.heads_T, per(i, 4, g + 1))
                mix_waits(a, pe, i, ("heads", g))
                for qt in range(NT):
                    m = pe.transpose(mix_bank[:, qt * P:(qt + 1) * P], heads_T[:, g % 2, qt * P:(qt + 1) * P], ident[:, :])
                m.then_inc(a.heads_Tt, 1)

            def attend(following):
                for g in range(4):
                    u = 0
                    for s in range(NS):
                        scores(g, s)
                        if s >= 3 and s % 2:
                            weigh(g, (s - 3) // 2)
                        if s == 2 and g:
                            turn_heads(g - 1)
                        while g < 3 and u < min(NU, 4 * (s + 1)):
                            scores_for_max(g + 1, u)
                            u += 1
                        if g < 3 and s == a.turn_at:
                            turn_max(g + 1)
                        if g == 3 and following and s in PREPARE_AT:
                            pe_prepare(pe, *following, PREPARE_AT.index(s))
                    weigh(g, NS // 2 - 1)

            def turn_back():
                pe.wait_ge(a.heads, per(i, 4, 4))
                for qt in range(NT):
                    m = pe.transpose(mix_bank[:, qt * P:(qt + 1) * P], heads[:, qt, :], ident[:, :])
                m.then_inc(a.heads_tr, 1)

            def project():
                pe.wait_ge(a.hT, per(i, 1, 1))
                for qt in range(NT):
                    out_q = mix_bank[:, qt * P:(qt + 1) * P]
                    if not a.causal:
                        pe.matmul(out_q, one_row[:, :], bo0x[:, :], start=True, stop=False)
                    m = pe.matmul(out_q, hT[:, qt * P:(qt + 1) * P], a.w[:, n_proj, :], start=a.causal, stop=True)
                m.then_inc(a.wo, 1)

            def first_maxima(u0, u1):
                for u in range(u0, min(u1, NU)):
                    scores_for_max(0, u)

            return attend, turn_heads, turn_back, project, first_maxima, turn_max

        def dve_norm_stats(dve, i, a, x_tiles):
            for c in range(NT):
                dve.bn_stats(stats[:, c, :], x_tiles(c)).then_inc(ln.stats, 1)
            for c in range(NT):
                dve.wait_ge(ln.stats, per(a.k0 + i, NT, c + 1))
                dve.bn_aggr(meanvar[:, c, :], stats[:, c, :]).then_inc(ln.mv, 1)

        def dve_norm_apply(dve, i, a, x_tiles):
            dve.wait_ge(ln.rs, per(a.k0 + i, 1, 1))
            for c in range(NT):
                dve.tensor_scalar(xn[:, c, :], x_tiles(c), meanvar[:, c, 0:1], rstd[:, c:c + 1],
                                  ALU.subtract, ALU.mult).then_inc(ln.xn, 1)

        def dve_norm(dve, i, a, x_tiles):
            dve_norm_stats(dve, i, a, x_tiles)
            dve_norm_apply(dve, i, a, x_tiles)

        def tokens_of(i):
            return lambda c: x_sb[:, i, c, :]

        def dve_prepare(dve, i, a):
            if a.causal:
                src = [smax_bank[0][:, :], smax_bank[1][:, :]] * 2
                for n in range(2):
                    dve.wait_ge(a.proj, per(i, 5, 2 * n + 1))
                    dve.tensor_tensor(turn_a[:, n, :], src[2 * n], rope0[:, 2 * n, :], ALU.mult).then_inc(a.turned, 1)
                    dve.wait_ge(a.proj, per(i, 5, 2 * n + 2))
                    dve.tensor_tensor(turn_b[:, n, :], src[2 * n + 1], rope0[:, 2 * n + 1, :], ALU.mult).then_inc(a.turned, 1)
                    dve.wait_ge(a.turned, per(i, 4, 2 * n + 2))
                    dve.tensor_tensor(qk_f[:, n, :], turn_a[:, n, :], turn_b[:, n, :], ALU.add).then_inc(a.qk_sum, 1)
            else:
                dve.wait_ge(a.proj, per(i, 3, 1))
                dve.tensor_scalar(qk_f[:, 0, :], smax_bank[0][:, :], DH ** -0.5, None, ALU.mult).then_inc(a.turned, 1)
                dve.wait_ge(a.proj, per(i, 3, 2))
                dve.tensor_copy(qk_f[:, 1, :], smax_bank[1][:, :]).then_inc(a.turned, 1)
                dve.wait_ge(a.ctx_tr, per(i, 1, 1))
                dve.tensor_copy(ctxT[:, :], smax_bank[1][:, 0:SC]).then_inc(a.ctx_f, 1)

            def split(dst, res, full, done, before, count, base):
                dve.tensor_copy(dst(0), full).then_inc(done, 1)
                dve.wait_ge(done, per(i, count, base + 1))
                dve.tensor_tensor(res, full, dst(0), ALU.subtract).then_inc(done, 1)
                dve.wait_ge(done, per(i, count, base + 2))
                dve.tensor_copy(dst(1), res).then_inc(done, 1)
                dve.wait_ge(done, per(i, count, base + 3))
                dve.tensor_tensor(dst(2), res, dst(1), ALU.subtract).then_inc(done, 1)

            if a.causal:
                dve.wait_ge(a.qk_sum, per(i, 2, 1))
            else:
                dve.wait_ge(a.turned, per(i, 2, 1))
            split(lambda c: parts[:, 0, c, :], qk_r[:, 0, :], qk_f[:, 0, :], a.q_parts, None, 4, 0)
            if not a.causal:
                dve.wait_ge(a.ctx_f, per(i, 1, 1))
                split(lambda c: cparts[:, c, :], cres[:, :], ctxT[:, :], a.c_parts, None, 4, 0)

        def dve_attention(dve, i, a):
            NU = len(a.units)

            def maxima(g, u0=0, u1=NU):
                for u, (qt, j) in list(enumerate(a.units))[u0:u1]:
                    n = g * NU + u
                    dve.wait_ge(a.smax, per(i, 4 * NU, n + 1))
                    if u == 0 and g >= 2:
                        dve.wait_ge(a.mx_split, per(i, 4, g - 1))
                    if j < 4:
                        w = (qt + 1) * P if a.causal else T
                        dve.tensor_reduce(mx[:, g % 2, qt, j:j + 1], smax_bank[n % 2][:, 0:w], AX.X, ALU.max).then_inc(a.mx_done, 1)
                    else:
                        dve.tensor_reduce(mxc[:, g % 2, qt, :], smax_bank[n % 2][:, 0:4 * SC].rearrange("p (j s) -> p j s", s=SC),
                                          AX.X, ALU.max).then_inc(a.mx_done, 1)
                if not a.causal and u1 >= NU:
                    dve.wait_ge(a.mx_done, per(i, 4 * NU, (g + 1) * NU))
                    dve.tensor_tensor(mx[:, g % 2, :, :], mx[:, g % 2, :, :], mxc[:, g % 2, :, :], ALU.max).then_inc(a.mx_comb, 1)

            def normalize(g):
                dve.wait_ge(a.heads_Tt, per(i, 4, g + 1))
                src = mix_bank[:, :].rearrange("p (q j d) -> p q j d", q=NT, j=4)
                dve.reciprocal(rden[:, g % 2, :, :], src[:, :, :, DH]).then_inc(a.rden, 1)
                dve.wait_ge(a.rden, per(i, 4, g + 1))
                for qt in range(NT):
                    m = dve.tensor_tensor(heads[:, qt, 32 * g:32 * g + 32].rearrange("p (j d) -> p j d", d=DH), src[:, qt, :, 0:DH],
                                          rden[:, g % 2, qt, :].unsqueeze(2).to_broadcast([P, 4, DH]), ALU.mult)
                m.then_inc(a.heads, 1)

            def residual():
                dve.wait_ge(a.wo, per(i, 1, 1))
                xi = x_sb[:, i, :, :].rearrange("p c d -> p (c d)")
                dve.tensor_tensor(xi, xi, mix_bank[:, :], ALU.add).then_inc(a.res, 1)
                dve.wait_ge(a.res, per(i, 1, 1))

            return maxima, normalize, residual

        def act_prepare(act, i, a, part):
            if part == 0:
                act.wait_ge(ln.tr, per(a.k0 + i, NT, NT))
                act.activation(xT[:, :], smax_bank[0][:, :], ACT.Copy).then_inc(ln.xT, 1)
            else:
                act.wait_ge(a.proj, per(i, 5 if a.causal else 3, 5 if a.causal else 3))
                act.activation(v_augs[i % 2][:, 0:NT, :, 0:DH], smax_bank[0][:, :].rearrange("p (c h d) -> p c h d", c=NT, h=H),
                               ACT.Copy).then_inc(a.v_in, 1)

        def act_attention(act, i, a):
            NS = len(a.steps)

            def max_rows(g):
                act.wait_ge(a.mx_tr, per(i, 4, g + 1))
                if g >= 2:
                    act.wait_ge(a.mx_scr, per(i, 64, 16 * (g - 1)))
                act.activation(mx_rows[:, g % 2, :], mix_bf[0:12, 0:T], ACT.Copy).then_inc(a.mx_row, 1)

            def take_heads(g):
                act.wait_ge(a.pv, per(i, 2 * NS, (g + 1) * (NS // 2)))
                if g >= 2:
                    act.wait_ge(a.heads_Tt, per(i, 4, g - 1))
                act.activation(heads_T[:, g % 2, :], pv_bank[:, :], ACT.Copy).then_inc(a.heads_T, 1)

            def attend(following):
                for g in range(4):
                    for s, (kt, pair) in enumerate(a.steps):
                        n = g * NS + s
                        k0, kn, q0 = a.tiles[kt]
                        act.wait_ge(a.st, per(i, 4 * NS, n + 1))
                        if n >= NPR:
                            act.wait_ge(a.pv, per(i, 2 * NS, (n - NPR) // 2 + 1))
                        act.activation(probs[0:kn, n % NPR, :, 0:T - q0], st_bank[n % 2][0:kn, :, 0:T - q0],
                                       ACT.Exp).then_inc(a.ex, 1)
                        if s == 1 and g:
                            take_heads(g - 1)
                        if g < 3 and s == a.turn_at:
                            max_rows(g + 1)
                        if g == 3 and following and s == PREPARE_AT[0]:
                            act_prepare(act, *following, 0)
                        if g == 3 and following and s == PREPARE_AT[-1]:
                            act_prepare(act, *following, 1)
                take_heads(3)
                act.wait_ge(a.heads_tr, per(i, 1, 1))
                act.activation(hT[:, :], mix_bank[:, :], ACT.Copy).then_inc(a.hT, 1)

            return attend, max_rows

        def pool_norm(pool, i, a):
            pool.wait_ge(ln.mv, per(a.k0 + i, NT, NT))
            pool.tensor_scalar(sdev[:, :], meanvar[:, :, 1], LN_EPS, None, ALU.add).then_inc(ln.sd, 1)
            pool.wait_ge(ln.sd, per(a.k0 + i, 1, 1))
            pool.tensor_tensor(rstd[:, :], sdev[:, :], neg_half[:, :], ALU.pow).then_inc(ln.rs, 1)

        def pool_prepare(pool, i, a):
            v_aug = v_augs[i % 2]
            pool_norm(pool, i, a)
            if a.causal:
                pool.wait_ge(a.qk_sum, per(i, 2, 2))
            else:
                for n, src in enumerate((ctx_hd, ctx_dh)):
                    pool.tensor_scalar(ctx_now[:, n, :], src[:, i, :],
                                       keep[0:SC, i:i + 1], None, ALU.mult).then_inc(a.ctx_copy, 1)
                pool.wait_ge(a.ctx_copy, per(i, 2, 2))
                pool.tensor_copy(v_aug[0:SC, NT, :, 0:DH], ctx_now[:, 0, :].rearrange("p (h d) -> p h d", h=H)).then_inc(a.v_in, 1)
                pool.wait_ge(a.turned, per(i, 2, 2))
            full, res = qk_f[:, 1, :], qk_r[:, 1, :]
            dst = [parts[:, 1, c, :] for c in range(3)]
            pool.tensor_copy(dst[0], full).then_inc(a.k_parts, 1)
            pool.wait_ge(a.k_parts, per(i, 4, 1))
            pool.tensor_tensor(res, full, dst[0], ALU.subtract).then_inc(a.k_parts, 1)
            pool.wait_ge(a.k_parts, per(i, 4, 2))
            pool.tensor_copy(dst[1], res).then_inc(a.k_parts, 1)
            pool.wait_ge(a.k_parts, per(i, 4, 3))
            pool.tensor_tensor(dst[2], res, dst[1], ALU.subtract).then_inc(a.k_parts, 1)

        def pool_attention(pool, i, a):
            NU = len(a.units)
            CH = a.chain_n
            for g in range(4):
                b0 = CH * g
                pool.wait_ge(a.mx_done, per(i, 4 * NU, (g + 1) * NU))
                if g >= 2:
                    pool.wait_ge(a.mx_tr, per(i, 4, g - 1))
                if not a.causal:
                    pool.wait_ge(a.mx_comb, per(i, 4, g + 1))
                neg, res = mx_f[:, g % 2, 0, :, :], mx_f[:, g % 2, 1, :, :]
                part = [mx_parts[:, g % 2, :, c, :] for c in range(3)]
                pool.tensor_scalar(neg, mx[:, g % 2, :, :], -1.0, None, ALU.mult).then_inc(a.mx_chain, 1)
                pool.wait_ge(a.mx_chain, per(i, 4 * CH, b0 + 1))
                pool.tensor_copy(part[0], neg).then_inc(a.mx_chain, 1)
                pool.wait_ge(a.mx_chain, per(i, 4 * CH, b0 + 2))
                pool.tensor_tensor(res, neg, part[0], ALU.subtract).then_inc(a.mx_chain, 1)
                pool.wait_ge(a.mx_chain, per(i, 4 * CH, b0 + 3))
                pool.tensor_copy(part[1], res).then_inc(a.mx_chain, 1)
                pool.wait_ge(a.mx_chain, per(i, 4 * CH, b0 + 4))
                pool.tensor_tensor(part[2], res, part[1], ALU.subtract).then_inc(a.mx_split, 1)

        def sp_attention(sp, i, a):
            q_stack, k_stack = q_stacks[i % 2], k_stacks[i % 2]

            if not a.causal and i == 0:
                sp.wait_ge(s_mask, 1)
                sp.wait_ge(s_load, LOADED)
                for n in range(2):
                    sp.dma_start(k_stacks[n][0:1, :, T:T + SC], mask_row[:, :].rearrange("p (h s) -> p h s", h=H)).then_inc(a.mask_in, 16)
            def to_stack(parts_in_dram, stack, span):
                at = ROW_HI
                for last in (3, 2, 1):
                    sp.dma_start(stack[at:at + DH * last, :, span],
                                 parts_in_dram.rearrange("c (d h) t -> (c d) h t", h=H)[0:DH * last]).then_inc(a.stack, 16)
                    at += DH * last

            sp.wait_ge(a.q_parts, per(i, 4, 4))
            sp.dma_start(scr_qk[0].rearrange("c p t -> p c t"), parts[:, 0, :, :]).then_inc(a.scr_q, 16)
            if not a.causal:
                sp.wait_ge(a.c_parts, per(i, 4, 4))
                sp.dma_start(scr_c.rearrange("c p t -> p c t"), cparts[:, :, :]).then_inc(a.scr_ck, 16)
            sp.wait_ge(a.scr_q, per(i, 16, 16))
            flat = scr_qk[0].rearrange("c (d h) t -> c d (h t)", h=H)
            at = ROW_HI
            for c, times in ((0, 3), (1, 2), (2, 1)):
                sp.dma_start(q_stack[at:at + DH * times, :, :].rearrange("p h t -> p (h t)"),
                             flat[c:c + 1].to_broadcast([times, DH, H * T])).then_inc(a.stack, 16)
                at += DH * times
            if not a.causal:
                sp.wait_ge(a.scr_ck, per(i, 16, 16))
                to_stack(scr_c, k_stack, slice(T, T + SC))
            sp.wait_ge(a.k_parts, per(i, 4, 4))
            sp.dma_start(scr_qk[1].rearrange("c p t -> p c t"), parts[:, 1, :, :]).then_inc(a.scr_k, 16)
            sp.wait_ge(a.scr_k, per(i, 16, 16))
            to_stack(scr_qk[1], k_stack, slice(0, T))
            if not a.causal and i == 0:
                sp.wait_ge(a.mask_in, 32)
            for g in range(4):
                sp.wait_ge(a.mx_row, per(i, 4, g + 1))
                sp.dma_start(scr_mx[g % 2], mx_rows[:, g % 2, :]).then_inc(a.mx_scr, 16)
                sp.wait_ge(a.mx_scr, per(i, 64, 16 * (g + 1)))
                sp.dma_start(q_stack[ROW_MAX:ROWS, 4 * g:4 * g + 4, :].rearrange("p h t -> p (h t)"),
                             scr_mx[g % 2].rearrange("(c j) t -> c (j t)", c=3)).then_inc(a.mx_in, 16)

        PREPARE_AT = (0, 2, 3, 4)

        s_mask = sem("s_mask")
        s_len = sem("s_len")
        in_block_1 = []
        own = attention("own", True, w0, 0)
        cross = attention("cross", False, w0x, B, " ctx_copy ctx_tr ctx_f c_parts mask_in scr_ck")
        cleared.extend(in_block_1)

        def chunk(c):
            return lambda b: x_sb[:, b, c, :]

        def pe_norm(pe, c, a, to=None):
            to = mix_bank[:, :] if to is None else to
            for b in range(B):
                pe.wait_ge(ln.xn, per(a.k0 + c, B, b + 1))
                pe.transpose(to[:, b * P:(b + 1) * P], xn[:, b, :], ident[:, :]).then_inc(ln.tr, 1)

        def tiles(ap):
            return ap.rearrange("p (b t) -> p b t", b=B)

        ring = [smax_bank[0][:, :], smax_bank[1][:, :], st_bank[0][:, 0, :], st_bank[0][:, 1, :]]
        y_bank = [st_bank[1][:, 0, :], st_bank[1][:, 1, :]]
        mix = mix_bank[:, :]

        f = signals("ffn0", "load up_in down_in logits lmax shift exp sum rec prob top idx idxf ga gb gates up gelu down skip acc", k0=2 * B)
        NF = F0 // P
        ffn0_loads = [(router_w[:, :], "router_w"),
                      (router_b[:, :], "router_b"), (places[:, :], "places")]

        def pe_route0(pe, c, part):
            if part == 0:
                for b in range(B):
                    pe.wait_ge(ln.xn, per(f.k0 + c, B, b + 1))
                    pe.transpose(mix[:, b * P:(b + 1) * P], xn0[:, c % 2, b, :], ident[:, :]).then_inc(ln.tr, 1)
            else:
                pe.wait_ge(ln.xT, f.k0 + c + 1)
                logits = mix[:, 0:B * 16].rearrange("p (b e) -> p b e", e=16)
                for b in range(B):
                    pe.matmul(logits[:, b, 0:E0 + 1], one_row[:, :], router_b[:, :], start=True, stop=False)
                    m = pe.matmul(logits[:, b, 0:E0 + 1], x0_T[:, c % 2, b * P:(b + 1) * P], router_w[:, :], start=False, stop=True)
                m.then_inc(f.logits, 1)

        def pe_ffn0(pe, c):
            if c == 0:
                pe.wait_ge(f.up_in, 16)

            def up(e):
                for n in range(NF):
                    k = NF * e + n
                    if c or k >= 4:
                        pe.wait_ge(f.gelu, per(c, E0 * NF, k - 3))
                    pe.matmul(ring[k % 4], up0[:, e, n * P:(n + 1) * P], x0_T[:, c % 2, :], start=True, stop=True).then_inc(f.up, 1)

            def down(e):
                if c == 0 and e == 0:
                    pe.wait_ge(f.down_in, 16)
                if c or e >= 2:
                    pe.wait_ge(f.acc, per(c, E0 * B, (e - 1) * B))
                pe.wait_ge(f.gelu, per(c, E0 * NF, NF * (e + 1)))
                for b in range(B):
                    for n in range(NF):
                        m = pe.matmul(y_bank[e % 2][:, b * P:(b + 1) * P], hidden[:, e % 2, n, b * P:(b + 1) * P], down0[:, e, n, :],
                                      start=(n == 0), stop=(n == NF - 1))
                m.then_inc(f.down, 1)

            up(0)
            up(1)
            for e in range(E0):
                down(e)
                if e + 2 < E0:
                    up(e + 2)
                if e in (3, 4) and c + 1 < NT:
                    pe_route0(pe, c + 1, e - 3)

        def dve_norm0(dve, c):
            dve.wait_ge(ln.rs, f.k0 + c + 1)
            for b in range(B):
                dve.tensor_scalar(xn0[:, c % 2, b, :], x_sb[:, b, c, :], meanvar[:, b, 0:1], rstd[:, b:b + 1],
                                  ALU.subtract, ALU.mult).then_inc(ln.xn, 1)

        def dve_route0(dve, c):
            logits = mix[:, 0:B * 16].rearrange("p (b e) -> p b e", e=16)[:, :, 0:E0 + 1]
            wide = [P, B, E0 + 1]
            dve.wait_ge(f.logits, c + 1)
            dve.tensor_reduce(lmax[:, :], logits, AX.X, ALU.max).then_inc(f.lmax, 1)
            dve.wait_ge(f.lmax, c + 1)
            dve.tensor_tensor(shifted[:, :, :], logits, lmax[:, :].unsqueeze(2).to_broadcast(wide), ALU.subtract).then_inc(f.shift, 1)
            dve.wait_ge(f.exp, c + 1)
            dve.tensor_reduce(esum[:, :], expd[:, :, :], AX.X, ALU.add).then_inc(f.sum, 1)
            dve.wait_ge(f.sum, c + 1)
            dve.reciprocal(erec[:, :], esum[:, :]).then_inc(f.rec, 1)
            dve.wait_ge(f.rec, c + 1)
            dve.tensor_tensor(gprobs[:, :, :], expd[:, :, :], erec[:, :].unsqueeze(2).to_broadcast(wide), ALU.mult).then_inc(f.prob, 1)
            dve.wait_ge(f.prob, c + 1)
            for b in range(B):
                dve.max(top_v[:, b, :], gprobs[:, b, :]).then_inc(f.top, 1)
            for b in range(B):
                dve.wait_ge(f.top, per(c, B, b + 1))
                dve.max_index(top_i[:, b, :], top_v[:, b, :], gprobs[:, b, :]).then_inc(f.idx, 1)
            dve.wait_ge(f.idx, per(c, B, B))
            dve.tensor_copy(top_f[:, :, :], top_i[:, :, :]).then_inc(f.idxf, 1)
            dve.wait_ge(f.idxf, c + 1)
            for b in range(B):
                dve.tensor_scalar(gate_a[:, b, :], places[:, :], top_f[:, b, 0:1], top_v[:, b, 0:1], ALU.is_equal, ALU.mult).then_inc(f.ga, 1)
                dve.tensor_scalar(gate_b[:, b, :], places[:, :], top_f[:, b, 1:2], top_v[:, b, 1:2], ALU.is_equal, ALU.mult).then_inc(f.gb, 1)
            dve.wait_ge(f.ga, per(c, B, B))
            dve.wait_ge(f.gb, per(c, B, B))
            dve.tensor_tensor(gates[:, c % 2, :, :], gate_a[:, :, :], gate_b[:, :, :], ALU.add).then_inc(f.gates, 1)

        def dve_ffn0(dve, c):
            dve.wait_ge(f.gates, c + 1)
            for b in range(B):
                dve.scalar_tensor_tensor(out=x_sb[:, b, c, :], in0=xn0[:, c % 2, b, :], scalar=gates[:, c % 2, b, E0:E0 + 1], in1=x_sb[:, b, c, :],
                                         op0=ALU.mult, op1=ALU.add).then_inc(f.skip, 1)
            dve.wait_ge(f.skip, per(c, B, B))
            for e in range(E0):
                if e:
                    dve.wait_ge(f.acc, per(c, E0 * B, e * B))
                dve.wait_ge(f.down, per(c, E0, e + 1))
                for b in range(B):
                    dve.scalar_tensor_tensor(out=x_sb[:, b, c, :], in0=y_bank[e % 2][:, b * P:(b + 1) * P],
                                             scalar=gates[:, c % 2, b, e:e + 1], in1=x_sb[:, b, c, :],
                                             op0=ALU.mult, op1=ALU.add).then_inc(f.acc, 1)
                if c + 1 < NT:
                    if e == 0:
                        dve_norm_stats(dve, c + 1, f, chunk(c + 1))
                    if e == 1:
                        dve_norm0(dve, c + 1)
                    if e == 4:
                        dve_route0(dve, c + 1)
            dve.wait_ge(f.acc, per(c + 1, E0 * B, 0))

        def act_route0(act, c, part):
            if part == 0:
                act.wait_ge(ln.tr, per(f.k0 + c, B, B))
                act.activation(x0_T[:, c % 2, :], mix, ACT.Copy).then_inc(ln.xT, 1)
            else:
                act.wait_ge(f.shift, c + 1)
                act.activation(expd[:, :, :], shifted[:, :, :], ACT.Exp).then_inc(f.exp, 1)

        def act_ffn0(act, c):
            def gelu(e):
                for n in range(NF):
                    k = NF * e + n
                    act.wait_ge(f.up, per(c, E0 * NF, k + 1))
                    if e >= 2:
                        act.wait_ge(f.down, per(c, E0, e - 1))
                    act.activation(hidden[:, e % 2, n, :], ring[k % 4], ACT.Gelu).then_inc(f.gelu, 1)

            for e in range(E0):
                gelu(e)
                if e in (5, 6) and c + 1 < NT:
                    act_route0(act, c + 1, e - 5)

        r = signals("rec", "init load edge xx mixed proj kept sq n2 n2f n2s inv unit scr seq "
                    "dprod dots kbd rows vkp vk prod sum outer step wr oprod osum omore oadd oscr oT mean cen osq var sd oinv on gn gated wo res", k0=2 * B + NT)
        rec_loads = [(w1a[:, :, :], "w1a"), (mix1[:, :], "mix1"), (bo1a[:, :], "bo1a"), (gn_w[:, :], "gn_w"), (gn_b[:, :], "gn_b")]
        R_, W_, K_, V_, A_, B_, G_ = range(7)
        scr_seq = nc.dram_tensor("scr_seq", [6, B, D, T], F32, kind="Internal").ap()
        scr_o = nc.dram_tensor("scr_o", [B * H, DH, T], F32, kind="Internal").ap()
        PLACE = {K_: 0, B_: 1, A_: 2, W_: 3, R_: 4}

        def pe_rec(pe, c):
            pe_norm(pe, c, r)
            for n in range(7):
                pe.wait_ge(r.mixed, per(c, 7, n + 1))
                if n >= 4:
                    pe.wait_ge(r.kept, per(c, 5, n - 3))
                pe.matmul(ring[n % 4], w1a[:, n, :], xi[:, n % 3, :], start=True, stop=True).then_inc(r.proj, 1)
                if n in (A_, B_):
                    pe.wait_ge(r.sq, per(c, 2, n - A_ + 1))
                    pe.matmul(y_bank[n - A_], blk_ones[:, :], sq[:, n - A_, :], start=True, stop=True).then_inc(r.n2, 1)

        def dve_rec_mix(dve, c, which):
            dve.wait_ge(r.xx, c + 1)
            dve.wait_ge(ln.xT, r.k0 + c + 1)
            for n in which:
                if n >= 3:
                    dve.wait_ge(r.proj, per(c, 7, n - 2))
                dve.scalar_tensor_tensor(out=tiles(xi[:, n % 3, :]), in0=xx[:, :, :], scalar=mix1[:, n:n + 1],
                                         in1=xs[:, c % 2, :, 1:P + 1], op0=ALU.mult, op1=ALU.add).then_inc(r.mixed, 1)

        def dve_rec_norms(dve, c):
            for k in range(2):
                dve.wait_ge(r.n2, per(c, 2, k + 1))
                dve.tensor_scalar(nrm[:, k, :], y_bank[k], NORM_EPS ** 2, None, ALU.max).then_inc(r.n2f, 1)

        def dve_rec_units(dve, c):
            for k in range(2):
                dve.wait_ge(r.n2s, per(c, 2, k + 1))
                dve.reciprocal(inv[:, k, :], sq[:, k, :]).then_inc(r.inv, 1)
            if c:
                dve.wait_ge(r.scr, per(c - 1, 96, 96))
            for k in range(2):
                dve.wait_ge(r.inv, per(c, 2, k + 1))
                dve.tensor_tensor(dense[:, A_ + k, :], ring[(A_ + k) % 4], inv[:, k, :], ALU.mult).then_inc(r.unit, 1)

        def act_rec(act, c):
            act.wait_ge(ln.tr, per(r.k0 + c, B, B))
            act.activation(xs[:, c % 2, :, 1:P + 1], mix.rearrange("p (b t) -> p b t", b=B), ACT.Copy).then_inc(ln.xT, 1)
            func = {R_: ACT.Copy, W_: ACT.Sigmoid, K_: ACT.Tanh, V_: ACT.Copy}
            for n in (R_, W_, K_, V_):
                act.wait_ge(r.proj, per(c, 7, n + 1))
                if c:
                    act.wait_ge(r.scr, per(c - 1, 96, 96))
                act.activation(dense[:, n, :], ring[n % 4], func[n], scale=-1.0 if n == W_ else 1.0).then_inc(r.kept, 1)
            for k in range(2):
                act.wait_ge(r.proj, per(c, 7, A_ + k + 1))
                act.activation(sq[:, k, :], ring[(A_ + k) % 4], ACT.Square).then_inc(r.sq, 1)
            act.wait_ge(r.proj, per(c, 7, 7))
            act.activation(gate_T[:, c, :], ring[G_ % 4], ACT.Sigmoid).then_inc(r.kept, 1)
            for k in range(2):
                act.wait_ge(r.n2f, per(c, 2, k + 1))
                act.activation(sq[:, k, :], nrm[:, k, :], ACT.Sqrt).then_inc(r.n2s, 1)

        def pool_rec_before(pool, c):
            pool.wait_ge(ln.xT, r.k0 + c + 1)
            if c:
                pool.tensor_copy(xs[:, c % 2, :, 0:1], xs[:, (c - 1) % 2, :, P:P + 1]).then_inc(r.edge, 1)
                pool.wait_ge(r.edge, c)
            pool.tensor_tensor(xx[:, :, :], xs[:, c % 2, :, 0:P], xs[:, c % 2, :, 1:P + 1], ALU.subtract).then_inc(r.xx, 1)

        def sp_rec(sp, c):
            span = slice(c * P, (c + 1) * P)
            for k, n in enumerate((R_, W_, K_, V_, A_, B_)):
                if n >= A_:
                    sp.wait_ge(r.unit, per(c, 2, n - A_ + 1))
                else:
                    sp.wait_ge(r.kept, per(c, 5, n + 1))
                sp.dma_start(scr_seq[n].rearrange("b r t -> r b t")[:, :, span], tiles(dense[:, n, :])).then_inc(r.scr, 16)
            sp.wait_ge(r.scr, per(c, 96, 96))
            if c >= 2:
                sp.wait_ge(r.oadd, (c - 1) * NB)
            for k, n in enumerate((R_, W_, K_, V_, A_, B_)):
                src = scr_seq[n].rearrange("b (h k) t -> (b h) k t", h=H)
                for half in range(2):
                    rows = src[:, 4 * half:4 * half + 4, span] if n == V_ else src[:, :, span]
                    to = seq_v[:, c % 2, :, :] if n == V_ else seqs[:, c % 2, PLACE[n], :, :]
                    sp.dma_start(to[64 * half:64 * half + 64], rows).then_inc(r.seq, 16)

        I = DH // 2
        KB = slice(0, 2)

        def seq_of(blk, which, first):
            t0 = (blk % NB) * HB
            return seqs[:, (blk // NB) % 2, which, :, t0 + 1 - first:t0 + HB:2]

        def v_of(blk, first):
            t0 = (blk % NB) * HB
            return seq_v[:, (blk // NB) % 2, :, t0 + 1 - first:t0 + HB:2]

        def pool_pairs_a(pool, blk):
            buf = blk % 2
            two = [P, 2, DH, PB]
            pool.wait_ge(r.seq, per(blk // NB, 192, 192))
            if blk >= 2:
                pool.wait_ge(r.step, (blk - 1) * PB)
            kb = seq_of(blk, KB, 1)
            pool.tensor_tensor(dot_prod[:, buf, 0:2, :, :], kb, seq_of(blk, PLACE[A_], 0).unsqueeze(1).to_broadcast(two), ALU.mult)
            pool.tensor_tensor(dot_prod[:, buf, 2:4, :, :], kb, seq_of(blk, PLACE[R_], 1).unsqueeze(1).to_broadcast(two),
                               ALU.mult).then_inc(r.dprod, 1)
            pool.tensor_tensor(kb_w[:, buf, :, :, :], kb, seq_of(blk, PLACE[W_], 0).unsqueeze(1).to_broadcast(two), ALU.mult)
            pool.tensor_copy(by_state[:, buf, 0, :, :], seq_of(blk, PLACE[A_], 1))
            pool.tensor_tensor(by_state[:, buf, 1:3, :, :], seq_of(blk, slice(PLACE[A_], PLACE[W_] + 1), 0),
                               seq_of(blk, PLACE[W_], 1).unsqueeze(1).to_broadcast(two), ALU.mult)
            pool.tensor_copy(rows_kb[:, buf, 2, :, :], seq_of(blk, PLACE[B_], 0)).then_inc(r.wr, 1)

        def dve_dots(dve, blk):
            dve.wait_ge(r.dprod, blk + 1)
            if blk >= 2:
                dve.wait_ge(r.omore, 3 * (blk - 1))
            dve.tensor_reduce(dots[:, blk % 2, :, :], dot_prod[:, blk % 2, :, :, :].rearrange("p x k t -> p x t k"), AX.X,
                              ALU.add).then_inc(r.dots, 1)

        def pool_pairs_b(pool, blk):
            buf = blk % 2
            two = [P, 2, DH, PB]
            pool.wait_ge(r.dots, blk + 1)
            pool.wait_ge(r.wr, blk + 1)
            pool.tensor_tensor(kb_dot[:, buf, :, :, :], dots[:, buf, 0:2, :].unsqueeze(2).to_broadcast(two),
                               rows_kb[:, buf, 2, :, :].unsqueeze(1).to_broadcast(two), ALU.mult).then_inc(r.kbd, 1)
            pool.wait_ge(r.kbd, blk + 1)
            pool.tensor_tensor(rows_kb[:, buf, 0:2, :, :], kb_dot[:, buf, :, :, :], kb_w[:, buf, :, :, :], ALU.add).then_inc(r.rows, 1)
            wide = [P, PB, I, DH]
            pool.tensor_tensor(vk[:, 1, :, :, :], v_of(blk, 0).rearrange("p i t -> p t i").unsqueeze(3).to_broadcast(wide),
                               seq_of(blk, PLACE[K_], 0).rearrange("p k t -> p t k").unsqueeze(2).to_broadcast(wide), ALU.mult)
            pool.wait_ge(r.rows, blk + 1)
            pool.tensor_tensor(vk[:, 0, :, :, :], v_of(blk, 1).rearrange("p i t -> p t i").unsqueeze(3).to_broadcast(wide),
                               rows_kb[:, buf, 0, :, :].rearrange("p k t -> p t k").unsqueeze(2).to_broadcast(wide),
                               ALU.mult).then_inc(r.vkp, 1)
            pool.wait_ge(r.vkp, blk + 1)
            pool.tensor_tensor(terms[:, buf, :, 5, :, :], vk[:, 0, :, :, :], vk[:, 1, :, :, :], ALU.add).then_inc(r.vk, 1)

        def dve_steps(dve, c, t0, t1):
            for n in range((c * P + t0) // 2, (c * P + t1) // 2):
                blk, s = n // PB, n % PB
                buf = blk % 2
                if s == 0:
                    dve.wait_ge(r.vk, blk + 1)
                    if blk >= 2:
                        dve.wait_ge(r.oadd, blk - 1)
                if n:
                    dve.wait_ge(r.step, n)
                    prev = hist[:, ((n - 1) // PB) % 2, (n - 1) % PB, :, :]
                else:
                    prev = state0[:, :, :]
                dve.tensor_tensor(terms[:, buf, s, 0:3, :, :], prev.unsqueeze(1).to_broadcast([P, 3, I, DH]),
                                  by_state[:, buf, :, :, s].unsqueeze(2).to_broadcast([P, 3, I, DH]), ALU.mult).then_inc(r.prod, 1)
                dve.wait_ge(r.prod, n + 1)
                dve.tensor_reduce(sums[:, buf, s, :, :], terms[:, buf, s, 0:2, :, :], AX.X, ALU.add).then_inc(r.sum, 1)
                dve.wait_ge(r.sum, n + 1)
                dve.tensor_tensor(terms[:, buf, s, 3:5, :, :], sums[:, buf, s, :, :].unsqueeze(3).to_broadcast([P, 2, I, DH]),
                                  rows_kb[:, buf, 1:3, :, s].unsqueeze(2).to_broadcast([P, 2, I, DH]), ALU.mult).then_inc(r.outer, 1)
                dve.wait_ge(r.outer, n + 1)
                dve.tensor_reduce(hist[:, buf, s, :, :], terms[:, buf, s, 2:6, :, :].rearrange("p x i k -> p i k x"), AX.X,
                                  ALU.add).then_inc(r.step, 1)
                if s == 8 and blk + 1 < NT * NB:
                    dve_dots(dve, blk + 1)
                if s == 12 and blk:
                    dve_outputs(dve, blk - 1)

        def pool_products(pool, blk):
            buf = blk % 2
            pool.tensor_tensor(first_r[:, buf, :, :], seq_of(blk, PLACE[W_], 1), seq_of(blk, PLACE[R_], 1), ALU.mult).then_inc(r.omore, 1)
            pool.wait_ge(r.step, (blk + 1) * PB)
            if blk >= 2:
                pool.wait_ge(r.osum, blk - 1)
            wide = [P, PB, I, DH]
            pool.tensor_tensor(o_prod[:, buf, :, 1, :, :], hist[:, buf, :, :, :],
                               seq_of(blk, PLACE[R_], 0).rearrange("p k t -> p t k").unsqueeze(2).to_broadcast(wide), ALU.mult)
            by = first_r[:, buf, :, :].rearrange("p k t -> p t k").unsqueeze(2).to_broadcast(wide)
            before = hist[:, 1 - buf, PB - 1:PB, :, :] if blk else state0[:, :, :].unsqueeze(1)
            pool.wait_ge(r.omore, 3 * blk + 1)
            pool.tensor_tensor(o_prod[:, buf, 0:1, 0, :, :], before, by[:, 0:1], ALU.mult)
            pool.tensor_tensor(o_prod[:, buf, 1:PB, 0, :, :], hist[:, buf, 0:PB - 1, :, :], by[:, 1:PB], ALU.mult).then_inc(r.oprod, 1)
            small = [P, I, PB]
            pool.tensor_tensor(o_more[:, buf, 0, :, :], sums[:, buf, :, 0, :].rearrange("p t i -> p i t"),
                               dots[:, buf, 3, :].unsqueeze(1).to_broadcast(small), ALU.mult)
            pool.tensor_tensor(o_more[:, buf, 1, :, :], v_of(blk, 1), dots[:, buf, 2, :].unsqueeze(1).to_broadcast(small),
                               ALU.mult).then_inc(r.omore, 1)
            pool.wait_ge(r.omore, 3 * blk + 2)
            pool.tensor_tensor(o_more[:, buf, 2, :, :], o_more[:, buf, 0, :, :], o_more[:, buf, 1, :, :], ALU.add).then_inc(r.omore, 1)

        def dve_outputs(dve, blk):
            c, t0 = blk // NB, (blk % NB) * HB
            dve.wait_ge(r.oprod, blk + 1)
            if c >= 2 and t0 == 0:
                dve.wait_ge(r.oscr, per(c - 2, 32, 32))
            dve.tensor_reduce(o_seq[:, c % 2, :, t0:t0 + HB].rearrange("p i (s x) -> p s x i", x=2), o_prod[:, blk % 2, :, :, :, :],
                              AX.X, ALU.add).then_inc(r.osum, 1)

        def pool_outputs(pool, blk):
            c, t0 = blk // NB, (blk % NB) * HB
            o1 = o_seq[:, c % 2, :, t0:t0 + HB:2]
            pool.wait_ge(r.osum, blk + 1)
            pool.wait_ge(r.omore, 3 * blk + 3)
            pool.tensor_tensor(o1, o1, o_more[:, blk % 2, 2, :, :], ALU.add).then_inc(r.oadd, 1)

        def sp_out1(sp, c):
            span = slice(c * P, (c + 1) * P)
            sp.wait_ge(r.oadd, per(c, NB, NB))
            for half in range(2):
                sp.dma_start(scr_o[:, 4 * half:4 * half + 4, span], o_seq[64 * half:64 * half + 64, c % 2, :, :]).then_inc(r.oscr, 16)
            sp.wait_ge(r.oscr, per(c, 32, 32))
            if c:
                sp.wait_ge(r.cen, c)
            sp.dma_start(o_T[:, :, :],
                         scr_o.rearrange("(b h) v t -> b (h v) t", b=B).rearrange("b r t -> r b t")[:, :, span]).then_inc(r.oT, 16)

        def pe_out1(pe, c):
            pe.wait_ge(r.unit, per(min(c + 2, NT - 1), 2, 2))
            pe.wait_ge(r.oT, per(c, 16, 16))
            pe.matmul(ring[0], blk_mean[:, :], o_T[:, :, :], start=True, stop=True).then_inc(r.mean, 1)
            pe.wait_ge(r.osq, c + 1)
            pe.matmul(ring[1], blk_mean[:, :], o_sq[:, :], start=True, stop=True).then_inc(r.var, 1)
            pe.wait_ge(r.gated, c + 1)
            for b in range(B):
                pe.matmul(mix[:, b * P:(b + 1) * P], one_row[:, :], bo1a[:, :], start=True, stop=False)
                m = pe.matmul(mix[:, b * P:(b + 1) * P], o_n[:, b * P:(b + 1) * P], w1a[:, 7, :], start=False, stop=True)
            m.then_inc(r.wo, 1)

        def dve_out1_center(dve, c):
            dve.wait_ge(r.mean, c + 1)
            dve.tensor_tensor(tiles(o_cen[:, :]), o_T[:, :, :], tiles(ring[0]), ALU.subtract).then_inc(r.cen, 1)

        def dve_out1_norm(dve, c):
            dve.wait_ge(r.sd, c + 1)
            dve.reciprocal(o_inv[:, :], o_sd[:, :]).then_inc(r.oinv, 1)
            dve.wait_ge(r.oinv, c + 1)
            dve.tensor_tensor(o_n[:, :], o_cen[:, :], o_inv[:, :], ALU.mult).then_inc(r.on, 1)
            dve.wait_ge(r.on, c + 1)
            dve.tensor_scalar(o_cen[:, :], o_n[:, :], gn_w[:, 0:1], gn_b[:, 0:1], ALU.mult, ALU.add).then_inc(r.gn, 1)
            dve.wait_ge(r.gn, c + 1)
            dve.tensor_tensor(o_n[:, :], o_cen[:, :], gate_T[:, c, :], ALU.mult).then_inc(r.gated, 1)

        def dve_out1_residual(dve, c):
            dve.wait_ge(r.wo, c + 1)
            dve.tensor_tensor(x_sb[:, :, c, :], x_sb[:, :, c, :], mix.rearrange("p (b d) -> p b d", b=B), ALU.add).then_inc(r.res, 1)
            dve.wait_ge(r.res, c + 1)

        def act_out1(act, c):
            act.wait_ge(r.cen, c + 1)
            act.activation(o_sq[:, :], o_cen[:, :], ACT.Square).then_inc(r.osq, 1)
            act.wait_ge(r.var, c + 1)
            act.activation(o_sd[:, :], ring[1], ACT.Sqrt, bias=gn_eps[:, :]).then_inc(r.sd, 1)

        z = signals("cross1", "init load ctxT ctxTs ck ckt kf kparts cscr cstk cv cvs pad padf pm proj turned full split scr "
                    "stack sc masked mx sub ex ptr pT pv o1 o1t rd hd hdt hT wo res", k0=2 * B + 2 * NT)
        cross1_loads = [(w1x[:, :, :], "w1x"), (b1x[:, :], "b1x"), (bv1x[:, :], "bv1x"), (bo1x[:, :], "bo1x"),
                        (rope1[:, :, :], "rope1"), (causal1[:, :], "causal1")]
        scr_k1 = nc.dram_tensor("scr_k1", [3, P, B, SC], BF16, kind="Internal").ap()
        scr_q1 = nc.dram_tensor("scr_q1", [3, P, T], BF16, kind="Internal").ap()
        NSC = B * SC
        HEADS_OF = [(0, 6), (6, 6), (12, 4)]

        def pe_ctx1(pe):
            for b in range(B):
                m = pe.transpose(mix[:, b * SC:(b + 1) * SC], ctx1[:, b, :], ident[0:SC, 0:SC])
            m.then_inc(z.ctxT, 1)
            pe.wait_ge(z.ctxTs, 1)
            for n in range(2):
                pe.matmul(ring[n][:, 0:NSC], w1x[:, 2 + n, :], ctx1_T[:, :, :].rearrange("p b s -> p (b s)"),
                          start=True, stop=True).then_inc(z.ck, 1)
            for b in range(B):
                pe.matmul(ring[2][0:SC, b * P:(b + 1) * P], one_row[:, 0:SC], bv1x[:, :], start=True, stop=False)
                m = pe.matmul(ring[2][0:SC, b * P:(b + 1) * P], ctx1_T[:, b, :], w1x[:, 4, :], start=False, stop=True)
            m.then_inc(z.cv, 1)

        def dve_ctx1(dve):
            flat = [turn1_a[:, 0:NSC], turn1_b[:, 0:NSC]]
            for n in range(2):
                dve.wait_ge(z.ck, n + 1)
                table = rope1[:, 2 + n, 0:SC].unsqueeze(1).to_broadcast([P, B, SC])
                dve.scalar_tensor_tensor(out=flat[n].rearrange("p (b s) -> p b s", b=B),
                                         in0=ring[n][:, 0:NSC].rearrange("p (b s) -> p b s", b=B),
                                         scalar=b1x[:, 2 + n:3 + n], in1=table, op0=ALU.add, op1=ALU.mult).then_inc(z.ckt, 1)
            dve.wait_ge(z.ckt, 2)
            dve.tensor_tensor(full1[:, 0:NSC], flat[0], flat[1], ALU.add).then_inc(z.kf, 1)
            dve.wait_ge(z.kf, 1)
            split(dve, [parts1[:, k, 0:NSC] for k in range(3)], res1[:, 0:NSC], full1[:, 0:NSC], z.kparts, 0)
            dve.tensor_copy(pad_f[:, :, :], pad_i[:, :, :]).then_inc(z.pad, 1)
            dve.wait_ge(z.pad, 1)
            dve.tensor_scalar(mask1[:, :, :], pad_f[:, :, :], -1e9, None, ALU.mult).then_inc(z.padf, 1)
            dve.wait_ge(z.padf, 1)
            dve.tensor_tensor(mask1c[:, :, :], mask1[:, :, :], causal1[:, :].unsqueeze(1).to_broadcast([P, B, SC]),
                              ALU.add).then_inc(z.pm, 1)
            dve.wait_ge(z.pm, 1)

        def act_ctx1(act):
            act.wait_ge(z.ctxT, 1)
            act.activation(ctx1_T[:, :, :], mix[:, 0:NSC].rearrange("p (b s) -> p b s", b=B), ACT.Copy).then_inc(z.ctxTs, 1)
            act.wait_ge(z.cv, 1)
            act.wait_ge(z.init, 3)
            for b in range(B):
                act.activation(v1_aug[:, b, :, 0:DH], ring[2][0:SC, b * P:(b + 1) * P].rearrange("p (h d) -> p h d", h=H),
                               ACT.Copy).then_inc(z.cvs, 1)

        def sp_ctx1(sp):
            sp.wait_ge(z.kparts, 4)
            sp.dma_start(scr_k1.rearrange("k p b s -> p k (b s)"), parts1[:, :, 0:NSC]).then_inc(z.cscr, 16)
            sp.wait_ge(z.cscr, 16)
            sp.wait_ge(z.init, 3)
            for b in range(B):
                rows = scr_k1.rearrange("k (d h) b s -> (k d) b h s", h=H)
                at = ROW_HI
                for last in (3, 2, 1):
                    sp.dma_start(k1_stack[at:at + DH * last, b, :, :], rows[0:DH * last, b]).then_inc(z.cstk, 16)
                    at += DH * last

        q_bank = ring[3]

        def pe_query1(pe, c, n):
            if n == 0:
                pe.wait_ge(ln.xT, z.k0 + c + 1)
            else:
                pe.wait_ge(z.turned, per(c, 2, 1))
            pe.matmul(q_bank, w1x[:, n, :], xT[:, :], start=True, stop=True).then_inc(z.proj, 1)

        def dve_query1(dve, c, n):
            dve.wait_ge(z.proj, per(c, 2, n + 1))
            table = rope1[:, n, c * P:(c + 1) * P].unsqueeze(1).to_broadcast([P, B, P])
            dve.scalar_tensor_tensor(out=tiles((turn1_a if n == 0 else turn1_b)[:, :]), in0=tiles(q_bank),
                                     scalar=b1x[:, n:n + 1], in1=table, op0=ALU.add, op1=ALU.mult).then_inc(z.turned, 1)

        def dve_query1_parts(dve, c):
            dve.wait_ge(z.turned, per(c, 2, 2))
            dve.tensor_tensor(full1[:, :], turn1_a[:, :], turn1_b[:, :], ALU.add).then_inc(z.full, 1)
            dve.wait_ge(z.full, c + 1)
            if c == 0:
                dve.wait_ge(z.cscr, 16)
            else:
                dve.wait_ge(z.scr, per(c - 1, 16, 16))
            split(dve, [parts1[:, k, :] for k in range(3)], res1[:, :], full1[:, :], z.split, c)

        def act_query1(act, c):
            act.wait_ge(ln.tr, per(z.k0 + c, B, B))
            act.activation(xT[:, :], q_bank, ACT.Copy).then_inc(ln.xT, 1)

        def pe_cross1(pe, c):
            pe.wait_ge(z.stack, per(c, 96, 96))
            if c == 0:
                pe.wait_ge(z.cstk, 16 * 12)
                pe.wait_ge(z.cvs, B)

            def scores(b):
                k0 = 3 * (B * c + b)
                for k, (h0, nh) in enumerate(HEADS_OF):
                    if b:
                        pe.wait_ge(z.masked, k0 + k - 2)
                    for h in range(h0, h0 + nh):
                        m = pe.matmul(ring[k][:, (h - h0) * SC:(h - h0 + 1) * SC], q_stack[0:ROW_MAX, h, b * P:(b + 1) * P],
                                      k1_stack[:, b, h, :], start=True, stop=True)
                    m.then_inc(z.sc, 1)

            def turn_probs(b):
                n0 = 4 * (B * c + b)
                pe.wait_ge(z.ex, B * c + b + 1)
                for g in range(4):
                    n = n0 + g
                    if n >= 2:
                        pe.wait_ge(z.pT, n - 1)
                    for j in range(4):
                        m = pe.transpose(y_bank[n % 2][0:SC, j * P:(j + 1) * P], p1[:, b % 2, 4 * g + j, :], ident[:, :])
                    m.then_inc(z.ptr, 1)

            def weigh(b):
                n0 = 4 * (B * c + b)
                if B * c + b:
                    pe.wait_ge(z.o1, B * c + b)
                for g in range(4):
                    pe.wait_ge(z.pT, n0 + g + 1)
                    for j in range(4):
                        m = pe.matmul(pv_bank[32 * j:32 * j + 32, g * P:(g + 1) * P], v1_aug[:, b, 4 * g + j, :],
                                      p1_T[:, b % 2, 4 * g + j, :], start=True, stop=True)
                m.then_inc(z.pv, 1)

            def back(b):
                n = B * c + b
                pe.wait_ge(z.o1, n + 1)
                if b:
                    pe.wait_ge(z.hd, n)
                for g in range(4):
                    m = pe.transpose(mix[:, g * P:(g + 1) * P], o1_T[:, b % 2, g, :], ident[:, :])
                m.then_inc(z.o1t, 1)

            scores(0)
            for b in range(B):
                if b + 1 < B:
                    scores(b + 1)
                turn_probs(b)
                if b == 3 and c + 1 < NT:
                    pe_query1(pe, c + 1, 1)
                if b:
                    back(b - 1)
                weigh(b)
                if b == 1 and c + 1 < NT:
                    pe_norm(pe, c + 1, z, q_bank)
                if b == 2 and c + 1 < NT:
                    pe_query1(pe, c + 1, 0)
            back(B - 1)
            pe.wait_ge(z.hd, per(c, B, B))
            for b in range(B):
                m = pe.transpose(mix[:, b * P:(b + 1) * P], heads1[:, b, :], ident[:, :])
            m.then_inc(z.hdt, 1)
            pe.wait_ge(z.hT, c + 1)
            for b in range(B):
                pe.matmul(mix[:, b * P:(b + 1) * P], one_row[:, :], bo1x[:, :], start=True, stop=False)
                m = pe.matmul(mix[:, b * P:(b + 1) * P], h1_T[:, b, :], w1x[:, 5, :], start=False, stop=True)
            m.then_inc(z.wo, 1)

        def dve_cross1(dve, c):
            mask = (mask1 if c else mask1c)

            def masked(b):
                n = B * c + b
                if n >= 2:
                    dve.wait_ge(z.sub, n - 1)
                for k, (h0, nh) in enumerate(HEADS_OF):
                    dve.wait_ge(z.sc, 3 * n + k + 1)
                    dve.tensor_tensor(t1[:, b % 2, h0:h0 + nh, :], ring[k][:, 0:nh * SC].rearrange("p (h s) -> p h s", s=SC),
                                      mask[:, b, :].unsqueeze(1).to_broadcast([P, nh, SC]), ALU.add).then_inc(z.masked, 1)
                dve.wait_ge(z.masked, 3 * n + 3)
                dve.tensor_reduce(mx1[:, b % 2, :], t1[:, b % 2, :, :], AX.X, ALU.max).then_inc(z.mx, 1)

            def finish(b):
                n = B * c + b
                dve.wait_ge(z.o1t, n + 1)
                src = mix.rearrange("p (g j d) -> p g j d", g=4, j=4)
                dve.reciprocal(rden1[:, b % 2, :, :], src[:, :, :, DH]).then_inc(z.rd, 1)
                dve.wait_ge(z.rd, n + 1)
                for g in range(4):
                    m = dve.tensor_tensor(heads1[:, b, 32 * g:32 * g + 32].rearrange("p (j d) -> p j d", d=DH), src[:, g, :, 0:DH],
                                          rden1[:, b % 2, g, :].unsqueeze(2).to_broadcast([P, 4, DH]), ALU.mult)
                m.then_inc(z.hd, 1)

            masked(0)
            for b in range(B):
                if b + 1 < B:
                    masked(b + 1)
                if b == 3 and c + 1 < NT:
                    dve_query1(dve, c + 1, 1)
                    dve_query1_parts(dve, c + 1)
                if b:
                    finish(b - 1)
                if b == 0 and c + 1 < NT:
                    dve_norm_stats(dve, c + 1, z, chunk(c + 1))
                if b == 1 and c + 1 < NT:
                    dve_norm_apply(dve, c + 1, z, chunk(c + 1))
                if b == 2 and c + 1 < NT:
                    dve_query1(dve, c + 1, 0)
            finish(B - 1)
            dve.wait_ge(z.wo, c + 1)
            dve.tensor_tensor(x_sb[:, :, c, :], x_sb[:, :, c, :], mix.rearrange("p (b d) -> p b d", b=B), ALU.add).then_inc(z.res, 1)
            dve.wait_ge(z.res, c + 1)

        def act_cross1(act, c):
            def expo(b):
                n = B * c + b
                act.wait_ge(z.sub, n + 1)
                if n >= 2:
                    act.wait_ge(z.ptr, 4 * (n - 1))
                act.activation(p1[:, b % 2, :, :], t2[:, b % 2, :, :], ACT.Exp).then_inc(z.ex, 1)

            expo(0)
            for b in range(B):
                n = B * c + b
                for g in range(4):
                    act.wait_ge(z.ptr, 4 * n + g + 1)
                    if n >= 2:
                        act.wait_ge(z.pv, n - 1)
                    act.activation(p1_T[:, b % 2, 4 * g:4 * g + 4, :], y_bank[(4 * n + g) % 2][0:SC, :].rearrange("p (j q) -> p j q", j=4),
                                   ACT.Copy).then_inc(z.pT, 1)
                if b + 1 < B:
                    expo(b + 1)
                act.wait_ge(z.pv, n + 1)
                if n >= 2:
                    act.wait_ge(z.o1t, n - 1)
                act.activation(o1_T[:, b % 2, :, :], pv_bank[:, :].rearrange("p (g q) -> p g q", g=4), ACT.Copy).then_inc(z.o1, 1)
                if b == 1 and c + 1 < NT:
                    act_query1(act, c + 1)
            act.wait_ge(z.hdt, c + 1)
            act.activation(h1_T[:, :, :], tiles(mix), ACT.Copy).then_inc(z.hT, 1)

        def pool_cross1(pool, c):
            for b in range(B):
                n = B * c + b
                pool.wait_ge(z.mx, n + 1)
                if n >= 2:
                    pool.wait_ge(z.ex, n - 1)
                pool.tensor_tensor(t2[:, b % 2, :, :], t1[:, b % 2, :, :], mx1[:, b % 2, :].unsqueeze(2).to_broadcast([P, H, SC]),
                                   ALU.subtract).then_inc(z.sub, 1)
                if b == 1 and c + 1 < NT:
                    pool_norm(pool, c + 1, z)

        def sp_cross1(sp, c):
            sp.wait_ge(z.split, per(c, 4, 4))
            sp.dma_start(scr_q1.rearrange("k p t -> p k t"), parts1[:, :, :]).then_inc(z.scr, 16)
            sp.wait_ge(z.scr, per(c, 16, 16))
            if c:
                sp.wait_ge(z.sc, per(c, 3 * B, 0))
            flat = scr_q1.rearrange("k (d h) t -> k d (h t)", h=H)
            at = ROW_HI
            for k, times in ((0, 3), (1, 2), (2, 1)):
                for _ in range(times):
                    sp.dma_start(q_stack[at:at + DH, :, :].rearrange("p h t -> p (h t)"), flat[k]).then_inc(z.stack, 16)
                    at += DH

        m1 = signals("ffn1", "init load cast logits sig bias top idx idxf sa sb sel wgt wsplit wtr wT pick rin up relu sq "
                     "sup srelu ssq sdown y y_sb res", k0=2 * B + 3 * NT)
        ffn1_loads = [(gate1_w[:, :], "gate1_w"), (bias1[:, :, :], "bias1"), (up1_f[:, :, :], "up1"), (down1_f[:, 0, :, :], "down1_a"),
                      (down1_f[0:HID - P, 1, :, :], "down1_b"), (sup[:, :], "sup"), (sdown[:, 0, :], "sdown_a"),
                      (sdown[0:HID - P, 1, :], "sdown_b"), (pick1[:, :, :], "pick1"), (places1[:, :], "places1")]
        HR = HID - P
        HP = [P, HR]

        def pe_route1(pe, c, part):
            if part == 0:
                pe_norm(pe, c, m1)
            elif part == 1:
                pe.wait_ge(ln.xT, m1.k0 + c + 1)
                logits = mix[:, 0:B * 16].rearrange("p (b e) -> p b e", e=16)
                for b in range(B):
                    m = pe.matmul(logits[:, b, 0:E1], x1_T[:, c % 2, b * P:(b + 1) * P], gate1_w[:, :], start=True, stop=True)
                m.then_inc(m1.logits, 1)
            else:
                pe.wait_ge(m1.wsplit, per(c, 4, 4))
                for b in range(B):
                    m = pe.transpose(mix_bf[0:3 * E1, b * P:(b + 1) * P], wgt_parts[:, b, :, :].rearrange("p k e -> p (k e)"), ident_bf[:, :])
                m.then_inc(m1.wtr, 1)

        def pe_ffn1(pe, c):
            for k in range(2):
                if c:
                    pe.wait_ge(m1.relu, 2 * E1 * c)
                pe.matmul(ring[k][0:HP[k], :], sup[:, k * P:k * P + HP[k]], x1_T[:, c % 2, :], start=True, stop=True).then_inc(m1.sup, 1)
            if c:
                pe.wait_ge(m1.y_sb, (E1 + 1) * c)
            for k in range(2):
                pe.wait_ge(m1.ssq, per(c, 2, k + 1))
            for b in range(B):
                for k in range(2):
                    m = pe.matmul(y_bank[0][:, b * P:(b + 1) * P], hs_2[0:HP[k], k, b * P:(b + 1) * P], sdown[0:HP[k], k, :],
                                  start=(k == 0), stop=(k == 1))
            m.then_inc(m1.sdown, 1)
            pe.wait_ge(m1.wT, c + 1)

            def pick(e):
                n = E1 * c + e
                if e >= 1:
                    pe.wait_ge(m1.rin, n)
                pe.matmul(pv_bank[:, :], pick1[:, e, :], wgt_T[:, c % 2, :], start=True, stop=True).then_inc(m1.pick, 1)

            def up(e):
                n = E1 * c + e
                pe.wait_ge(m1.rin, n + 1)
                for k in range(2):
                    if e >= 2:
                        pe.wait_ge(m1.relu, 2 * (n - 2) + k + 1)
                    pe.matmul(ring[2 * (e % 2) + k][0:HP[k], :], up1[:, e, k * P:k * P + HP[k]], rin[:, e % 2, :],
                              start=True, stop=True).then_inc(m1.up, 1)

            def down(e):
                n = E1 * c + e
                use = (E1 + 1) * c + e + 1
                for k in range(2):
                    pe.wait_ge(m1.sq, 2 * n + k + 1)
                if use >= 2:
                    pe.wait_ge(m1.y_sb, use - 1)
                for b in range(B):
                    for k in range(2):
                        m = pe.matmul(y_bank[(e + 1) % 2][:, b * P:(b + 1) * P], h2_bf[0:HP[k], e % 2, k, b * P:(b + 1) * P],
                                      down1[0:HP[k], k, e, :], start=(k == 0), stop=(k == 1))
                m.then_inc(m1.y, 1)

            pick(0)
            for e in range(E1):
                up(e)
                if e + 1 < E1:
                    pick(e + 1)
                if e >= 1:
                    down(e - 1)
                if e in (2, 3, 6) and c + 1 < NT:
                    pe_route1(pe, c + 1, (2, 3, 6).index(e))
            down(E1 - 1)

        def dve_route1(dve, c):
            dve.wait_ge(m1.sig, c + 1)
            dve.tensor_tensor(biased1[:, :, :], scores1[:, :, :], bias1[:, :, :], ALU.add).then_inc(m1.bias, 1)
            dve.wait_ge(m1.bias, c + 1)
            for b in range(B):
                dve.max(top1_v[:, b, :], biased1[:, b, :]).then_inc(m1.top, 1)
            for b in range(B):
                dve.wait_ge(m1.top, per(c, B, b + 1))
                dve.max_index(top1_i[:, b, :], top1_v[:, b, :], biased1[:, b, :]).then_inc(m1.idx, 1)
            dve.wait_ge(m1.idx, per(c, B, B))
            dve.tensor_copy(top1_f[:, :, :], top1_i[:, :, :]).then_inc(m1.idxf, 1)
            dve.wait_ge(m1.idxf, c + 1)
            for b in range(B):
                dve.tensor_scalar(sel_a[:, b, :], places1[:, :], top1_f[:, b, 0:1], None, ALU.is_equal).then_inc(m1.sa, 1)
                dve.tensor_scalar(sel_b[:, b, :], places1[:, :], top1_f[:, b, 1:2], None, ALU.is_equal).then_inc(m1.sb, 1)
            dve.wait_ge(m1.sa, per(c, B, B))
            dve.wait_ge(m1.sb, per(c, B, B))
            dve.tensor_tensor(sel_s[:, :, :], sel_a[:, :, :], sel_b[:, :, :], ALU.add).then_inc(m1.sel, 1)
            dve.wait_ge(m1.sel, c + 1)
            dve.tensor_tensor(wgt1[:, :, :], sel_s[:, :, :], scores1[:, :, :], ALU.mult).then_inc(m1.wgt, 1)
            dve.wait_ge(m1.wgt, c + 1)
            split(dve, [wgt_parts[:, :, k, :] for k in range(3)], wgt_r[:, :, :], wgt1[:, :, :], m1.wsplit, c)

        def dve_ffn1(dve, c):
            dve.wait_ge(m1.sdown, c + 1)
            dve.tensor_tensor(x_sb[:, :, c, :], x_sb[:, :, c, :], y_bank[0].rearrange("p (b d) -> p b d", b=B), ALU.add).then_inc(m1.y_sb, 1)
            for e in range(E1):
                n = E1 * c + e
                dve.wait_ge(m1.pick, n + 1)
                if n >= 2:
                    dve.wait_ge(m1.up, 2 * (n - 1))
                dve.tensor_tensor(rin[:, e % 2, :], x1_T[:, c % 2, :], pv_bank[:, :], ALU.mult).then_inc(m1.rin, 1)
                if e:
                    square(dve, n - 1)
                if e >= 2:
                    round_y(dve, c, e - 2)
                if e == 0 and c + 1 < NT:
                    dve_norm_stats(dve, c + 1, m1, chunk(c + 1))
                if e == 1 and c + 1 < NT:
                    dve_norm_apply(dve, c + 1, m1, chunk(c + 1))
                if e == 5 and c + 1 < NT:
                    dve_route1(dve, c + 1)
            square(dve, E1 * c + E1 - 1)
            for e in range(E1 - 2, E1):
                round_y(dve, c, e)

        def round_y(dve, c, e):
            n = E1 * c + e
            dve.wait_ge(m1.y, n + 1)
            if n >= 2:
                dve.wait_ge(m1.res, n - 1)
            dve.tensor_copy(y1[:, n % 2, :, :], y_bank[(e + 1) % 2].rearrange("p (b d) -> p b d", b=B)).then_inc(m1.y_sb, 1)

        def pool_ffn1(pool, c):
            for e in range(E1):
                n = E1 * c + e
                if e == 0 and c + 1 < NT:
                    pool_norm(pool, c + 1, m1)
                pool.wait_ge(m1.y_sb, (E1 + 1) * c + e + 2)
                if n:
                    pool.wait_ge(m1.res, n)
                pool.tensor_tensor(x_sb[:, :, c, :], x_sb[:, :, c, :], y1[:, n % 2, :, :], ALU.add).then_inc(m1.res, 1)

        def square(dve, n):
            for k in range(2):
                dve.wait_ge(m1.relu, 2 * n + k + 1)
                dve.tensor_tensor(h2_bf[0:HP[k], n % 2, k, :], hr_bf[0:HP[k], n % 2, k, :], hr_bf[0:HP[k], n % 2, k, :],
                                  ALU.mult).then_inc(m1.sq, 1)

        def act_route1(act, c, part):
            if part == 0:
                act.wait_ge(ln.tr, per(m1.k0 + c, B, B))
                act.activation(x1_T[:, c % 2, :], mix, ACT.Copy).then_inc(ln.xT, 1)
            elif part == 1:
                logits = mix[:, 0:B * 16].rearrange("p (b e) -> p b e", e=16)
                act.wait_ge(m1.logits, c + 1)
                act.activation(scores1[:, :, :], logits[:, :, 0:E1], ACT.Sigmoid).then_inc(m1.sig, 1)
            else:
                act.wait_ge(m1.wtr, c + 1)
                act.activation(wgt_T[0:3 * E1, c % 2, :], mix_bf[0:3 * E1, 0:T], ACT.Copy).then_inc(m1.wT, 1)

        def act_ffn1(act, c):
            for k in range(2):
                act.wait_ge(m1.sup, per(c, 2, k + 1))
                act.activation(hs_r[0:HP[k], k, :], ring[k][0:HP[k], :], ACT.Relu).then_inc(m1.srelu, 1)
            for k in range(2):
                act.wait_ge(m1.srelu, per(c, 2, k + 1))
                act.activation(hs_2[0:HP[k], k, :], hs_r[0:HP[k], k, :], ACT.Square).then_inc(m1.ssq, 1)
            for e in range(E1):
                n = E1 * c + e
                for k in range(2):
                    act.wait_ge(m1.up, 2 * n + k + 1)
                    if n >= 2:
                        act.wait_ge(m1.sq, 2 * (n - 2) + k + 1)
                    act.activation(hr_bf[0:HP[k], e % 2, k, :], ring[2 * (e % 2) + k][0:HP[k], :], ACT.Relu).then_inc(m1.relu, 1)
                if e in (2, 3, 6) and c + 1 < NT:
                    act_route1(act, c + 1, (2, 3, 6).index(e))

        def split(eng, dst, res, full, done, i):
            eng.tensor_copy(dst[0], full).then_inc(done, 1)
            eng.wait_ge(done, per(i, 4, 1))
            eng.tensor_tensor(res, full, dst[0], ALU.subtract).then_inc(done, 1)
            eng.wait_ge(done, per(i, 4, 2))
            eng.tensor_copy(dst[1], res).then_inc(done, 1)
            eng.wait_ge(done, per(i, 4, 3))
            eng.tensor_tensor(dst[2], res, dst[1], ALU.subtract).then_inc(done, 1)

        def load_stage(eng, sem_, what):
            for dst, name in what:
                eng.dma_start(dst, io[name]).then_inc(sem_, 16)

        jobs = [(i, a) for a in (own, cross) for i in range(B)]
        attention_block = ctx.enter_context(ExitStack())
        block = attention_block.enter_context(nc.Block())

        @block.sync
        def _(sp):
            for dst, src in first_loads:
                sp.dma_start(dst, src).then_inc(s_first, 16)
            for dst, src in loads:
                sp.dma_start(dst, src).then_inc(s_load, 16)
            for i, a in jobs:
                sp_attention(sp, i, a)

        @block.tensor
        def _(pe):
            pe.wait_ge(s_first, FIRST_LOADED)
            pe.wait_ge(s_init, INIT)
            for part in range(4):
                pe_prepare(pe, *jobs[0], part)
            pe.wait_ge(s_load, LOADED)
            attend, turn_heads, turn_back, project, first_maxima, turn_max = pe_attention(pe, *jobs[0])
            first_maxima(0, P)
            turn_max(0)
            for n in range(len(jobs)):
                following = jobs[n + 1] if n + 1 < len(jobs) else None
                attend(following)
                if following:
                    next_pieces = pe_attention(pe, *following)
                    next_maxima = next_pieces[4]
                    next_maxima(0, 2)
                    turn_heads(3)
                    next_maxima(2, 6)
                    turn_back()
                    next_maxima(6, 10)
                    project()
                    next_maxima(10, P)
                    attend, turn_heads, turn_back, project, first_maxima, turn_max = next_pieces
                    turn_max(0)
                else:
                    turn_heads(3)
                    turn_back()
                    project()

        @block.vector
        def _(dve):
            dve.memset(neg_half[:, :], -0.5).then_inc(s_init, 1)
            dve.memset(one_row[:, :], 1.0).then_inc(s_init, 1)
            dve.memset(gn_eps[:, :], GN_EPS).then_inc(s_init, 1)
            dve.wait_ge(s_first, FIRST_LOADED)
            dve_norm(dve, *jobs[0], tokens_of(0))
            dve_prepare(dve, *jobs[0])
            dve.wait_ge(s_load, LOADED)
            dve.tensor_copy(len_f[:, :], len_i[:, :]).then_inc(s_len, 1)
            dve.wait_ge(s_len, 1)
            dve.tensor_scalar(keep[:, :], len_f[:, :], pos_col[:, 0:1], None, ALU.is_gt).then_inc(s_len, 1)
            dve.tensor_reduce(len_max[:, :], len_f[:, :], AX.X, ALU.max).then_inc(s_len, 1)
            dve.wait_ge(s_len, 3)
            dve.tensor_scalar(mask_row[:, :], pos_row[:, :], len_max[0:1, 0:1], NEG, ALU.is_ge, ALU.mult).then_inc(s_mask, 1)
            maxima, normalize, residual = dve_attention(dve, *jobs[0])
            maxima(0)
            for n in range(len(jobs)):
                following = jobs[n + 1] if n + 1 < len(jobs) else None
                for g in range(4):
                    if g < 3:
                        maxima(g + 1)
                    if g == 2 and following:
                        dve_norm(dve, *following, tokens_of(following[0]))
                    if g:
                        normalize(g - 1)
                if following:
                    dve_prepare(dve, *following)
                    next_pieces = dve_attention(dve, *following)
                    next_maxima = next_pieces[0]
                    next_maxima(0, 0, 2)
                    normalize(3)
                    next_maxima(0, 2, 10)
                    residual()
                    next_maxima(0, 10, P)
                    maxima, normalize, residual = next_pieces
                else:
                    normalize(3)
                    residual()

        @block.scalar
        def _(act):
            act.wait_ge(s_init, INIT)
            for part in range(2):
                act_prepare(act, *jobs[0], part)
            attend, max_rows = act_attention(act, *jobs[0])
            max_rows(0)
            for n in range(len(jobs)):
                following = jobs[n + 1] if n + 1 < len(jobs) else None
                attend(following)
                if following:
                    attend, max_rows = act_attention(act, *following)
                    max_rows(0)

        @block.gpsimd
        def _(pool):
            for v_aug in v_augs:
                pool.memset(v_aug[:, :, :, :], 0.0).then_inc(s_init, 1)
            pool.wait_ge(s_init, 5)
            for v_aug in v_augs:
                pool.memset(v_aug[:, :, :, DH:DH + 1], 1.0).then_inc(s_init, 1)
            pool.wait_ge(s_init, INIT)
            for i, a in jobs:
                if (i, a) == (0, cross):
                    pool.wait_ge(s_load, LOADED)
                    pool.wait_ge(s_len, 3)
                pool_prepare(pool, i, a)
                pool_attention(pool, i, a)

        attention_block.close()
        with nc.Block() as reset:
            @reset.gpsimd
            def _(pool):
                for s in in_block_1:
                    pool.sem_clear(s)

        block = ctx.enter_context(nc.Block())

        @block.sync
        def _(sp):
            load_stage(sp, f.load, ffn0_loads)
            load_stage(sp, f.up_in, [(up0[:, :, :], "up0")])
            load_stage(sp, f.down_in, [(down0[:, :, :, :], "down0")])
            load_stage(sp, r.load, rec_loads)
            sp_rec(sp, 0)
            for c in range(NT):
                if c:
                    sp_out1(sp, c - 1)
                if c + 1 < NT:
                    sp_rec(sp, c + 1)
            sp.wait_ge(r.scr, per(NT - 1, 96, 96))
            load_stage(sp, z.load, cross1_loads)
            sp.dma_start(ctx1[:, :, :], io["ctx"].rearrange("b s d -> s b d")).then_inc(z.load, 16)
            sp.dma_start(pad_i[:, :, :].rearrange("p b s -> p (b s)"), io["pad"].partition_broadcast(P)).then_inc(z.load, 16)
            sp_out1(sp, NT - 1)
            sp_ctx1(sp)
            sp_cross1(sp, 0)
            load_stage(sp, m1.load, ffn1_loads)
            for c in range(1, NT):
                sp_cross1(sp, c)
            sp.wait_ge(m1.res, NT * E1)
            for b in range(B):
                sp.dma_start(out[b].rearrange("(c p) d -> p c d", p=P), x_sb[:, b, :, :]).then_inc(s_out, 16)
            sp.wait_ge(s_out, 16 * B)

        @block.tensor
        def _(pe):
            pe.wait_ge(f.load, 16 * len(ffn0_loads))
            for part in range(2):
                pe_route0(pe, 0, part)
            for c in range(NT):
                pe_ffn0(pe, c)
            pe.wait_ge(r.load, 16 * len(rec_loads))
            pe_rec(pe, 0)
            for c in range(NT):
                if c + 1 < NT:
                    pe_rec(pe, c + 1)
                if c:
                    pe_out1(pe, c - 1)
            pe_out1(pe, NT - 1)
            pe.wait_ge(z.load, 16 * (len(cross1_loads) + 2))
            pe.wait_ge(r.res, NT)
            pe_ctx1(pe)
            pe_norm(pe, 0, z, q_bank)
            pe_query1(pe, 0, 0)
            pe_query1(pe, 0, 1)
            for c in range(NT):
                pe_cross1(pe, c)
            pe.wait_ge(m1.load, 16 * len(ffn1_loads))
            pe.wait_ge(m1.init, 1)
            pe.wait_ge(m1.cast, 3)
            for part in range(3):
                pe_route1(pe, 0, part)
            for c in range(NT):
                pe_ffn1(pe, c)

        @block.vector
        def _(dve):
            dve.wait_ge(f.load, 16 * len(ffn0_loads))
            dve_norm_stats(dve, 0, f, chunk(0))
            dve_norm0(dve, 0)
            dve_route0(dve, 0)
            for c in range(NT):
                dve_ffn0(dve, c)
            dve.memset(xs[:, 0, :, 0:1], 0.0).then_inc(r.init, 1)
            dve.memset(state0[:, :, :], 0.0).then_inc(r.init, 1)
            dve.wait_ge(r.load, 16 * len(rec_loads))
            dve.wait_ge(r.init, 2)
            dve_norm(dve, 0, r, chunk(0))
            dve_rec_mix(dve, 0, range(7))
            dve_rec_norms(dve, 0)
            dve_rec_units(dve, 0)
            dve_dots(dve, 0)
            for c in range(NT):
                before, after = c > 0, c + 1 < NT
                dve_steps(dve, c, 0, 6)
                if after:
                    dve_norm_stats(dve, c + 1, r, chunk(c + 1))
                dve_steps(dve, c, 6, 16)
                if after:
                    dve_norm_apply(dve, c + 1, r, chunk(c + 1))
                dve_steps(dve, c, 16, 28)
                if after:
                    dve_rec_mix(dve, c + 1, range(4))
                dve_steps(dve, c, 28, 34)
                if after:
                    dve_rec_mix(dve, c + 1, range(4, 7))
                dve_steps(dve, c, 34, 42)
                if after:
                    dve_rec_norms(dve, c + 1)
                dve_steps(dve, c, 42, 50)
                if after:
                    dve_rec_units(dve, c + 1)
                dve_steps(dve, c, 50, 60)
                if before:
                    dve_out1_center(dve, c - 1)
                dve_steps(dve, c, 60, 76)
                if before:
                    dve_out1_norm(dve, c - 1)
                dve_steps(dve, c, 76, 92)
                if before:
                    dve_out1_residual(dve, c - 1)
                dve_steps(dve, c, 92, P)
            dve_outputs(dve, NT * NB - 1)
            dve_out1_center(dve, NT - 1)
            dve_out1_norm(dve, NT - 1)
            dve_out1_residual(dve, NT - 1)
            dve.wait_ge(z.load, 16 * (len(cross1_loads) + 2))
            dve_ctx1(dve)
            dve_norm(dve, 0, z, chunk(0))
            dve_query1(dve, 0, 0)
            dve_query1(dve, 0, 1)
            dve_query1_parts(dve, 0)
            for c in range(NT):
                dve_cross1(dve, c)
            dve.memset(wgt_T[:, :, :], 0.0).then_inc(m1.init, 1)
            dve.wait_ge(m1.load, 16 * len(ffn1_loads))
            dve_norm(dve, 0, m1, chunk(0))
            dve_route1(dve, 0)
            for c in range(NT):
                dve_ffn1(dve, c)

        @block.scalar
        def _(act):
            for part in range(2):
                act_route0(act, 0, part)
            for c in range(NT):
                act_ffn0(act, c)
            act_rec(act, 0)
            for c in range(NT):
                if c + 1 < NT:
                    act_rec(act, c + 1)
                if c:
                    act_out1(act, c - 1)
            act_out1(act, NT - 1)
            act_ctx1(act)
            act_query1(act, 0)
            for c in range(NT):
                act_cross1(act, c)
            act.wait_ge(m1.init, 1)
            for part in range(3):
                act_route1(act, 0, part)
            for c in range(NT):
                act_ffn1(act, c)

        @block.gpsimd
        def _(pool):
            for c in range(NT):
                pool_norm(pool, c, f)
            pool.wait_ge(r.init, 2)
            pool_norm(pool, 0, r)
            pool_rec_before(pool, 0)
            pool_pairs_a(pool, 0)
            pool_pairs_b(pool, 0)
            for blk in range(NT * NB):
                c, k = blk // NB, blk % NB
                ahead = blk + 1 < NT * NB
                if ahead:
                    pool_pairs_a(pool, blk + 1)
                if k == 0 and c + 1 < NT:
                    pool_norm(pool, c + 1, r)
                if blk:
                    pool_products(pool, blk - 1)
                if ahead:
                    pool_pairs_b(pool, blk + 1)
                if blk:
                    pool_outputs(pool, blk - 1)
                if k == 0 and c + 1 < NT:
                    pool_rec_before(pool, c + 1)
            pool_products(pool, NT * NB - 1)
            pool_outputs(pool, NT * NB - 1)
            pool.memset(k1_stack[0:1, :, :, :], 0.0).then_inc(z.init, 1)
            pool.memset(v1_aug[:, :, :, :], 0.0).then_inc(z.init, 1)
            pool.wait_ge(z.init, 2)
            pool.memset(v1_aug[:, :, :, DH:DH + 1], 1.0).then_inc(z.init, 1)
            pool_norm(pool, 0, z)
            pool_cross1(pool, 0)
            pool.wait_ge(m1.load, 16 * len(ffn1_loads))
            pool.tensor_copy(up1[:, :, :], up1_f[:, :, :]).then_inc(m1.cast, 1)
            pool.tensor_copy(down1[:, 0, :, :], down1_f[:, 0, :, :]).then_inc(m1.cast, 1)
            pool.tensor_copy(down1[0:HR, 1, :, :], down1_f[0:HR, 1, :, :]).then_inc(m1.cast, 1)
            for c in range(1, NT):
                pool_cross1(pool, c)
            pool_norm(pool, 0, m1)
            for c in range(NT):
                pool_ffn1(pool, c)


HD = np.arange(H * DH).reshape(H, DH)
DH_ORDER = HD.T.reshape(-1)


def _rope_tables(positions, turned_sign, freqs, scale):
    ang = positions[None, :].astype(np.float32) * freqs[:, None].astype(np.float32)
    cos = np.cos(ang) * np.float32(scale)
    sin = np.sin(ang) * turned_sign[:, None] * np.float32(scale)
    return (np.repeat(cos, H, axis=0).astype(np.float32), np.repeat(sin, H, axis=0).astype(np.float32))


def _columns(w, order):
    return np.ascontiguousarray(np.asarray(w).T[:, order])


def _layout(inp):
    bf = mybir.dt.np(BF16)
    a = {k: np.asarray(v) for k, v in inp.items()}
    pair = np.arange(DH) ^ 1
    turn0 = HD[:, pair].T.reshape(-1)
    io = {}
    io["x"] = a["x"]
    io["ident"] = np.eye(P, dtype=np.float32)
    io["ident_bf"] = np.eye(P, dtype=bf)
    later = np.triu(np.ones((P, P), np.float32), 1) * np.float32(NEG)
    io["mask_qk"] = later.astype(bf)
    io["mask_kq"] = np.ascontiguousarray(later.T).astype(bf)
    f0 = np.exp(-np.log(np.float32(10000.0)) * np.arange(0, DH, 2, dtype=np.float32) / np.float32(DH)).astype(np.float32)
    sign0 = np.where(np.arange(DH) % 2 == 0, -1.0, 1.0).astype(np.float32)
    pos = np.arange(T, dtype=np.float32)
    cq, sq = _rope_tables(pos, sign0, np.repeat(f0, 2), DH ** -0.5)
    ck, sk = _rope_tables(pos, sign0, np.repeat(f0, 2), 1.0)
    io["rope0"] = np.ascontiguousarray(np.stack([cq, sq, ck, sk], axis=1))
    wq, wk, wv = np.split(a["L0_attn_Wqkv"], 3, axis=0)
    plain = np.arange(D)
    io["w0"] = np.ascontiguousarray(np.stack([_columns(wq, DH_ORDER), _columns(wq, turn0), _columns(wk, DH_ORDER),
                                              _columns(wk, turn0), _columns(wv, plain), _columns(a["L0_attn_Wo"], plain)], axis=1))
    io["w0x"] = np.ascontiguousarray(np.stack([_columns(a["L0_xattn_wq"], DH_ORDER), _columns(a["L0_xattn_wk"], DH_ORDER),
                                               _columns(a["L0_xattn_wv"], plain), _columns(a["L0_xattn_wo"], plain)], axis=1))
    io["bo0x"] = a["L0_xattn_bo"][None]
    io["ones_row"] = np.ones((1, H * KW), bf)
    io["zero_row"] = np.zeros((1, H * KW), bf)
    io["ones_rows"] = np.ones((3, H * KW), bf)
    io["ctx"] = a["ctx_1024"]
    io["ctx_dh"] = np.ascontiguousarray(a["ctx_1024"][:, :, DH_ORDER])
    io["lens"] = a["_lenS2"].astype(np.int32)
    io["pos_col"] = np.arange(P, dtype=np.float32)[:, None]
    io["pos_row"] = np.tile(np.arange(SC, dtype=np.float32), H)[None]
    io["up0"] = np.ascontiguousarray(a["L0_ffn_w1"].transpose(1, 0, 2))
    io["down0"] = np.ascontiguousarray(a["L0_ffn_w2"].reshape(E0, F0 // P, P, D).transpose(2, 0, 1, 3))
    io["router_w"], io["router_b"] = a["L0_ffn_router_w"], a["L0_ffn_router_b"][None]

    def picks(rows, experts):
        out = np.zeros((64, experts, P), bf)
        for e in range(experts):
            out[[e, rows + e, 2 * rows + e], e, :] = 1
        return out

    io["pick1"] = picks(E1, E1)
    io["places"] = np.tile(np.arange(E0 + 1, dtype=np.float32), (P, 1))
    io["places1"] = np.tile(np.arange(E1, dtype=np.float32), (P, 1))
    names = ["r", "w", "k", "v", "a", "b", "g"]
    io["w1a"] = np.ascontiguousarray(np.stack([a[f"L1_attn_W_{n}"].T for n in names + ["o"]], axis=1))
    io["mix1"] = np.ascontiguousarray(np.stack([a[f"L1_attn_x_{n}"] for n in names], axis=1))
    io["bo1a"] = a["L1_attn_b_o"][None]
    io["gn_w"], io["gn_b"] = a["L1_attn_gn_w"][:, None], a["L1_attn_gn_b"][:, None]
    same = np.kron(np.eye(H), np.ones((DH, DH))).astype(np.float32)
    io["blk_ones"], io["blk_mean"] = same, (same / DH).astype(np.float32)
    turn1 = HD[:, (np.arange(DH) + DH // 2) % DH].T.reshape(-1)
    sign1 = np.where(np.arange(DH) < DH // 2, -1.0, 1.0).astype(np.float32)
    f1 = (1.0 / 10000.0 ** (np.arange(0, DH, 2, dtype=np.float32) / np.float32(DH))).astype(np.float32)
    cq, sq = _rope_tables(pos, sign1, np.tile(f1, 2), DH ** -0.5)
    ck, sk = _rope_tables(pos, sign1, np.tile(f1, 2), 1.0)
    io["rope1"] = np.ascontiguousarray(np.stack([cq, sq, ck, sk], axis=1))
    wq, wk = a["L1_xattn_wq"], a["L1_xattn_wk"]
    io["w1x"] = np.ascontiguousarray(np.stack([_columns(wq, DH_ORDER), _columns(wq, turn1), _columns(wk, DH_ORDER),
                                               _columns(wk, turn1), a["L1_xattn_wv"].T, a["L1_xattn_wo"].T], axis=1))
    bq, bk = a["L1_xattn_bq"], a["L1_xattn_bk"]
    io["b1x"] = np.ascontiguousarray(np.stack([bq[DH_ORDER], bq[turn1], bk[DH_ORDER], bk[turn1]], axis=1))
    io["bv1x"], io["bo1x"] = a["L1_xattn_bv"][None], a["L1_xattn_bo"][None]
    io["causal1"] = np.where(np.arange(SC)[None, :] > np.arange(P)[:, None], -1e9, 0.0).astype(np.float32)
    io["pad"] = a["mask_BxS2_bk1"].astype(np.int32).reshape(-1)
    io["gate1_w"] = np.ascontiguousarray(a["L1_ffn_gate_w"].T)
    io["bias1"] = np.ascontiguousarray(np.broadcast_to(a["L1_ffn_expert_bias"], (P, NT, E1)))
    io["up1"] = np.ascontiguousarray(a["L1_ffn_w_up"].transpose(2, 0, 1))
    down = a["L1_ffn_w_down"].transpose(2, 0, 1)
    io["down1_a"], io["down1_b"] = np.ascontiguousarray(down[0:P]), np.ascontiguousarray(down[P:])
    io["sup"] = np.ascontiguousarray(a["L1_ffn_shared_w_up"].T)
    sd = a["L1_ffn_shared_w_down"].T
    io["sdown_a"], io["sdown_b"] = np.ascontiguousarray(sd[0:P]), np.ascontiguousarray(sd[P:])
    return io


def kernel(**inputs):
    import concourse.bacc as _bacc
    from concourse.bass_utils import run_bass_kernel_spmd as _run

    io = _layout(inputs)
    nc = _bacc.Bacc("TRN2", target_bir_lowering=False, num_devices=1)
    arrays, aps = {}, {}
    for name, arr in io.items():
        arrays[f"in_{name}"] = arr
        aps[name] = nc.dram_tensor(f"in_{name}", arr.shape, mybir.dt.from_np(arr.dtype), kind="ExternalInput").ap()
    out = nc.dram_tensor("out_x", [B, T, D], F32, kind="ExternalOutput").ap()
    decoder(nc, aps, out)
    r = _run(nc, [arrays], core_ids=[0])
    return r.results[0]["out_x"]
```
